# Optimizing a Trainium2 kernel written in Bass

```python
import numpy as np
import jax
import jax.numpy as jnp

def _softmax(x, axis=-1):
    return jax.nn.softmax(x, axis=axis)

def _gelu(x):
    return jax.nn.gelu(x, approximate=True)

def _silu(x):
    return jax.nn.silu(x)

def _sigmoid(x):
    return jax.nn.sigmoid(x)

def _layernorm(x, axis=-1, eps=1e-05):
    m = jnp.mean(x, axis=axis, keepdims=True)
    v = jnp.var(x, axis=axis, keepdims=True)
    return (x - m) / jnp.sqrt(v + eps)

def _scatter_add(tgt, idx, src, axis=0):
    return tgt.at[idx].add(src)

def _segment_sum(src, seg, n):
    return jax.ops.segment_sum(src, seg, n)
kernel_name = 'mk_gnn_ffn_d4_gnn_r32_57afaa'

def setup_inputs(seed: int=0):
    np.random.seed(seed)
    _w = jnp.asarray

    def _rec_inputs():
        import jax
        import jax.numpy as jnp
        _gk = jax.random.key(seed)
        x = -0.0003713 + 1 * jax.random.normal(jax.random.fold_in(_gk, 1), (3125, 256), jnp.float32)
        _s = jax.random.randint(jax.random.fold_in(_gk, 2), (25000,), 0, 3125, jnp.int32)
        _d = jax.random.randint(jax.random.fold_in(_gk, 3), (25000,), 0, 3125, jnp.int32)
        _loop = jnp.arange(3125, dtype=jnp.int32)
        src = jnp.concatenate([_s, _d, _loop])
        dst = jnp.concatenate([_d, _s, _loop])
        _o = jnp.argsort(dst, stable=True)
        src = src[_o]
        dst = dst[_o]
        edge_attr_3 = -1.09012e-05 + 0.99985 * jax.random.normal(jax.random.fold_in(_gk, 12), (53125, 3), jnp.float32)
        edge_attr_64 = 0.000151818 + 1.00006 * jax.random.normal(jax.random.fold_in(_gk, 13), (53125, 64), jnp.float32)
        edge_weight = jax.random.uniform(jax.random.fold_in(_gk, 15), (53125,), jnp.float32, 0.0, 4.99999)
        return (x, src, dst, edge_attr_3, edge_attr_64, edge_weight)
    x, src, dst, edge_attr_3, edge_attr_64, edge_weight = _rec_inputs()

    def _L0_gnn_setup():
        import jax, jax.numpy as jnp
        import numpy as np
        N = 50000
        E = 12500
        IN = 256
        H = 8
        D = 32
        EF = 3
        key = jax.random.key(seed)
        ks = jax.random.split(key, 8)
        x = jax.random.normal(ks[0], (N, IN), dtype=jnp.float32)
        edge_index = jax.random.randint(ks[1], (2, E), 0, N, dtype=jnp.int64)
        edge_attr = jax.random.normal(ks[2], (E, EF), dtype=jnp.float32)
        W = jax.random.normal(ks[3], (H * D, IN), dtype=jnp.float32) * np.float32(np.sqrt(2.0 / (IN + H * D)))
        a_src = jax.random.normal(ks[4], (H, D), dtype=jnp.float32) * np.float32(np.sqrt(2.0 / (H + D)))
        a_dst = jax.random.normal(ks[5], (H, D), dtype=jnp.float32) * np.float32(np.sqrt(2.0 / (H + D)))
        edge_W = jax.random.normal(ks[6], (H * D, EF), dtype=jnp.float32) * np.float32(np.sqrt(2.0 / (EF + H * D)))
        edge_b = jnp.zeros((H * D,), dtype=jnp.float32)
        bias = jnp.zeros((H * D,), dtype=jnp.float32)
        return {'x': x, 'W': W, 'a_src': a_src, 'a_dst': a_dst, 'edge_W': edge_W, 'edge_b': edge_b, 'bias': bias, 'edge_attr': edge_attr, 'edge_index': edge_index}
    _L0_gnn_all = _L0_gnn_setup()
    _L0_gnn_in = {k: v for k, v in _L0_gnn_all.items() if k in ('W', 'a_src', 'a_dst', 'edge_W', 'edge_b', 'bias')}
    del _L0_gnn_all

    def _L0_ffn_setup():
        import jax, jax.numpy as jnp
        import numpy as np
        E = 8
        K = 2
        D = 256
        H = 512
        DOUT = 256
        EPS = 1e-05
        key = jax.random.key(seed)
        ks = jax.random.split(key, 9)
        s = 0.02
        return {'x': jax.random.normal(ks[0], (4, 256, D), jnp.float32), 'gamma': 1.0 + 0.05 * jax.random.normal(ks[1], (D,), jnp.float32), 'beta': 0.05 * jax.random.normal(ks[2], (D,), jnp.float32), 'Wr': 0.01 * jax.random.normal(ks[3], (D, E), jnp.float32), 'br': jnp.zeros((E,), jnp.float32), 'W1': s * jax.random.normal(ks[4], (E, D, H), jnp.float32), 'b1': s * jax.random.normal(ks[5], (E, H), jnp.float32), 'W2': s * jax.random.normal(ks[6], (E, H, DOUT), jnp.float32), 'b2': s * jax.random.normal(ks[7], (E, DOUT), jnp.float32)}
    _L0_ffn_all = _L0_ffn_setup()
    _L0_ffn_in = {k: v for k, v in _L0_ffn_all.items() if k in ('gamma', 'beta', 'Wr', 'br', 'W1', 'b1', 'W2', 'b2')}
    del _L0_ffn_all

    def _L1_gnn_setup():
        import jax, jax.numpy as jnp
        import numpy as np
        H = 256
        R = 64
        N = 625
        E = 10000
        CUTOFF_LO = 0.0
        CUTOFF_UP = 5.0
        LN_EPS = 1e-05

        def _layernorm(x, g, b):
            mu = jnp.mean(x, axis=-1, keepdims=True)
            var = jnp.var(x, axis=-1, keepdims=True)
            return (x - mu) * jax.lax.rsqrt(var + LN_EPS) * g + b

        def _cosine_cutoff(r):
            c = 0.5 * (jnp.cos(r * (jnp.pi / CUTOFF_UP)) + 1.0)
            return c * (r < CUTOFF_UP).astype(r.dtype)
        key = jax.random.key(seed)
        ks = jax.random.split(key, 16)

        def xavier(k, shape):
            fan_in, fan_out = (shape[1], shape[0])
            lim = np.sqrt(6.0 / (fan_in + fan_out))
            return jax.random.uniform(k, shape, jnp.float32, -lim, lim)
        x = jax.random.normal(ks[0], (N, H), jnp.float32)
        edge_index = jax.random.randint(ks[1], (2, E), 0, N, jnp.int64)
        edge_weight = jax.random.uniform(ks[2], (E,), jnp.float32, 0.0, CUTOFF_UP)
        edge_attr = jax.random.normal(ks[3], (E, R), jnp.float32)
        return {'x': x, 'edge_index': edge_index, 'edge_weight': edge_weight, 'edge_attr': edge_attr, 'ln_g': jnp.ones((H,), jnp.float32), 'ln_b': jnp.zeros((H,), jnp.float32), 'Wq': xavier(ks[4], (H, H)), 'bq': jnp.zeros((H,), jnp.float32), 'Wk': xavier(ks[5], (H, H)), 'bk': jnp.zeros((H,), jnp.float32), 'Wv': xavier(ks[6], (H, H)), 'bv': jnp.zeros((H,), jnp.float32), 'Wo': xavier(ks[7], (H, H)), 'bo': jnp.zeros((H,), jnp.float32), 'Wdk': xavier(ks[8], (H, R)), 'bdk': jnp.zeros((H,), jnp.float32), 'Wdv': xavier(ks[9], (H, R)), 'bdv': jnp.zeros((H,), jnp.float32)}
    _L1_gnn_all = _L1_gnn_setup()
    _L1_gnn_in = {k: v for k, v in _L1_gnn_all.items() if k in ('ln_g', 'ln_b', 'Wq', 'bq', 'Wk', 'bk', 'Wv', 'bv', 'Wo', 'bo', 'Wdk', 'bdk', 'Wdv', 'bdv')}
    del _L1_gnn_all

    def _L1_ffn_setup():
        import jax, jax.numpy as jnp
        import numpy as np
        B, N, D = (16, 128, 256)
        NUM_EXPERTS, TOP_K, HEADS = (4, 2, 4)
        N_EDGES = 32768
        LN_EPS = 1e-05

        def _layernorm(x, g, b):
            mu = x.mean(-1, keepdims=True)
            var = ((x - mu) ** 2).mean(-1, keepdims=True)
            return (x - mu) * jax.lax.rsqrt(var + LN_EPS) * g + b

        def _forward(x, edge_index, W_gat, att_src, att_dst, b_gat, ln_gamma, ln_beta, W1, b1, W2, b2):
            Bc, Nc, Dc = x.shape
            M = Bc * Nc
            x_flat = x.reshape(M, Dc)
            h = (x_flat @ W_gat).reshape(M, HEADS, NUM_EXPERTS)
            loops = jnp.arange(M, dtype=edge_index.dtype)
            src = jnp.concatenate([edge_index[0], loops])
            dst = jnp.concatenate([edge_index[1], loops])
            a_src = (h * att_src).sum(-1)
            a_dst = (h * att_dst).sum(-1)
            e = jax.nn.leaky_relu(a_src[src] + a_dst[dst], negative_slope=0.2)
            e_max = jax.ops.segment_max(e, dst, num_segments=M)
            ee = jnp.exp(e - e_max[dst])
            denom = jax.ops.segment_sum(ee, dst, num_segments=M)
            alpha = ee / (denom[dst] + 1e-16)
            msg = h[src] * alpha[:, :, None]
            agg = jax.ops.segment_sum(msg, dst, num_segments=M).reshape(M, HEADS * NUM_EXPERTS) + b_gat
            scores = _layernorm(agg, ln_gamma, ln_beta).reshape(M, HEADS, NUM_EXPERTS).mean(1)
            scores = scores.reshape(Bc, Nc, NUM_EXPERTS)
            topk_s, topk_i = jax.lax.top_k(scores, TOP_K)
            w = jax.nn.softmax(topk_s, axis=-1)
            out = jnp.zeros_like(x)
            for ei in range(NUM_EXPERTS):
                g = jnp.where(topk_i == ei, w, 0.0).sum(-1)
                hh = jax.nn.gelu(x @ W1[ei] + b1[ei], approximate=False)
                out = out + g[..., None] * (hh @ W2[ei] + b2[ei])
            return out
        key = jax.random.key(seed)
        ks = jax.random.split(key, 8)
        s = 0.05
        return {'x': jax.random.normal(ks[0], (B, N, D), jnp.float32), 'W_gat': jax.random.normal(ks[1], (D, HEADS * NUM_EXPERTS), jnp.float32) * s, 'att_src': jax.random.normal(ks[2], (HEADS, NUM_EXPERTS), jnp.float32) * s, 'att_dst': jax.random.normal(ks[3], (HEADS, NUM_EXPERTS), jnp.float32) * s, 'b_gat': jnp.zeros((HEADS * NUM_EXPERTS,), jnp.float32), 'ln_gamma': jnp.ones((HEADS * NUM_EXPERTS,), jnp.float32), 'ln_beta': jnp.zeros((HEADS * NUM_EXPERTS,), jnp.float32), 'W1': jax.random.normal(ks[4], (NUM_EXPERTS, D, 2 * D), jnp.float32) * s, 'b1': jnp.zeros((NUM_EXPERTS, 2 * D), jnp.float32), 'W2': jax.random.normal(ks[5], (NUM_EXPERTS, 2 * D, D), jnp.float32) * s, 'b2': jnp.zeros((NUM_EXPERTS, D), jnp.float32), 'edge_index': jax.random.randint(ks[6], (2, N_EDGES), 0, B * N, jnp.int32)}
    _L1_ffn_all = _L1_ffn_setup()
    _L1_ffn_in = {k: v for k, v in _L1_ffn_all.items() if k in ('W_gat', 'att_src', 'att_dst', 'b_gat', 'ln_gamma', 'ln_beta', 'W1', 'b1', 'W2', 'b2', 'edge_index')}
    del _L1_ffn_all

    def _L2_gnn_setup():
        import jax, jax.numpy as jnp
        import numpy as np
        N_NODES = 50000

        def _add_self_loops(src, dst, n):
            loop = jnp.arange(n, dtype=src.dtype)
            return (jnp.concatenate([src, loop]), jnp.concatenate([dst, loop]))

        def gcn_conv(x, src, dst, W, b, n):
            h = x @ W
            deg = jnp.zeros((n,), h.dtype).at[dst].add(1.0)
            dinv = jax.lax.rsqrt(jnp.maximum(deg, 1e-12))
            norm = dinv[src] * dinv[dst]
            msg = h[src] * norm[:, None]
            return jax.ops.segment_sum(msg, dst, num_segments=n) + b
        key = jax.random.key(seed)
        ks = jax.random.split(key, 10)
        num_features, hidden = (256, 64)
        x = jax.random.normal(ks[0], (N_NODES, num_features), jnp.float32)
        edge_index = jax.random.randint(ks[1], (2, 50000), 0, N_NODES, jnp.int64)

        def glorot(k, fi, fo):
            s = jnp.sqrt(6.0 / (fi + fo)).astype(jnp.float32)
            return jax.random.uniform(k, (fi, fo), jnp.float32, -s, s)
        dims = [(num_features, 2 * hidden), (2 * hidden, hidden), (hidden, 2 * hidden), (2 * hidden, num_features)]
        params = {}
        for i, (fi, fo) in enumerate(dims):
            params[f'W{i + 1}'] = glorot(ks[2 + i], fi, fo)
            params[f'b{i + 1}'] = jnp.zeros((fo,), jnp.float32)
        return {'x': x, 'edge_index': edge_index, **params}
    _L2_gnn_all = _L2_gnn_setup()
    _L2_gnn_in = {k: v for k, v in _L2_gnn_all.items() if k in ('W1', 'b1', 'W2', 'b2', 'W3', 'b3', 'W4', 'b4')}
    del _L2_gnn_all

    def _L2_ffn_setup():
        import jax, jax.numpy as jnp
        import numpy as np
        BN_EPS = 0.001

        def _bn(h, g, b, m, v):
            return g * (h - m) * jax.lax.rsqrt(v + BN_EPS) + b
        key = jax.random.key(seed)
        ks = jax.random.split(key, 8)
        B, F, Df = (256, 64, 256)
        E, H, D = (8, 256, 256)
        s1 = 1.0 / np.sqrt(Df)
        s2 = 1.0 / np.sqrt(H)
        return {'x': jax.random.normal(ks[0], (B, F, Df), jnp.float32), 'Wr': jax.random.normal(ks[1], (Df, E), jnp.float32) * s1, 'br': jnp.zeros((E,), jnp.float32), 'W1': jax.random.normal(ks[2], (E, Df, H), jnp.float32) * s1, 'b1': jnp.zeros((E, H), jnp.float32), 'g1': jnp.ones((E, H), jnp.float32), 'be1': jnp.zeros((E, H), jnp.float32), 'm1': jnp.zeros((E, H), jnp.float32), 'v1': jnp.ones((E, H), jnp.float32), 'W2': jax.random.normal(ks[3], (E, H, H), jnp.float32) * s2, 'b2': jnp.zeros((E, H), jnp.float32), 'g2': jnp.ones((E, H), jnp.float32), 'be2': jnp.zeros((E, H), jnp.float32), 'm2': jnp.zeros((E, H), jnp.float32), 'v2': jnp.ones((E, H), jnp.float32), 'Wo': jax.random.normal(ks[4], (E, H, D), jnp.float32) * s2, 'bo': jnp.zeros((E, D), jnp.float32)}
    _L2_ffn_all = _L2_ffn_setup()
    _L2_ffn_in = {k: v for k, v in _L2_ffn_all.items() if k in ('Wr', 'br', 'W1', 'b1', 'g1', 'be1', 'm1', 'v1', 'W2', 'b2', 'g2', 'be2', 'm2', 'v2', 'Wo', 'bo')}
    del _L2_ffn_all

    def _L3_gnn_setup():
        import jax, jax.numpy as jnp
        import numpy as np
        N = 3125
        E = 100000
        F = 256
        O = 256
        EPS = 1e-05
        key = jax.random.key(seed)
        k0, k1, k2, k3, k4 = jax.random.split(key, 5)
        x = jax.random.normal(k0, (N, F), dtype=jnp.float32)
        edge_row = jax.random.randint(k1, (E,), 0, N, dtype=jnp.int32)
        edge_col = jax.random.randint(k2, (E,), 0, N, dtype=jnp.int32)
        edge_weight = jax.random.uniform(k3, (E,), dtype=jnp.float32)
        bound = float(np.sqrt(6.0 / (O + 2 * F)))
        W = jax.random.uniform(k4, (O, 2 * F), minval=-bound, maxval=bound, dtype=jnp.float32)
        gamma = jnp.ones((O,), dtype=jnp.float32)
        beta = jnp.zeros((O,), dtype=jnp.float32)
        return {'x': x, 'W': W, 'gamma': gamma, 'beta': beta, 'edge_weight': edge_weight, 'edge_row': edge_row, 'edge_col': edge_col}
    _L3_gnn_all = _L3_gnn_setup()
    _L3_gnn_in = {k: v for k, v in _L3_gnn_all.items() if k in ('W', 'gamma', 'beta')}
    del _L3_gnn_all

    def _L3_ffn_setup():
        import jax, jax.numpy as jnp
        import numpy as np
        B, K, D = (512, 16, 256)
        E = 32
        H = int(D * 0.25)
        key = jax.random.key(seed)
        ks = jax.random.split(key, 7)
        d_rs = D ** (-0.5)
        h_rs = H ** (-0.5)
        x = jax.random.normal(ks[0], (B, K, D), dtype=jnp.float32)
        router_w = jax.random.uniform(ks[1], (E, D), jnp.float32, -d_rs, d_rs)
        router_b = jax.random.uniform(ks[2], (E,), jnp.float32, -d_rs, d_rs)
        W1 = jax.random.uniform(ks[3], (E, D, H), jnp.float32, -h_rs, h_rs)
        b1 = jax.random.uniform(ks[4], (E, H), jnp.float32, -h_rs, h_rs)
        W2 = jax.random.uniform(ks[5], (E, H, D), jnp.float32, -d_rs, d_rs)
        b2 = jax.random.uniform(ks[6], (E, D), jnp.float32, -d_rs, d_rs)
        return {'x': x, 'router_w': router_w, 'router_b': router_b, 'W1': W1, 'b1': b1, 'W2': W2, 'b2': b2}
    _L3_ffn_all = _L3_ffn_setup()
    _L3_ffn_in = {k: v for k, v in _L3_ffn_all.items() if k in ('router_w', 'router_b', 'W1', 'b1', 'W2', 'b2')}
    del _L3_ffn_all
    return {'x': x, 'src': src, 'dst': dst, 'edge_attr_3': edge_attr_3, 'edge_attr_64': edge_attr_64, 'edge_weight': edge_weight, 'L0_gnn_W': _L0_gnn_in['W'], 'L0_gnn_a_src': _L0_gnn_in['a_src'], 'L0_gnn_a_dst': _L0_gnn_in['a_dst'], 'L0_gnn_edge_W': _L0_gnn_in['edge_W'], 'L0_gnn_edge_b': _L0_gnn_in['edge_b'], 'L0_gnn_bias': _L0_gnn_in['bias'], 'L0_ffn_gamma': _L0_ffn_in['gamma'], 'L0_ffn_beta': _L0_ffn_in['beta'], 'L0_ffn_Wr': _L0_ffn_in['Wr'], 'L0_ffn_br': _L0_ffn_in['br'], 'L0_ffn_W1': _L0_ffn_in['W1'], 'L0_ffn_b1': _L0_ffn_in['b1'], 'L0_ffn_W2': _L0_ffn_in['W2'], 'L0_ffn_b2': _L0_ffn_in['b2'], 'L1_gnn_ln_g': _L1_gnn_in['ln_g'], 'L1_gnn_ln_b': _L1_gnn_in['ln_b'], 'L1_gnn_Wq': _L1_gnn_in['Wq'], 'L1_gnn_bq': _L1_gnn_in['bq'], 'L1_gnn_Wk': _L1_gnn_in['Wk'], 'L1_gnn_bk': _L1_gnn_in['bk'], 'L1_gnn_Wv': _L1_gnn_in['Wv'], 'L1_gnn_bv': _L1_gnn_in['bv'], 'L1_gnn_Wo': _L1_gnn_in['Wo'], 'L1_gnn_bo': _L1_gnn_in['bo'], 'L1_gnn_Wdk': _L1_gnn_in['Wdk'], 'L1_gnn_bdk': _L1_gnn_in['bdk'], 'L1_gnn_Wdv': _L1_gnn_in['Wdv'], 'L1_gnn_bdv': _L1_gnn_in['bdv'], 'L1_ffn_W_gat': _L1_ffn_in['W_gat'], 'L1_ffn_att_src': _L1_ffn_in['att_src'], 'L1_ffn_att_dst': _L1_ffn_in['att_dst'], 'L1_ffn_b_gat': _L1_ffn_in['b_gat'], 'L1_ffn_ln_gamma': _L1_ffn_in['ln_gamma'], 'L1_ffn_ln_beta': _L1_ffn_in['ln_beta'], 'L1_ffn_W1': _L1_ffn_in['W1'], 'L1_ffn_b1': _L1_ffn_in['b1'], 'L1_ffn_W2': _L1_ffn_in['W2'], 'L1_ffn_b2': _L1_ffn_in['b2'], 'L1_ffn_edge_index': _L1_ffn_in['edge_index'], 'L2_gnn_W1': _L2_gnn_in['W1'], 'L2_gnn_b1': _L2_gnn_in['b1'], 'L2_gnn_W2': _L2_gnn_in['W2'], 'L2_gnn_b2': _L2_gnn_in['b2'], 'L2_gnn_W3': _L2_gnn_in['W3'], 'L2_gnn_b3': _L2_gnn_in['b3'], 'L2_gnn_W4': _L2_gnn_in['W4'], 'L2_gnn_b4': _L2_gnn_in['b4'], 'L2_ffn_Wr': _L2_ffn_in['Wr'], 'L2_ffn_br': _L2_ffn_in['br'], 'L2_ffn_W1': _L2_ffn_in['W1'], 'L2_ffn_b1': _L2_ffn_in['b1'], 'L2_ffn_g1': _L2_ffn_in['g1'], 'L2_ffn_be1': _L2_ffn_in['be1'], 'L2_ffn_m1': _L2_ffn_in['m1'], 'L2_ffn_v1': _L2_ffn_in['v1'], 'L2_ffn_W2': _L2_ffn_in['W2'], 'L2_ffn_b2': _L2_ffn_in['b2'], 'L2_ffn_g2': _L2_ffn_in['g2'], 'L2_ffn_be2': _L2_ffn_in['be2'], 'L2_ffn_m2': _L2_ffn_in['m2'], 'L2_ffn_v2': _L2_ffn_in['v2'], 'L2_ffn_Wo': _L2_ffn_in['Wo'], 'L2_ffn_bo': _L2_ffn_in['bo'], 'L3_gnn_W': _L3_gnn_in['W'], 'L3_gnn_gamma': _L3_gnn_in['gamma'], 'L3_gnn_beta': _L3_gnn_in['beta'], 'L3_ffn_router_w': _L3_ffn_in['router_w'], 'L3_ffn_router_b': _L3_ffn_in['router_b'], 'L3_ffn_W1': _L3_ffn_in['W1'], 'L3_ffn_b1': _L3_ffn_in['b1'], 'L3_ffn_W2': _L3_ffn_in['W2'], 'L3_ffn_b2': _L3_ffn_in['b2']}

def reference(x, src, dst, edge_attr_3, edge_attr_64, edge_weight, L0_gnn_W, L0_gnn_a_src, L0_gnn_a_dst, L0_gnn_edge_W, L0_gnn_edge_b, L0_gnn_bias, L0_ffn_gamma, L0_ffn_beta, L0_ffn_Wr, L0_ffn_br, L0_ffn_W1, L0_ffn_b1, L0_ffn_W2, L0_ffn_b2, L1_gnn_ln_g, L1_gnn_ln_b, L1_gnn_Wq, L1_gnn_bq, L1_gnn_Wk, L1_gnn_bk, L1_gnn_Wv, L1_gnn_bv, L1_gnn_Wo, L1_gnn_bo, L1_gnn_Wdk, L1_gnn_bdk, L1_gnn_Wdv, L1_gnn_bdv, L1_ffn_W_gat, L1_ffn_att_src, L1_ffn_att_dst, L1_ffn_b_gat, L1_ffn_ln_gamma, L1_ffn_ln_beta, L1_ffn_W1, L1_ffn_b1, L1_ffn_W2, L1_ffn_b2, L1_ffn_edge_index, L2_gnn_W1, L2_gnn_b1, L2_gnn_W2, L2_gnn_b2, L2_gnn_W3, L2_gnn_b3, L2_gnn_W4, L2_gnn_b4, L2_ffn_Wr, L2_ffn_br, L2_ffn_W1, L2_ffn_b1, L2_ffn_g1, L2_ffn_be1, L2_ffn_m1, L2_ffn_v1, L2_ffn_W2, L2_ffn_b2, L2_ffn_g2, L2_ffn_be2, L2_ffn_m2, L2_ffn_v2, L2_ffn_Wo, L2_ffn_bo, L3_gnn_W, L3_gnn_gamma, L3_gnn_beta, L3_ffn_router_w, L3_ffn_router_b, L3_ffn_W1, L3_ffn_b1, L3_ffn_W2, L3_ffn_b2):
    import jax
    import jax.numpy as jnp

    def _L0_gnn_ref(x, W, a_src, a_dst, edge_W, edge_b, bias, edge_attr, edge_index):
        import jax, jax.numpy as jnp
        import numpy as np
        N = 50000
        E = 12500
        IN = 256
        H = 8
        D = 32
        EF = 3
        n = x.shape[0]
        h = (x @ W.T).reshape(n, H, D)
        src, dst = (edge_index[0], edge_index[1])
        h_src = h[src]
        h_dst = h[dst]
        alpha = jnp.einsum('ehd,hd->eh', h_src, a_src) + jnp.einsum('ehd,hd->eh', h_dst, a_dst)
        enc = jax.nn.relu(edge_attr @ edge_W.T + edge_b).reshape(-1, H, D)
        alpha = alpha + jnp.sum(enc * h_dst, axis=-1)
        alpha = jnp.where(alpha >= 0, alpha, 0.2 * alpha)
        amax = jax.ops.segment_max(alpha, dst, num_segments=n)
        ex = jnp.exp(alpha - amax[dst])
        denom = jax.ops.segment_sum(ex, dst, num_segments=n)
        attn = ex / jnp.maximum(denom[dst], 1e-10)
        out = jax.ops.segment_sum(h_src * attn[..., None], dst, num_segments=n)
        return out.reshape(n, H * D) + bias

    def _L0_ffn_ref(x, gamma, beta, Wr, br, W1, b1, W2, b2):
        import jax, jax.numpy as jnp
        import numpy as np
        E = 8
        K = 2
        D = 256
        H = 512
        DOUT = 256
        EPS = 1e-05
        mu = jnp.mean(x, axis=-1, keepdims=True)
        var = jnp.mean(jnp.square(x - mu), axis=-1, keepdims=True)
        xn = (x - mu) * jax.lax.rsqrt(var + EPS) * gamma + beta
        logits = jnp.einsum('bsd,de->bse', xn, Wr) + br
        top_vals, top_idx = jax.lax.top_k(logits, K)
        w = jax.nn.softmax(top_vals, axis=-1)
        w_full = jnp.einsum('bsk,bske->bse', w, jax.nn.one_hot(top_idx, E, dtype=w.dtype))
        y = jnp.zeros(x.shape[:-1] + (DOUT,), x.dtype)
        for e in range(E):
            h = jax.nn.gelu(jnp.einsum('bsd,dh->bsh', xn, W1[e]) + b1[e], approximate=False)
            y_e = jnp.einsum('bsh,hd->bsd', h, W2[e]) + b2[e]
            y = y + y_e * w_full[..., e, None]
        return y

    def _L1_gnn_ref(x, edge_index, edge_weight, edge_attr, ln_g, ln_b, Wq, bq, Wk, bk, Wv, bv, Wo, bo, Wdk, bdk, Wdv, bdv):
        import jax, jax.numpy as jnp
        import numpy as np
        H = 256
        R = 64
        N = 625
        E = 10000
        CUTOFF_LO = 0.0
        CUTOFF_UP = 5.0
        LN_EPS = 1e-05

        def _layernorm(x, g, b):
            mu = jnp.mean(x, axis=-1, keepdims=True)
            var = jnp.var(x, axis=-1, keepdims=True)
            return (x - mu) * jax.lax.rsqrt(var + LN_EPS) * g + b

        def _cosine_cutoff(r):
            c = 0.5 * (jnp.cos(r * (jnp.pi / CUTOFF_UP)) + 1.0)
            return c * (r < CUTOFF_UP).astype(r.dtype)
        src = edge_index[0]
        dst = edge_index[1]
        x_norm = _layernorm(x, ln_g, ln_b)
        q = x_norm @ Wq.T + bq
        k = x_norm @ Wk.T + bk
        v = x_norm @ Wv.T + bv
        dk = jax.nn.silu(edge_attr @ Wdk.T + bdk)
        dv = jax.nn.silu(edge_attr @ Wdv.T + bdv)
        q_i = q[dst]
        k_j = k[src]
        v_j = v[src]
        attn = jnp.sum(q_i * k_j * dk, axis=1)
        attn = jax.nn.silu(attn) * _cosine_cutoff(edge_weight)
        msg = v_j * dv * attn[:, None]
        agg = jax.ops.segment_sum(msg, dst, num_segments=x.shape[0])
        out = agg @ Wo.T + bo
        return x + out

    def _L1_ffn_ref(x, W_gat, att_src, att_dst, b_gat, ln_gamma, ln_beta, W1, b1, W2, b2, edge_index):
        import jax, jax.numpy as jnp
        import numpy as np
        B, N, D = (16, 128, 256)
        NUM_EXPERTS, TOP_K, HEADS = (4, 2, 4)
        N_EDGES = 32768
        LN_EPS = 1e-05

        def _layernorm(x, g, b):
            mu = x.mean(-1, keepdims=True)
            var = ((x - mu) ** 2).mean(-1, keepdims=True)
            return (x - mu) * jax.lax.rsqrt(var + LN_EPS) * g + b

        def _forward(x, edge_index, W_gat, att_src, att_dst, b_gat, ln_gamma, ln_beta, W1, b1, W2, b2):
            Bc, Nc, Dc = x.shape
            M = Bc * Nc
            x_flat = x.reshape(M, Dc)
            h = (x_flat @ W_gat).reshape(M, HEADS, NUM_EXPERTS)
            loops = jnp.arange(M, dtype=edge_index.dtype)
            src = jnp.concatenate([edge_index[0], loops])
            dst = jnp.concatenate([edge_index[1], loops])
            a_src = (h * att_src).sum(-1)
            a_dst = (h * att_dst).sum(-1)
            e = jax.nn.leaky_relu(a_src[src] + a_dst[dst], negative_slope=0.2)
            e_max = jax.ops.segment_max(e, dst, num_segments=M)
            ee = jnp.exp(e - e_max[dst])
            denom = jax.ops.segment_sum(ee, dst, num_segments=M)
            alpha = ee / (denom[dst] + 1e-16)
            msg = h[src] * alpha[:, :, None]
            agg = jax.ops.segment_sum(msg, dst, num_segments=M).reshape(M, HEADS * NUM_EXPERTS) + b_gat
            scores = _layernorm(agg, ln_gamma, ln_beta).reshape(M, HEADS, NUM_EXPERTS).mean(1)
            scores = scores.reshape(Bc, Nc, NUM_EXPERTS)
            topk_s, topk_i = jax.lax.top_k(scores, TOP_K)
            w = jax.nn.softmax(topk_s, axis=-1)
            out = jnp.zeros_like(x)
            for ei in range(NUM_EXPERTS):
                g = jnp.where(topk_i == ei, w, 0.0).sum(-1)
                hh = jax.nn.gelu(x @ W1[ei] + b1[ei], approximate=False)
                out = out + g[..., None] * (hh @ W2[ei] + b2[ei])
            return out
        return _forward(x, edge_index, W_gat, att_src, att_dst, b_gat, ln_gamma, ln_beta, W1, b1, W2, b2)

    def _L2_gnn_ref(x, edge_index, W1, b1, W2, b2, W3, b3, W4, b4):
        import jax, jax.numpy as jnp
        import numpy as np
        N_NODES = 50000

        def _add_self_loops(src, dst, n):
            loop = jnp.arange(n, dtype=src.dtype)
            return (jnp.concatenate([src, loop]), jnp.concatenate([dst, loop]))

        def gcn_conv(x, src, dst, W, b, n):
            h = x @ W
            deg = jnp.zeros((n,), h.dtype).at[dst].add(1.0)
            dinv = jax.lax.rsqrt(jnp.maximum(deg, 1e-12))
            norm = dinv[src] * dinv[dst]
            msg = h[src] * norm[:, None]
            return jax.ops.segment_sum(msg, dst, num_segments=n) + b
        n = x.shape[0]
        src, dst = _add_self_loops(edge_index[0], edge_index[1], n)
        h = jax.nn.relu(gcn_conv(x, src, dst, W1, b1, n))
        z = jax.nn.relu(gcn_conv(h, src, dst, W2, b2, n))
        h = jax.nn.relu(gcn_conv(z, src, dst, W3, b3, n))
        x_hat = gcn_conv(h, src, dst, W4, b4, n)
        return x_hat

    def _L2_ffn_ref(x, Wr, br, W1, b1, g1, be1, m1, v1, W2, b2, g2, be2, m2, v2, Wo, bo):
        import jax, jax.numpy as jnp
        import numpy as np
        BN_EPS = 0.001

        def _bn(h, g, b, m, v):
            return g * (h - m) * jax.lax.rsqrt(v + BN_EPS) + b
        feat = jnp.mean(x, axis=0)
        w = jax.nn.softmax(feat @ Wr + br, axis=-1)
        h = jnp.einsum('bfd,edh->bfeh', x, W1) + b1
        h = jax.nn.relu(_bn(h, g1, be1, m1, v1))
        h = jnp.einsum('bfeh,ehk->bfek', h, W2) + b2
        h = jax.nn.relu(_bn(h, g2, be2, m2, v2))
        y = jnp.einsum('bfeh,ehd->bfed', h, Wo) + bo
        return jnp.einsum('bfed,fe->bfd', y, w)

    def _L3_gnn_ref(x, W, gamma, beta, edge_weight, edge_row, edge_col):
        import jax, jax.numpy as jnp
        import numpy as np
        N = 3125
        E = 100000
        F = 256
        O = 256
        EPS = 1e-05
        agg = jax.ops.segment_sum(edge_weight[:, None] * x[edge_col], edge_row, num_segments=x.shape[0])
        support = jnp.concatenate([agg, x], axis=1)
        out = support @ W.T
        mu = jnp.mean(out, axis=-1, keepdims=True)
        var = jnp.mean(jnp.square(out - mu), axis=-1, keepdims=True)
        out = (out - mu) * jax.lax.rsqrt(var + EPS) * gamma + beta
        return jax.nn.relu(out)

    def _L3_ffn_ref(x, router_w, router_b, W1, b1, W2, b2):
        import jax, jax.numpy as jnp
        import numpy as np
        B, K, D = (512, 16, 256)
        E = 32
        H = int(D * 0.25)
        xf = x.reshape(-1, D)
        logits = xf @ router_w.T + router_b
        idx = jnp.argmax(logits, axis=-1)
        w1t = jnp.take(W1, idx, axis=0)
        h = jnp.einsum('nd,ndh->nh', xf, w1t) + jnp.take(b1, idx, axis=0)
        h = jax.nn.relu(h)
        w2t = jnp.take(W2, idx, axis=0)
        out = jnp.einsum('nh,nhd->nd', h, w2t) + jnp.take(b2, idx, axis=0)
        out = jax.nn.relu(out)
        return out.reshape(x.shape)
    edge_index = jnp.stack([src, dst])
    x = x + _L0_gnn_ref(_layernorm(x, axis=-1), L0_gnn_W, L0_gnn_a_src, L0_gnn_a_dst, L0_gnn_edge_W, L0_gnn_edge_b, L0_gnn_bias, edge_attr_3, edge_index)
    x = x + _L0_ffn_ref(_layernorm(x, axis=-1)[None], L0_ffn_gamma, L0_ffn_beta, L0_ffn_Wr, L0_ffn_br, L0_ffn_W1, L0_ffn_b1, L0_ffn_W2, L0_ffn_b2)[0]
    x = x + _L1_gnn_ref(_layernorm(x, axis=-1), edge_index, edge_weight, edge_attr_64, L1_gnn_ln_g, L1_gnn_ln_b, L1_gnn_Wq, L1_gnn_bq, L1_gnn_Wk, L1_gnn_bk, L1_gnn_Wv, L1_gnn_bv, L1_gnn_Wo, L1_gnn_bo, L1_gnn_Wdk, L1_gnn_bdk, L1_gnn_Wdv, L1_gnn_bdv)
    x = x + _L1_ffn_ref(_layernorm(x, axis=-1)[None], L1_ffn_W_gat, L1_ffn_att_src, L1_ffn_att_dst, L1_ffn_b_gat, L1_ffn_ln_gamma, L1_ffn_ln_beta, L1_ffn_W1, L1_ffn_b1, L1_ffn_W2, L1_ffn_b2, L1_ffn_edge_index)[0]
    x = x + _L2_gnn_ref(_layernorm(x, axis=-1), edge_index, L2_gnn_W1, L2_gnn_b1, L2_gnn_W2, L2_gnn_b2, L2_gnn_W3, L2_gnn_b3, L2_gnn_W4, L2_gnn_b4)
    x = x + _L2_ffn_ref(_layernorm(x, axis=-1)[None], L2_ffn_Wr, L2_ffn_br, L2_ffn_W1, L2_ffn_b1, L2_ffn_g1, L2_ffn_be1, L2_ffn_m1, L2_ffn_v1, L2_ffn_W2, L2_ffn_b2, L2_ffn_g2, L2_ffn_be2, L2_ffn_m2, L2_ffn_v2, L2_ffn_Wo, L2_ffn_bo)[0]
    x = x + _L3_gnn_ref(_layernorm(x, axis=-1), L3_gnn_W, L3_gnn_gamma, L3_gnn_beta, edge_weight, src, dst)
    x = x + _L3_ffn_ref(_layernorm(x, axis=-1)[None], L3_ffn_router_w, L3_ffn_router_b, L3_ffn_W1, L3_ffn_b1, L3_ffn_W2, L3_ffn_b2)[0]
    return x

_drawn_inputs = setup_inputs


def setup_inputs(seed=0):
    import zlib

    import numpy as np

    out = dict(_drawn_inputs(seed))
    spreads = {'L0_gnn_edge_b': (0.0, 0.1),
     'L0_gnn_bias': (0.0, 0.1),
     'L0_ffn_br': (0.0, 0.1),
     'L1_gnn_ln_g': (1.0, 0.2),
     'L1_gnn_ln_b': (0.0, 0.1),
     'L1_gnn_bq': (0.0, 0.1),
     'L1_gnn_bk': (0.0, 0.1),
     'L1_gnn_bv': (0.0, 0.1),
     'L1_gnn_bo': (0.0, 0.308),
     'L1_gnn_bdk': (0.0, 0.1),
     'L1_gnn_bdv': (0.0, 0.1),
     'L1_ffn_b_gat': (0.0, 0.1),
     'L1_ffn_ln_gamma': (1.0, 0.6),
     'L1_ffn_ln_beta': (0.0, 0.458),
     'L1_ffn_b1': (0.0, 0.608),
     'L1_ffn_b2': (0.0, 0.436),
     'L2_gnn_b1': (0.0, 0.8),
     'L2_gnn_b2': (0.0, 0.8),
     'L2_gnn_b3': (0.0, 1.617),
     'L2_gnn_b4': (0.0, 0.9),
     'L2_ffn_br': (0.0, 2.0),
     'L2_ffn_b1': (0.0, 0.8),
     'L2_ffn_g1': (1.0, 0.6),
     'L2_ffn_be1': (0.0, 0.8),
     'L2_ffn_m1': (0.0, 0.8),
     'L2_ffn_v1': (1.0, 0.6),
     'L2_ffn_b2': (0.0, 0.8),
     'L2_ffn_g2': (1.0, 0.6),
     'L2_ffn_be2': (0.0, 0.8),
     'L2_ffn_m2': (0.0, 0.8),
     'L2_ffn_v2': (1.0, 0.6),
     'L2_ffn_bo': (0.0, 0.672),
     'L3_gnn_gamma': (1.0, 0.541),
     'L3_gnn_beta': (0.0, 1.428)}
    factors = {'L0_ffn_gamma': 3.513,
     'L0_ffn_beta': 2.961,
     'L0_ffn_b1': 8.0,
     'L1_ffn_att_src': 7.4,
     'L1_ffn_att_dst': 44.135,
     'L2_gnn_W1': 8.0,
     'L2_gnn_W2': 4.489,
     'L2_gnn_W3': 4.028,
     'L3_ffn_router_b': 39.102,
     'L3_ffn_b1': 64.0,
     'L3_ffn_b2': 30.679,
     'L0_ffn_b2': 4.163,
     'L3_ffn_router_w': 3.176,
     'L3_ffn_W1': 6.042,
     'L3_ffn_W2': 4.388}
    for name, (base, spread) in spreads.items():
        noise = np.random.default_rng([zlib.crc32(name.encode()), seed]).standard_normal(out[name].shape)
        drawn = base * np.exp(spread * noise) if base else spread * noise
        out[name] = jnp.asarray(drawn.astype(out[name].dtype))
    for name, factor in factors.items():
        out[name] = (out[name] * factor).astype(out[name].dtype)
    return out
```

```python
from contextlib import ExitStack, contextmanager

import numpy as np

import concourse.bass as bass
from concourse import mybir
from concourse.alu_op_type import AluOpType as ALU

ACT = mybir.ActivationFunctionType
AX = mybir.AxisListType
F32 = mybir.dt.float32
I32 = mybir.dt.int32

P = 128
N = 3125
NT = -(-N // P)
NP = NT * P
NB = 5
NTAB = NP + P
D = 256
KC = D // P
EDGES = 53125
T1 = -(-EDGES // P)
ROUTES = 32768
T2 = ROUTES // P
NEG = -1.0e30
EPS = 1e-5

U = 8
LAG = 4
CHAINS = 4
MCHAINS = 8

SRC_G, DST_G, SRC_S, DST_S, SRC_F, DST_F, WGT, CUT, ATTR = range(9)
EC = 12


def past(value):
    return max(value, 0) if isinstance(value, int) else value


def ready(t):
    return t + 1


def freed(t, ring):
    return past(t + 1 - ring)


def landed(i):
    return 16 * i + 16


def reused(i):
    return 16 * i


class Kernel:
    def __init__(self, nc, ins, out):
        self.nc, self.ins, self.out = nc, ins, out

    @contextmanager
    def phase(self):
        nc, sems = self.nc, []

        def sem(name):
            sems.append(nc.alloc_semaphore(f"{name}_{nc.next_id()}"))
            return sems[-1]
        with ExitStack() as ctx:
            def sb(name, shape, dt=F32):
                return ctx.enter_context(nc.sbuf_tensor(f"{name}_{nc.next_id()}", shape, dt))

            def ps(name, shape, dt=F32):
                return ctx.enter_context(nc.psum_tensor(f"{name}_{nc.next_id()}", shape, dt))
            yield sem, sb, ps
            nc.clear_and_free_semaphores(sems)
            nc.all_engine_barrier()

    def dram(self, name, shape, dt=F32):
        return self.nc.dram_tensor(name, shape, dt, kind="Internal").ap()


def tiles_loop(eng, tiles, body, *ahead, unroll=U):
    steps = tiles // unroll
    for before in range(max([lag for lag, _ in ahead], default=0), 0, -1):
        for lag, do in ahead:
            if lag >= before:
                do(0, lag - before)

    def step(i, last):
        for u in range(unroll):
            for lag, do in ahead:
                if not (last and u + lag >= unroll):
                    do(i + (u + lag) // unroll, (u + lag) % unroll)
            body(i, u)
    step(0, False)
    with eng.Fori(1, steps - 1) as i:
        step(i, False)
    step(steps - 1, True)


def nodes(table):
    return table[0:NP, :].rearrange("(j p) w -> p j w", p=P)


def build_constants(k):
    nc = k.nc
    with k.phase() as (sem, sb, ps):
        iota_i = sb("iota_i", [P, P], I32)
        row_i = sb("row_i", [P, 1], I32)
        made = sem("made")
        with nc.Block() as block:
            @block.gpsimd
            def _(pool):
                pool.iota(iota_i[:, :], [[1, P]], base=0, channel_multiplier=0).then_inc(made, 1)
                pool.iota(row_i[:, :], [[1, 1]], base=0, channel_multiplier=1).then_inc(made, 1)

            @block.vector
            def _(dve):
                dve.wait_ge(made, 2)
                dve.tensor_copy(k.col[:, :], iota_i[:, :])
                dve.tensor_copy(k.row[:, :], row_i[:, :])
                dve.memset(k.ones[:, :], 1.0)
                dve.memset(k.x[:, :, :], 0.0)
                dve.drain()
                dve.tensor_scalar(k.ident[:, :], k.col[:, :], k.row[:, 0:1], None, ALU.is_equal)
                dve.tensor_scalar(k.lower[:, :], k.col[:, :], k.row[:, 0:1], None, ALU.is_lt)


def fill_tables(k, fills):
    nc = k.nc
    widest = NTAB // P * max(table.shape[1] for table, _ in fills)
    with k.phase() as (sem, sb, ps):
        values = sorted({v for _, v in fills}, reverse=True)
        fill = [sb(f"fill{n}", [P, max(NTAB // P * table.shape[1] for table, v in fills if v == value)])
                for n, value in enumerate(values)]
        filled, stored, loaded = sem("filled"), sem("stored"), sem("loaded")
        with nc.Block() as block:
            @block.vector
            def _(dve):
                for n, value in enumerate(values):
                    dve.memset(fill[n][:, :], value).then_inc(filled, 1)

            @block.sync
            def _(sp):
                sp.dma_start(k.x[:, 0:NT - 1, :],
                             k.ins["x"][0:(NT - 1) * P, :].rearrange("(j p) w -> p j w", p=P)).then_inc(loaded, 16)
                sp.dma_start(k.x[0:N - (NT - 1) * P, NT - 1, :], k.ins["x"][(NT - 1) * P:N, :]).then_inc(loaded, 16)
                sp.wait_ge(filled, len(values))
                for table, value in fills:
                    w = table.shape[1]
                    sp.dma_start(table.rearrange("(p r) w -> p (r w)", p=P),
                                 fill[values.index(value)][:, 0:NTAB // P * w]).then_inc(stored, 16)
                sp.wait_ge(stored, 16 * len(fills))
                sp.wait_ge(loaded, 32)


def build_edges(k, meta, tiles, edges, src, dst, weight=None, attr=None):
    nc = k.nc
    full = edges // tiles
    rest = edges - full * tiles
    R = 4
    assert not rest or full == P - 1
    with k.phase() as (sem, sb, ps):
        em = sb("em", [P, tiles, EC], I32)
        ids = sb("ids", [P, 2, tiles], I32)
        wt = sb("wt", [P, tiles])
        at = sb("at", [P, tiles, 3])
        pad = sb("pad", [P, tiles])
        num = sb("num", [P, 2, tiles])
        dup = sb("dup", [P, 2, tiles])
        tmp = sb("tmp", [P, 2, tiles])
        cell = sb("cell", [P, R, 2])
        junk = sb("junk", [P, R, 2, P])
        row_of = ps("row_of", [P, R, 512])
        cleared, loaded, numbered, stored = sem("cleared"), sem("loaded"), sem("numbered"), sem("stored")
        cell_ready, row_ready, dup_ready = sem("cell_ready"), sem("row_ready"), sem("dup_ready")
        angle_ready, cos_ready, packed = sem("angle_ready"), sem("cos_ready"), sem("packed")
        places = sem("places")
        step_act, step_pe, step_dve = sem("step_act"), sem("step_pe"), sem("step_dve")
        emf = em[:, :, :].bitcast(F32)
        loads = [(ids[:, 0, :], src), (ids[:, 1, :], dst)] + ([(wt[:, :], weight)] if weight is not None else [])
        n_loads = 16 * (len(loads) + (attr is not None)) * (2 if rest else 1)
        with nc.Block() as block:
            @block.sync
            def _(sp):
                sp.wait_ge(cleared, 1)
                for to, array in loads:
                    sp.dma_start(to[0:full, :], array[0:full * tiles].rearrange("(p t) -> p t", t=tiles))\
                        .then_inc(loaded, 16)
                    if rest:
                        sp.dma_start(to[full:full + 1, 0:rest],
                                     array[full * tiles:edges].rearrange("(p t) -> p t", p=1)).then_inc(loaded, 16)
                if attr is not None:
                    sp.dma_start(at[0:full, :, :], attr[0:full * tiles, :].rearrange("(p t) c -> p t c", t=tiles))\
                        .then_inc(loaded, 16)
                    if rest:
                        sp.dma_start(at[full:full + 1, 0:rest, :],
                                     attr[full * tiles:edges, :].rearrange("(p t) c -> p t c", p=1))\
                            .then_inc(loaded, 16)
                sp.wait_ge(packed, 1)
                sp.dma_start(meta.rearrange("(p t) c -> p (t c)", p=P), em[:, :, :].rearrange("p t c -> p (t c)"))\
                    .then_inc(stored, 16)
                sp.wait_ge(stored, 16)

            @block.gpsimd
            def _(pool):
                pool.iota(em[:, :, 0], [[1, tiles]], base=0, channel_multiplier=tiles).then_inc(places, 1)

            @block.vector
            def _(dve):
                dve.memset(ids[:, :, :], 0)
                dve.memset(wt[:, :], 0.0)
                dve.memset(at[:, :, :], 0.0)
                dve.memset(dup[:, :, :], 0.0)
                dve.drain()
                dve.memset(tmp[:, :, :], 0.0).then_inc(cleared, 1)
                dve.wait_ge(places, 1)
                dve.wait_ge(loaded, n_loads)
                dve.tensor_copy(tmp[:, 0, :], em[:, :, 0])
                dve.drain()
                dve.tensor_scalar(pad[:, :], tmp[:, 0, :], float(edges), float(NTAB - 1), ALU.is_ge, ALU.mult)
                dve.tensor_copy(num[:, :, :], ids[:, :, :])
                dve.drain()
                for s in range(2):
                    dve.tensor_tensor(num[:, s, :], num[:, s, :], pad[:, :], ALU.add)
                dve.scalar_tensor_tensor(tmp[:, 0, :], wt[:, :], -1.0, wt[:, :], ALU.mult, ALU.max)
                dve.drain()
                dve.tensor_scalar(tmp[:, 0, :], tmp[:, 0, :], 5.0, -float(np.pi / 5), ALU.min, ALU.mult)
                dve.drain()
                dve.tensor_scalar(tmp[:, 0, :], tmp[:, 0, :], float(np.pi / 2), None, ALU.add).then_inc(angle_ready, 1)
                dve.drain()
                dve.sem_inc(numbered, 1)

                def count(i, r):
                    dve.wait_ge(row_ready, ready(i * R + r))
                    dve.sem_inc(step_dve, 1)
                    for s in range(2):
                        done = dve.scalar_tensor_tensor(junk[:, r, s, :], row_of[:, r, s * P:(s + 1) * P],
                                                 num[:, s, bass.ds(i * R + r, 1)], k.lower[:, :],
                                                 ALU.is_equal, ALU.mult,
                                                 accum_out=dup[:, s, bass.ds(i * R + r, 1)])
                    done.then_inc(dup_ready, 1)
                tiles_loop(dve, tiles, count, unroll=R)
                dve.wait_ge(cos_ready, 1)
                dve.drain()
                dve.tensor_scalar(tmp[:, 0, :], tmp[:, 1, :], 0.5, 0.5, ALU.mult, ALU.add)
                dve.tensor_scalar(pad[:, :], wt[:, :], 5.0, None, ALU.is_lt)
                dve.drain()
                dve.tensor_tensor(emf[:, :, CUT], tmp[:, 0, :], pad[:, :], ALU.mult)
                dve.tensor_copy(emf[:, :, WGT], wt[:, :])
                dve.tensor_copy(emf[:, :, ATTR:ATTR + 3], at[:, :, :])
                dve.memset(emf[:, :, ATTR + 3], 1.0)
                dve.tensor_copy(emf[:, :, SRC_F], num[:, 0, :])
                dve.tensor_copy(emf[:, :, DST_F], num[:, 1, :])
                dve.tensor_copy(em[:, :, SRC_G], ids[:, 0, :])
                dve.tensor_copy(em[:, :, DST_G], ids[:, 1, :])
                dve.tensor_scalar(dup[:, :, :], dup[:, :, :], 0.0, None, ALU.is_gt)
                dve.drain()
                dve.tensor_scalar(tmp[:, :, :], num[:, :, :], -1.0, k.row[:, 0:1], ALU.mult, ALU.add)
                dve.drain()
                dve.tensor_scalar(tmp[:, :, :], tmp[:, :, :], float(NP), None, ALU.add)
                dve.drain()
                dve.tensor_tensor(tmp[:, :, :], tmp[:, :, :], dup[:, :, :], ALU.mult)
                dve.drain()
                dve.tensor_tensor(tmp[:, :, :], tmp[:, :, :], num[:, :, :], ALU.add)
                dve.drain()
                dve.tensor_copy(em[:, :, SRC_S], tmp[:, 0, :])
                dve.tensor_copy(em[:, :, DST_S], tmp[:, 1, :])
                dve.drain()
                dve.sem_inc(packed, 1)

            @block.scalar
            def _(act):
                act.wait_ge(angle_ready, 1)
                act.activation(tmp[:, 1, :], tmp[:, 0, :], ACT.Sin).then_inc(cos_ready, 1)
                act.wait_ge(numbered, 1)

                def pick(i, r):
                    act.wait_ge(row_ready, freed(i * R + r, R))
                    act.sem_inc(step_act, 1)
                    act.copy(cell[:, r, :], num[:, :, bass.ds(i * R + r, 1)].rearrange("p s t -> p (s t)"))\
                        .then_inc(cell_ready, 1)
                tiles_loop(act, tiles, pick, unroll=R)

            @block.tensor
            def _(pe):
                def spread(i, r):
                    pe.wait_ge(cell_ready, ready(i * R + r))
                    pe.wait_ge(dup_ready, freed(i * R + r, R))
                    pe.sem_inc(step_pe, 1)
                    for s in range(2):
                        done = pe.transpose(row_of[:, r, s * P:(s + 1) * P],
                                            cell[:, r, s:s + 1].to_broadcast([P, P]), k.ident[:, :])
                    done.then_inc(row_ready, 1)
                tiles_loop(pe, tiles, spread, unroll=R)


def layer_norm(k, source, target, gamma=None, beta=None):
    nc = k.nc
    width = source.shape[2]
    with k.phase() as (sem, sb, ps):
        stats = sb("stats", [P, NT, 6])
        mean = sb("mean", [P, NT])
        diff = sb("diff", [P, NT])
        var = sb("var", [P, NT])
        dev = sb("dev", [P, NT])
        scale = sb("scale", [P, width])
        shift = sb("shift", [P, width])
        var_ready, dev_ready, loaded = sem("var_ready"), sem("dev_ready"), sem("loaded")
        with nc.Block() as block:
            @block.sync
            def _(sp):
                if gamma is not None:
                    sp.dma_start(scale[:, :], gamma.partition_broadcast(P)).then_inc(loaded, 16)
                    sp.dma_start(shift[:, :], beta.partition_broadcast(P)).then_inc(loaded, 16)
                    sp.wait_ge(loaded, 32)

            @block.vector
            def _(dve):
                with dve.Fori(0, NT // NB) as i:
                    for u in range(NB):
                        dve.bn_stats(stats[:, bass.ds(i * NB + u, 1), :].rearrange("p a b -> p (a b)"),
                                     source[:, bass.ds(i * NB + u, 1), :].rearrange("p a b -> p (a b)"))
                dve.drain()
                dve.tensor_tensor(mean[:, :], stats[:, :, 1], stats[:, :, 4], ALU.add)
                dve.tensor_tensor(diff[:, :], stats[:, :, 1], stats[:, :, 4], ALU.subtract)
                dve.tensor_tensor(var[:, :], stats[:, :, 2], stats[:, :, 5], ALU.add)
                dve.drain()
                dve.tensor_tensor(diff[:, :], diff[:, :], diff[:, :], ALU.mult)
                dve.tensor_scalar(mean[:, :], mean[:, :], 0.5, None, ALU.mult)
                dve.tensor_scalar(var[:, :], var[:, :], 1.0 / width, EPS, ALU.mult, ALU.add)
                dve.drain()
                dve.scalar_tensor_tensor(var[:, :], diff[:, :], 0.25, var[:, :], ALU.mult, ALU.add)\
                    .then_inc(var_ready, 1)
                dve.wait_ge(dev_ready, 1)
                dve.reciprocal(var[:, :], dev[:, :])
                dve.drain()
                with dve.Fori(0, NT // NB) as i:
                    for u in range(NB):
                        j = bass.ds(i * NB + u, 1)
                        dve.tensor_scalar(target[:, j, :].rearrange("p a b -> p (a b)"),
                                          source[:, j, :].rearrange("p a b -> p (a b)"),
                                          mean[:, j], var[:, j], ALU.subtract, ALU.mult)
                if gamma is not None:
                    dve.wait_ge(loaded, 32)
                    dve.drain()
                    dve.tensor_tensor(target, target, scale[:, :].unsqueeze(1).to_broadcast([P, NT, width]), ALU.mult)
                    dve.drain()
                    dve.tensor_tensor(target, target, shift[:, :].unsqueeze(1).to_broadcast([P, NT, width]), ALU.add)

            @block.scalar
            def _(act):
                act.wait_ge(var_ready, 1)
                act.activation(dev[:, :], var[:, :], ACT.Sqrt).then_inc(dev_ready, 1)


def load(k, *pairs):
    nc = k.nc
    with k.phase() as (sem, sb, ps):
        loaded = sem("loaded")
        with nc.Block() as block:
            @block.sync
            def _(sp):
                for to, source in pairs:
                    sp.dma_start(to, source).then_inc(loaded, 16)
                sp.wait_ge(loaded, 16 * len(pairs))


def load_transposed(k, *pairs):
    nc = k.nc
    with k.phase() as (sem, sb, ps):
        natural, moves = [], []
        for n, (target, w) in enumerate(pairs):
            outs, inner = w.shape
            op, ip = min(P, outs), min(P, inner)
            tile = sb(f"natural{n}", [op, outs // op, inner])
            natural.append((tile, w, op))
            for o in range(outs // op):
                for c in range(inner // ip):
                    moves.append((target[0:ip, c, o * op:(o + 1) * op],
                                  tile[:, o, c * ip:(c + 1) * ip], ip, op))
        turned = ps("turned", [P, 4, 512])
        loaded, turn_ready, moved = sem("loaded"), sem("turn_ready"), sem("moved")
        with nc.Block() as block:
            @block.sync
            def _(sp):
                for tile, w, op in natural:
                    sp.dma_start(tile[:, :, :], w.rearrange("(a o) i -> o a i", o=op)).then_inc(loaded, 16)
                sp.wait_ge(loaded, 16 * len(natural))

            @block.tensor
            def _(pe):
                pe.wait_ge(loaded, 16 * len(natural))
                for n, (_, source, ip, op) in enumerate(moves):
                    if n >= 4:
                        pe.wait_ge(moved, n - 3)
                    pe.transpose(turned[0:ip, n % 4, 0:op], source, k.ident[0:op, 0:op]).then_inc(turn_ready, 1)

            @block.vector
            def _(dve):
                for n, (target, _, ip, op) in enumerate(moves):
                    dve.wait_ge(turn_ready, n + 1)
                    dve.tensor_copy(target, turned[0:ip, n % 4, 0:op]).then_inc(moved, 1)


def project(k, source, weights, target, bias=None, keep=None, add=False):
    nc = k.nc
    width = source.shape[2]
    kp = min(P, width)
    chunks = width // kp
    cols = target.shape[2] if target is not None else 0
    with k.phase() as (sem, sb, ps):
        staged = sb("staged", [P, NB, width])
        turned = sb("turned", [kp, NB, chunks, P])
        bank = ps("bank", [P, NB, 512])
        p_turned, p_out = bank[:, :, 0:2 * P], bank[:, :, 2 * P:512]
        stage_ready, turn_ready, turn_copied, out_ready, out_copied, kept = (
            sem("stage_ready"), sem("turn_ready"), sem("turn_copied"), sem("out_ready"), sem("out_copied"), sem("kept"))
        pace_act, pace_pe, pace_dve, pace_pool = sem("pace_act"), sem("pace_pe"), sem("pace_dve"), sem("pace_pool")

        def flat(tensor, i, u):
            return tensor[:, bass.ds(i * NB + u, 1), :].rearrange("p a b -> p (a b)")

        with nc.Block() as block:
            @block.gpsimd
            def _(pool):

                def stage(i, u):
                    pool.wait_ge(turn_ready, freed(i * NB + u, NB))
                    pool.sem_inc(pace_pool, 1)
                    pool.tensor_copy(staged[:, u, :], flat(source, i, u)).then_inc(stage_ready, 1)
                tiles_loop(pool, NT, stage, unroll=NB)

            @block.tensor
            def _(pe):

                def turn(i, u):
                    t = i * NB + u
                    pe.wait_ge(stage_ready, ready(t))
                    pe.wait_ge(turn_copied, freed(t, NB))
                    if cols:
                        pe.wait_ge(out_copied, freed(t, NB))
                    pe.sem_inc(pace_pe, 1)
                    for c in range(chunks):
                        done = pe.transpose(p_turned[0:kp, u, c * P:(c + 1) * P],
                                            staged[:, u, c * kp:(c + 1) * kp], k.ident[:, :])
                    done.then_inc(turn_ready, 1)

                def product(i, u):
                    t = i * NB + u
                    pe.wait_ge(turn_copied, ready(t))
                    pe.sem_inc(pace_pe, 1)
                    for c in range(chunks):
                        done = pe.matmul(p_out[:, u, 0:cols], turned[:, u, c, :], weights[0:kp, c, :],
                                         start=(c == 0), stop=(c == chunks - 1 and bias is None))
                    if bias is not None:
                        done = pe.matmul(p_out[:, u, 0:cols], k.ones[0:1, :], bias, start=False, stop=True)
                    done.then_inc(out_ready, 1)
                if cols:
                    tiles_loop(pe, NT, product, (1, turn), unroll=NB)
                else:
                    tiles_loop(pe, NT, turn, unroll=NB)

            @block.vector
            def _(dve):

                def copy(i, u):
                    t = i * NB + u
                    dve.wait_ge(turn_ready, ready(t))
                    if cols:
                        dve.wait_ge(out_ready, freed(t, NB))
                    if keep is not None:
                        dve.wait_ge(kept, freed(t, NB))
                    dve.sem_inc(pace_dve, 1)
                    dve.tensor_copy(turned[:, u, :, :].rearrange("p c n -> p (c n)"),
                                    p_turned[0:kp, u, 0:chunks * P]).then_inc(turn_copied, 1)
                tiles_loop(dve, NT, copy, unroll=NB)

            @block.scalar
            def _(act):

                def keep_turned(i, u):
                    act.wait_ge(turn_copied, ready(i * NB + u))
                    act.sem_inc(pace_act, 1)
                    act.copy(keep[0:kp, :, bass.ds((i * NB + u) * P, P)], turned[:, u, :, :]).then_inc(kept, 1)

                def copy_out(i, u):
                    act.wait_ge(out_ready, ready(i * NB + u))
                    act.sem_inc(pace_act, 1)
                    act.copy(flat(target, i, u), p_out[:, u, 0:cols]).then_inc(out_copied, 1)
                if cols and keep is not None:
                    tiles_loop(act, NT, copy_out, (1, keep_turned), unroll=NB)
                elif cols:
                    tiles_loop(act, NT, copy_out, unroll=NB)
                else:
                    tiles_loop(act, NT, keep_turned, unroll=NB)


def on_vector(k, work):
    with k.nc.Block() as block:
        @block.vector
        def _(dve):
            work(dve)
            dve.drain()


def on_scalar(k, work):
    with k.nc.Block() as block:
        @block.scalar
        def _(act):
            work(act)
            act.drain()


def wide(ap, j=NT):
    return ap.unsqueeze(1).to_broadcast([P, j, ap.shape[1]])


def head_scores(k, source, vector, target, scratch):
    heads = target.shape[2]
    w = source.shape[2]

    def work(dve):
        dve.tensor_tensor(scratch[:, :, 0:w], source, wide(vector), ALU.mult)
        dve.drain()
        dve.tensor_reduce(target, scratch[:, :, 0:w].rearrange('p j (h d) -> p j h d', h=heads), AX.X, ALU.add)
    on_vector(k, work)


def attention_maxima(k, meta, tiles, heads, src_scores, dst_rows, tables, alpha, edge_w=None):
    nc = k.nc
    dw = dst_rows.shape[1]
    de = dw - heads
    with k.phase() as (sem, sb, ps):
        edge = sb("edge", [P, U, EC], I32)
        edgef = edge[:, :, :].bitcast(F32)
        s_rows = [sb(f"s_rows{u}", [P, heads]) for u in range(U)]
        d_rows = [sb(f"d_rows{u}", [P, dw]) for u in range(U)]
        old = [sb(f"old{u}", [P, heads]) for u in range(U)]
        new = [sb(f"new{u}", [P, heads]) for u in range(U)]
        other = sb("other", [P, 2, P])
        junk = sb("junk", [P, heads, P])
        al = sb("al", [P, U, heads])
        part = sb("part", [P, 2, heads])
        attr = sb("attr", [4, 2, P])
        enc = sb("enc", [P, 2, D])
        prod = sb("prod", [P, D])
        p_dst = ps("p_dst", [P, 2, 512])
        p_enc = ps("p_enc", [P, 2, 512])
        p_al = ps("p_al", [P, 2, 1024])
        S = [sem(f"edge_in{u}") for u in range(U)]
        GS = [sem(f"src_in{u}") for u in range(U)]
        GD = [sem(f"dst_in{u}") for u in range(U)]
        GO = [sem(f"old_in{u}") for u in range(U)]
        OUT = [sem(f"new_out{u}") for u in range(U)]
        row_ready, other_ready, attr_ready, enc_ready, relu_ready, alpha_ready, spread_ready, max_ready = (
            sem("row_ready"), sem("other_ready"), sem("attr_ready"), sem("enc_ready"), sem("relu_ready"),
            sem("alpha_ready"), sem("spread_ready"), sem("max_ready"))
        pace_act, pace_pe, pace_dve, pace_pool, pace_sp = (
            sem("pace_act"), sem("pace_pe"), sem("pace_dve"), sem("pace_pool"), sem("pace_sp"))
        table_v = meta.rearrange("(p t) c -> p t c", p=P)
        with nc.Block() as block:
            @block.sync
            def _(sp):
                def fetch(i, u):
                    sp.wait_ge(OUT[u], reused(i))
                    sp.sem_inc(pace_sp, 1)
                    sp.dma_start(edge[:, u, :], table_v[:, bass.ds(i * U + u, 1), :].rearrange("p a c -> p (a c)"))\
                        .then_inc(S[u], 16)
                tiles_loop(sp, tiles, fetch)

            @block.gpsimd
            def _(pool):
                def gather(i, u):
                    pool.wait_ge(S[u], landed(i))
                    pool.wait_ge(alpha_ready, freed(i * U + u, U))
                    pool.wait_ge(max_ready, freed(i * U + u, U))
                    pool.wait_ge(OUT[u], reused(i))
                    pool.sem_inc(pace_pool, 1)
                    for to, table, c, s in ((s_rows, src_scores, SRC_G, GS), (d_rows, dst_rows, DST_G, GD)):
                        pool.indirect_dma_start(to[u][:, :], None, table,
                                                bass.IndirectOffsetOnAxis(ap=edge[:, u, c:c + 1], axis=0))\
                            .then_inc(s[u], 16)
                    pool.indirect_dma_start(old[u][:, :], None, tables[u],
                                            bass.IndirectOffsetOnAxis(ap=edge[:, u, DST_G:DST_G + 1], axis=0))\
                        .then_inc(GO[u], 16)

                def scatter(i, u):
                    pool.wait_ge(max_ready, ready(i * U + u))
                    pool.sem_inc(pace_pool, 1)
                    pool.indirect_dma_start(tables[u], bass.IndirectOffsetOnAxis(ap=edge[:, u, DST_S:DST_S + 1], axis=0),
                                            new[u][:, :], None).then_inc(OUT[u], 16)
                tiles_loop(pool, tiles, scatter, (LAG, gather))
                for u in range(U):
                    pool.wait_ge(OUT[u], landed(tiles // U - 1))

            @block.tensor
            def _(pe):

                def turn(i, u):
                    t, r = i * U + u, u % 2
                    pe.wait_ge(S[u], landed(i))
                    pe.wait_ge(other_ready, freed(t, 2))
                    if edge_w is not None:
                        pe.wait_ge(relu_ready, freed(t, 2))
                    pe.sem_inc(pace_pe, 1)
                    done = pe.transpose(p_dst[:, r, 0:P], edgef[:, u, DST_F:DST_F + 1].to_broadcast([P, P]),
                                        k.ident[:, :])
                    if edge_w is not None:
                        done = pe.transpose(p_enc[0:4, r, 0:P], edgef[:, u, ATTR:ATTR + 4], k.ident[:, :])
                    done.then_inc(row_ready, 1)

                def encode(i, u):
                    t, r = i * U + u, u % 2
                    pe.wait_ge(attr_ready, ready(t))
                    pe.sem_inc(pace_pe, 1)
                    pe.matmul(p_enc[:, r, 0:D], attr[:, r, :], edge_w, start=True, stop=True).then_inc(enc_ready, 1)

                def spread(i, u):
                    t, r = i * U + u, u % 2
                    pe.wait_ge(alpha_ready, ready(t))
                    pe.wait_ge(max_ready, freed(t, 2))
                    pe.sem_inc(pace_pe, 1)
                    for h in range(heads):
                        done = pe.transpose(p_al[:, r, h * P:(h + 1) * P],
                                            al[:, u, h:h + 1].to_broadcast([P, P]), k.ident[:, :])
                    done.then_inc(spread_ready, 1)
                tiles_loop(pe, tiles, spread, (3, turn), *([(2, encode)] if edge_w is not None else []))

            @block.scalar
            def _(act):
                if edge_w is None:
                    return

                def copy_attr(i, u):
                    act.wait_ge(row_ready, ready(i * U + u))
                    act.wait_ge(enc_ready, freed(i * U + u, 2))
                    act.sem_inc(pace_act, 1)
                    act.copy(attr[:, u % 2, :], p_enc[0:4, u % 2, 0:P]).then_inc(attr_ready, 1)

                def relu(i, u):
                    act.wait_ge(enc_ready, ready(i * U + u))
                    act.wait_ge(alpha_ready, freed(i * U + u, 2))
                    act.sem_inc(pace_act, 1)
                    act.activation(enc[:, u % 2, :], p_enc[:, u % 2, 0:D], ACT.Relu).then_inc(relu_ready, 1)
                tiles_loop(act, tiles, relu, (1, copy_attr))

            @block.vector
            def _(dve):

                def scores(i, u):
                    t, r = i * U + u, u % 2
                    dve.wait_ge(row_ready, ready(t))
                    dve.wait_ge(max_ready, freed(t, 2))
                    dve.sem_inc(pace_dve, 1)
                    dve.tensor_scalar(other[:, r, :], p_dst[:, r, 0:P], edgef[:, u, DST_F:DST_F + 1], NEG,
                                      ALU.not_equal, ALU.mult).then_inc(other_ready, 1)
                    dve.wait_ge(GS[u], landed(i))
                    dve.wait_ge(GD[u], landed(i))
                    dve.wait_ge(spread_ready, freed(t, U))
                    dve.wait_ge(alpha_ready, freed(t, 1))
                    dve.sem_inc(pace_dve, 1)
                    dve.tensor_tensor(part[:, 0, :], s_rows[u][:, :], d_rows[u][:, de:dw], ALU.add)
                    if edge_w is not None:
                        dve.wait_ge(relu_ready, ready(t))
                        dve.sem_inc(pace_dve, 1)
                        dve.tensor_tensor(prod[:, :], enc[:, r, :], d_rows[u][:, 0:de], ALU.mult)
                        dve.drain()
                        dve.tensor_reduce(part[:, 1, :], prod[:, :].rearrange("p (h d) -> p h d", h=heads),
                                          AX.X, ALU.add)
                        dve.drain()
                        dve.tensor_tensor(part[:, 0, :], part[:, 0, :], part[:, 1, :], ALU.add)
                    dve.drain()
                    dve.scalar_tensor_tensor(al[:, u, :], part[:, 0, :], 0.2, part[:, 0, :], ALU.mult, ALU.max)
                    dve.drain()
                    dve.tensor_copy(alpha[:, bass.ds(t, 1), :].rearrange("p a h -> p (a h)"), al[:, u, :])\
                        .then_inc(alpha_ready, 1)

                def maxima(i, u):
                    t, r = i * U + u, u % 2
                    dve.wait_ge(spread_ready, ready(t))
                    dve.wait_ge(GO[u], landed(i))
                    dve.wait_ge(max_ready, freed(t, 1))
                    dve.sem_inc(pace_dve, 1)
                    for h in range(heads):
                        done = dve.tensor_tensor_reduce(junk[:, h, :], p_al[:, r, h * P:(h + 1) * P], other[:, r, :],
                                                        1.0, old[u][:, h:h + 1], ALU.add, ALU.max,
                                                        new[u][:, h:h + 1])
                    done.then_inc(max_ready, 1)
                tiles_loop(dve, tiles, maxima, (1, scores))


def attention_sums(k, meta, tiles, heads, per, src_rows, maxima, alpha, sums):
    nc = k.nc
    fw = heads * per
    w = fw + heads
    sw = src_rows.shape[1]
    with k.phase() as (sem, sb, ps):
        edge = sb("edge", [P, U, EC], I32)
        edgef = edge[:, :, :].bitcast(F32)
        s_rows = [sb(f"s_rows{u}", [P, sw]) for u in range(U)]
        m_rows = [sb(f"m_rows{u}", [P, heads]) for u in range(U)]
        sent = [sb(f"sent{u}", [P, w]) for u in range(U)]
        same = sb("same", [P, 2, P])
        z = sb("z", [P, 2, heads])
        msg = sb("msg", [P, 2, w])
        p_dst = ps("p_dst", [P, 2, 512])
        p_sum = ps("p_sum", [P, 2, 512])
        S = [sem(f"edge_in{u}") for u in range(U)]
        GS = [sem(f"src_in{u}") for u in range(U)]
        GM = [sem(f"max_in{u}") for u in range(U)]
        OUT = [sem(f"sum_out{u}") for u in range(U)]
        row_ready, same_ready, z_ready, exp_ready, msg_ready, sum_ready, sent_ready = (
            sem("row_ready"), sem("same_ready"), sem("z_ready"), sem("exp_ready"), sem("msg_ready"),
            sem("sum_ready"), sem("sent_ready"))
        pace_act, pace_pe, pace_dve, pace_pool, pace_sp = (
            sem("pace_act"), sem("pace_pe"), sem("pace_dve"), sem("pace_pool"), sem("pace_sp"))
        table_v = meta.rearrange("(p t) c -> p t c", p=P)
        with nc.Block() as block:
            @block.sync
            def _(sp):
                def fetch(i, u):
                    sp.wait_ge(OUT[u], reused(i))
                    sp.sem_inc(pace_sp, 1)
                    sp.dma_start(edge[:, u, :], table_v[:, bass.ds(i * U + u, 1), :].rearrange("p a c -> p (a c)"))\
                        .then_inc(S[u], 16)
                tiles_loop(sp, tiles, fetch)

            @block.gpsimd
            def _(pool):
                def gather(i, u):
                    pool.wait_ge(S[u], landed(i))
                    pool.wait_ge(msg_ready, freed(i * U + u, U))
                    pool.sem_inc(pace_pool, 1)
                    for to, table, c, s in ((s_rows, src_rows, SRC_G, GS), (m_rows, maxima, DST_G, GM)):
                        pool.indirect_dma_start(to[u][:, :], None, table,
                                                bass.IndirectOffsetOnAxis(ap=edge[:, u, c:c + 1], axis=0))\
                            .then_inc(s[u], 16)

                def scatter(i, u):
                    pool.wait_ge(sent_ready, ready(i * U + u))
                    pool.wait_ge(OUT[(u - CHAINS) % U], landed(i) if u >= CHAINS else reused(i))
                    pool.sem_inc(pace_pool, 1)
                    pool.indirect_dma_start(sums[u % CHAINS],
                                            bass.IndirectOffsetOnAxis(ap=edge[:, u, DST_S:DST_S + 1], axis=0),
                                            sent[u][:, :], None, compute_op=ALU.add).then_inc(OUT[u], 16)
                tiles_loop(pool, tiles, scatter, (LAG, gather))
                for u in range(U):
                    pool.wait_ge(OUT[u], landed(tiles // U - 1))

            @block.tensor
            def _(pe):

                def turn(i, u):
                    pe.wait_ge(S[u], landed(i))
                    pe.wait_ge(same_ready, freed(i * U + u, 2))
                    pe.sem_inc(pace_pe, 1)
                    pe.transpose(p_dst[:, u % 2, 0:P], edgef[:, u, DST_F:DST_F + 1].to_broadcast([P, P]),
                                 k.ident[:, :]).then_inc(row_ready, 1)

                def add_up(i, u):
                    t = i * U + u
                    pe.wait_ge(same_ready, ready(t))
                    pe.wait_ge(msg_ready, ready(t))
                    pe.wait_ge(sent_ready, freed(t, 2))
                    pe.sem_inc(pace_pe, 1)
                    pe.matmul(p_sum[:, u % 2, 0:w], same[:, u % 2, :], msg[:, u % 2, :],
                              start=True, stop=True).then_inc(sum_ready, 1)
                tiles_loop(pe, tiles, add_up, (2, turn))

            @block.scalar
            def _(act):

                def exps(i, u):
                    t = i * U + u
                    act.wait_ge(z_ready, ready(t))
                    act.wait_ge(sum_ready, freed(t, 2))
                    act.sem_inc(pace_act, 1)
                    act.activation(msg[:, u % 2, fw:w], z[:, u % 2, :], ACT.Exp).then_inc(exp_ready, 1)

                def send(i, u):
                    t = i * U + u
                    act.wait_ge(sum_ready, ready(t))
                    act.wait_ge(OUT[u], reused(i))
                    act.sem_inc(pace_act, 1)
                    act.copy(sent[u][:, :], p_sum[:, u % 2, 0:w]).then_inc(sent_ready, 1)
                tiles_loop(act, tiles, send, (1, exps))

            @block.vector
            def _(dve):

                def shift(i, u):
                    t, r = i * U + u, u % 2
                    dve.wait_ge(row_ready, ready(t))
                    dve.wait_ge(sum_ready, freed(t, 2))
                    dve.sem_inc(pace_dve, 1)
                    dve.tensor_scalar(same[:, r, :], p_dst[:, r, 0:P], edgef[:, u, DST_F:DST_F + 1], None,
                                      ALU.is_equal).then_inc(same_ready, 1)
                    dve.wait_ge(GM[u], landed(i))
                    dve.wait_ge(exp_ready, freed(t, 2))
                    dve.wait_ge(z_ready, freed(t, 1))
                    dve.sem_inc(pace_dve, 1)
                    dve.tensor_tensor(z[:, r, :], alpha[:, bass.ds(t, 1), :].rearrange("p a h -> p (a h)"),
                                      m_rows[u][:, :], ALU.subtract)
                    dve.drain()
                    dve.tensor_scalar(z[:, r, :], z[:, r, :], 0.0, None, ALU.min).then_inc(z_ready, 1)

                def message(i, u):
                    t, r = i * U + u, u % 2
                    dve.wait_ge(exp_ready, ready(t))
                    dve.wait_ge(GS[u], landed(i))
                    dve.sem_inc(pace_dve, 1)
                    dve.tensor_tensor(msg[:, r, 0:fw].rearrange("p (h d) -> p h d", h=heads),
                                      s_rows[u][:, 0:fw].rearrange("p (h d) -> p h d", h=heads),
                                      msg[:, r, fw:w].unsqueeze(2).to_broadcast([P, heads, per]), ALU.mult)\
                        .then_inc(msg_ready, 1)
                tiles_loop(dve, tiles, message, (1, shift))


def gather_sums(k, sums, target):
    nc = k.nc
    with k.phase() as (sem, sb, ps):
        first, added = sem("first"), sem("added")
        with nc.Block() as block:
            @block.sync
            def _(sp):
                sp.dma_start(target, nodes(sums[0])).then_inc(first, 16)
                sp.wait_ge(first, 16)

            @block.gpsimd
            def _(pool):
                pool.wait_ge(first, 16)
                for c in range(1, len(sums)):
                    pool.dma_start(target, nodes(sums[c]), accum_op=ALU.add).then_inc(added, 16)
                    pool.wait_ge(added, 16 * c)


def gather_maxima(k, tables, target, scratch):
    c = len(tables)
    load(k, *[(scratch[:, i, :, :], nodes(tables[i])) for i in range(c)])

    def work(dve):
        dve.tensor_reduce(target, scratch[:, :, :, :].rearrange('p c j h -> p j h c'), AX.X, ALU.max)
    on_vector(k, work)


def store(k, *pairs):
    nc = k.nc
    with k.phase() as (sem, sb, ps):
        stored = sem("stored")
        with nc.Block() as block:
            @block.sync
            def _(sp):
                for to, source in pairs:
                    sp.dma_start(to, source).then_inc(stored, 16)
                sp.wait_ge(stored, 16 * len(pairs))


def layer0_gnn(k):
    ins, H0 = k.ins, 8
    t = k.t
    with ExitStack() as ctx:
        def sb(name, shape, dt=F32):
            return ctx.enter_context(k.nc.sbuf_tensor(f"{name}_g0", shape, dt))
        xn = sb("xn", [P, NT, D])
        rows = sb("rows", [P, NT, D + H0])
        layer_norm(k, k.x[:, :, :], xn[:, :, :])
        with k.nc.sbuf_tensor("wT_g0", [P, KC, D], F32) as wT:
            load_transposed(k, (wT, ins["L0_gnn_W"]))
            project(k, xn[:, :, :], wT[:, :, :], rows[:, :, 0:D])
        scores = sb("scores", [P, NT, H0])
        vec = sb("vec", [P, 3, D])
        ew = sb("ew", [4, D])
        ewT = sb("ewT", [4, 1, D])
        load(k, (vec[:, 0, :], ins["L0_gnn_a_src"].rearrange("h d -> (h d)").partition_broadcast(P)),
             (vec[:, 1, :], ins["L0_gnn_a_dst"].rearrange("h d -> (h d)").partition_broadcast(P)),
             (vec[:, 2, :], ins["L0_gnn_bias"].partition_broadcast(P)),
             (ew[3:4, :], ins["L0_gnn_edge_b"].rearrange("(a d) -> a d", a=1)))
        load_transposed(k, (ewT, ins["L0_gnn_edge_W"]))

        def work(dve):
            dve.tensor_copy(ew[0:3, :], ewT[0:3, 0, :])
        on_vector(k, work)
        head_scores(k, rows[:, :, 0:D], vec[:, 0, :], scores[:, :, :], xn)
        head_scores(k, rows[:, :, 0:D], vec[:, 1, :], rows[:, :, D:D + H0], xn)
        store(k, (nodes(t["rows0"]), rows[:, :, :]), (nodes(t["scores0"]), scores[:, :, :]))
        alpha = sb("alpha", [P, T1, H0])
        attention_maxima(k, k.meta1, T1, H0, t["scores0"], t["rows0"], t["max0"], alpha, ew[:, :])
        peak = sb("peak", [P, NT, H0])
        with k.nc.sbuf_tensor("all_g0", [P, MCHAINS, NT, H0], F32) as each:
            gather_maxima(k, t["max0"], peak[:, :, :], each)
        store(k, (nodes(t["peak0"]), peak[:, :, :]))
        attention_sums(k, k.meta1, T1, H0, D // H0, t["rows0"], t["peak0"], alpha, t["sum0"])
        gather_sums(k, t["sum0"], rows[:, :, :])
        den = rows[:, :, D:D + H0]
        num = rows[:, :, 0:D].rearrange("p j (h d) -> p j h d", h=H0)
        res = xn[:, :, :].rearrange("p j (h d) -> p j h d", h=H0)

        def divide(dve):
            for h in range(H0):
                dve.tensor_tensor(res[:, :, h, :], num[:, :, h, :],
                                  scores[:, :, h:h + 1].to_broadcast([P, NT, D // H0]), ALU.mult)

        def work(dve):
            dve.tensor_scalar(den, den, 1e-10, None, ALU.max)
            dve.drain()
            dve.reciprocal(scores[:, :, :], den)
            dve.drain()
            divide(dve)
            dve.drain()
            dve.tensor_tensor(xn[:, :, :], xn[:, :, :], wide(vec[:, 2, :]), ALU.add)
            dve.drain()
            dve.tensor_tensor(k.x[:, :, :], k.x[:, :, :], xn[:, :, :], ALU.add)
        on_vector(k, work)


def aggregate(k, meta, tiles, table, sums, gather_col, scatter_col, number_col, weighted=False):
    nc = k.nc
    w = table.shape[1]
    with k.phase() as (sem, sb, ps):
        edge = sb("edge", [P, U, EC], I32)
        edgef = edge[:, :, :].bitcast(F32)
        rows = [sb(f"rows{u}", [P, w]) for u in range(U)]
        sent = [sb(f"sent{u}", [P, w]) for u in range(U)]
        same = sb("same", [P, 2, P])
        p_num = ps("p_num", [P, 2, 512])
        p_sum = ps("p_sum", [P, 2, 512])
        S = [sem(f"edge_in{u}") for u in range(U)]
        G = [sem(f"rows_in{u}") for u in range(U)]
        OUT = [sem(f"sum_out{u}") for u in range(U)]
        row_ready, same_ready, sum_ready, sent_ready = (
            sem("row_ready"), sem("same_ready"), sem("sum_ready"), sem("sent_ready"))
        pace_act, pace_pe, pace_dve, pace_pool, pace_sp = (
            sem("pace_act"), sem("pace_pe"), sem("pace_dve"), sem("pace_pool"), sem("pace_sp"))
        table_v = meta.rearrange("(p t) c -> p t c", p=P)
        with nc.Block() as block:
            @block.sync
            def _(sp):
                def fetch(i, u):
                    sp.wait_ge(OUT[u], reused(i))
                    sp.sem_inc(pace_sp, 1)
                    sp.dma_start(edge[:, u, :], table_v[:, bass.ds(i * U + u, 1), :].rearrange("p a c -> p (a c)"))\
                        .then_inc(S[u], 16)
                tiles_loop(sp, tiles, fetch)

            @block.gpsimd
            def _(pool):
                def gather(i, u):
                    pool.wait_ge(S[u], landed(i))
                    pool.wait_ge(sum_ready, freed(i * U + u, U))
                    pool.sem_inc(pace_pool, 1)
                    pool.indirect_dma_start(rows[u][:, :], None, table,
                                            bass.IndirectOffsetOnAxis(ap=edge[:, u, gather_col:gather_col + 1], axis=0))\
                        .then_inc(G[u], 16)

                def scatter(i, u):
                    pool.wait_ge(sent_ready, ready(i * U + u))
                    pool.wait_ge(OUT[(u - CHAINS) % U], landed(i) if u >= CHAINS else reused(i))
                    pool.sem_inc(pace_pool, 1)
                    pool.indirect_dma_start(sums[u % CHAINS],
                                            bass.IndirectOffsetOnAxis(ap=edge[:, u, scatter_col:scatter_col + 1], axis=0),
                                            sent[u][:, :], None, compute_op=ALU.add).then_inc(OUT[u], 16)
                tiles_loop(pool, tiles, scatter, (LAG, gather))
                for u in range(U):
                    pool.wait_ge(OUT[u], landed(tiles // U - 1))

            @block.tensor
            def _(pe):
                def turn(i, u):
                    pe.wait_ge(S[u], landed(i))
                    pe.wait_ge(same_ready, freed(i * U + u, 2))
                    pe.sem_inc(pace_pe, 1)
                    pe.transpose(p_num[:, u % 2, 0:P], edgef[:, u, number_col:number_col + 1].to_broadcast([P, P]),
                                 k.ident[:, :]).then_inc(row_ready, 1)

                def add_up(i, u):
                    t = i * U + u
                    pe.wait_ge(same_ready, ready(t))
                    pe.wait_ge(G[u], landed(i))
                    pe.wait_ge(sent_ready, freed(t, 2))
                    pe.sem_inc(pace_pe, 1)
                    pe.matmul(p_sum[:, u % 2, 0:w], same[:, u % 2, :], rows[u][:, :],
                              start=True, stop=True).then_inc(sum_ready, 1)
                tiles_loop(pe, tiles, add_up, (2, turn))

            @block.scalar
            def _(act):
                def send(i, u):
                    t = i * U + u
                    act.wait_ge(sum_ready, ready(t))
                    act.wait_ge(OUT[u], reused(i))
                    act.sem_inc(pace_act, 1)
                    act.copy(sent[u][:, :], p_sum[:, u % 2, 0:w]).then_inc(sent_ready, 1)
                tiles_loop(act, tiles, send)

            @block.vector
            def _(dve):
                def compare(i, u):
                    t, r = i * U + u, u % 2
                    dve.wait_ge(row_ready, ready(t))
                    dve.wait_ge(sum_ready, freed(t, 2))
                    dve.sem_inc(pace_dve, 1)
                    number = edgef[:, u, number_col:number_col + 1]
                    if weighted:
                        dve.tensor_scalar(same[:, r, :], p_num[:, r, 0:P], number, edgef[:, u, WGT:WGT + 1],
                                          ALU.is_equal, ALU.mult).then_inc(same_ready, 1)
                    else:
                        dve.tensor_scalar(same[:, r, :], p_num[:, r, 0:P], number, None,
                                          ALU.is_equal).then_inc(same_ready, 1)
                tiles_loop(dve, tiles, compare)


def filtered_messages(k, queries, keyvals, radial, filters, sums):
    nc = k.nc
    tiles, meta = T1, k.meta1
    R = radial.shape[2]
    w = D + 1
    with k.phase() as (sem, sb, ps):
        edge = sb("edge", [P, U, EC], I32)
        edgef = edge[:, :, :].bitcast(F32)
        feats = sb("feats", [P, U, R])
        q_rows = [sb(f"q_rows{u}", [P, D]) for u in range(U)]
        kv_rows = [sb(f"kv_rows{u}", [P, 2 * D]) for u in range(U)]
        sent = [sb(f"sent{u}", [P, w]) for u in range(U)]
        same = sb("same", [P, 2, P])
        featT = sb("featT", [R + 1, 2, P])
        gates = sb("gates", [P, 2, 2 * D])
        qk = sb("qk", [P, D])
        junk = sb("junk", [P, D])
        vd = sb("vd", [P, 2, D])
        score = sb("score", [P, 2, 1])
        curve = sb("curve", [P, 2, 1])
        attn = sb("attn", [P, 2, 1])
        msg = sb("msg", [P, 2, w])
        p_num = ps("p_num", [P, 2, 512])
        p_filt = ps("p_filt", [P, 2, 512])
        p_sum = ps("p_sum", [P, 2, 512])
        p_feat = ps("p_feat", [P, 2, 512])
        S = [sem(f"edge_in{u}") for u in range(U)]
        F = [sem(f"feat_in{u}") for u in range(U)]
        GQ = [sem(f"q_in{u}") for u in range(U)]
        GK = [sem(f"kv_in{u}") for u in range(U)]
        OUT = [sem(f"sum_out{u}") for u in range(U)]
        row_ready, same_ready, sum_ready, sent_ready = (
            sem("row_ready"), sem("same_ready"), sem("sum_ready"), sem("sent_ready"))
        feat_ready, featT_ready, filt_ready, gates_ready, score_ready, curve_ready, msg_ready, ones_ready, attn_ready = (
            sem("feat_ready"), sem("featT_ready"), sem("filt_ready"), sem("gates_ready"), sem("score_ready"),
            sem("curve_ready"), sem("msg_ready"), sem("ones_ready"), sem("attn_ready"))
        pace_act, pace_pe, pace_dve, pace_pool, pace_sp = (
            sem("pace_act"), sem("pace_pe"), sem("pace_dve"), sem("pace_pool"), sem("pace_sp"))
        table_v = meta.rearrange("(p t) c -> p t c", p=P)
        with nc.Block() as block:
            @block.sync
            def _(sp):
                def fetch(i, u):
                    t = bass.ds(i * U + u, 1)
                    sp.wait_ge(OUT[u], reused(i))
                    sp.sem_inc(pace_sp, 1)
                    sp.dma_start(edge[:, u, :], table_v[:, t, :].rearrange("p a c -> p (a c)")).then_inc(S[u], 16)
                    sp.dma_start(feats[:, u, :], radial[:, t, :].rearrange("p a c -> p (a c)")).then_inc(F[u], 16)
                tiles_loop(sp, tiles, fetch)

            @block.gpsimd
            def _(pool):
                def gather(i, u):
                    pool.wait_ge(S[u], landed(i))
                    pool.wait_ge(msg_ready, freed(i * U + u, U))
                    pool.sem_inc(pace_pool, 1)
                    for to, table, c, s in ((q_rows, queries, DST_G, GQ), (kv_rows, keyvals, SRC_G, GK)):
                        pool.indirect_dma_start(to[u][:, :], None, table,
                                                bass.IndirectOffsetOnAxis(ap=edge[:, u, c:c + 1], axis=0))\
                            .then_inc(s[u], 16)

                def scatter(i, u):
                    pool.wait_ge(sent_ready, ready(i * U + u))
                    pool.wait_ge(OUT[(u - CHAINS) % U], landed(i) if u >= CHAINS else reused(i))
                    pool.sem_inc(pace_pool, 1)
                    pool.indirect_dma_start(sums[u % CHAINS],
                                            bass.IndirectOffsetOnAxis(ap=edge[:, u, DST_S:DST_S + 1], axis=0),
                                            sent[u][:, :], None, compute_op=ALU.add).then_inc(OUT[u], 16)
                tiles_loop(pool, tiles, scatter, (LAG, gather))
                for u in range(U):
                    pool.wait_ge(OUT[u], landed(tiles // U - 1))

            @block.tensor
            def _(pe):
                def turn(i, u):
                    t, r = i * U + u, u % 2
                    pe.wait_ge(S[u], landed(i))
                    pe.wait_ge(F[u], landed(i))
                    pe.wait_ge(same_ready, freed(t, 2))
                    pe.wait_ge(featT_ready, freed(t, 2))
                    pe.sem_inc(pace_pe, 1)
                    pe.transpose(p_num[:, r, 0:P], edgef[:, u, DST_F:DST_F + 1].to_broadcast([P, P]), k.ident[:, :])
                    pe.transpose(p_feat[0:R, r, 0:P], feats[:, u, :], k.ident[:, :]).then_inc(row_ready, 1)

                def filt(i, u):
                    t, r = i * U + u, u % 2
                    pe.wait_ge(featT_ready, ready(t))
                    pe.wait_ge(gates_ready, freed(t, 2))
                    pe.sem_inc(pace_pe, 1)
                    pe.matmul(p_filt[:, r, :], featT[:, r, :], filters, start=True, stop=True).then_inc(filt_ready, 1)

                def add_up(i, u):
                    t, r = i * U + u, u % 2
                    pe.wait_ge(same_ready, ready(t))
                    pe.wait_ge(msg_ready, ready(t))
                    pe.wait_ge(sent_ready, freed(t, 2))
                    pe.sem_inc(pace_pe, 1)
                    pe.matmul(p_sum[:, r, 0:w], same[:, r, :], msg[:, r, :], start=True, stop=True)\
                        .then_inc(sum_ready, 1)
                tiles_loop(pe, tiles, add_up, (3, turn), (2, filt))

            @block.scalar
            def _(act):
                def copy_feat(i, u):
                    t, r = i * U + u, u % 2
                    act.wait_ge(row_ready, ready(t))
                    act.wait_ge(filt_ready, freed(t, 2))
                    act.wait_ge(ones_ready, 1)
                    act.sem_inc(pace_act, 1)
                    act.copy(featT[0:R, r, :], p_feat[0:R, r, 0:P]).then_inc(featT_ready, 1)

                def gate(i, u):
                    t, r = i * U + u, u % 2
                    act.wait_ge(filt_ready, ready(t))
                    act.wait_ge(msg_ready, freed(t, 2))
                    act.sem_inc(pace_act, 1)
                    act.activation(gates[:, r, :], p_filt[:, r, :], ACT.Silu).then_inc(gates_ready, 1)

                def attention(i, u):
                    t, r = i * U + u, u % 2
                    act.wait_ge(score_ready, ready(t))
                    act.wait_ge(attn_ready, freed(t, 2))
                    act.sem_inc(pace_act, 1)
                    act.activation(curve[:, r, :], score[:, r, :], ACT.Silu).then_inc(curve_ready, 1)

                def send(i, u):
                    t = i * U + u
                    act.wait_ge(sum_ready, ready(t))
                    act.wait_ge(OUT[u], reused(i))
                    act.sem_inc(pace_act, 1)
                    act.copy(sent[u][:, :], p_sum[:, u % 2, 0:w]).then_inc(sent_ready, 1)
                tiles_loop(act, tiles, send, (3, copy_feat), (2, gate), (1, attention))

            @block.vector
            def _(dve):
                dve.memset(featT[R:R + 1, :, :], 1.0).then_inc(ones_ready, 1)
                dve.memset(msg[:, :, D:w], 1.0)

                def compare(i, u):
                    t, r = i * U + u, u % 2
                    dve.wait_ge(row_ready, ready(t))
                    dve.wait_ge(sum_ready, freed(t, 2))
                    dve.sem_inc(pace_dve, 1)
                    dve.tensor_scalar(same[:, r, :], p_num[:, r, 0:P], edgef[:, u, DST_F:DST_F + 1], None,
                                      ALU.is_equal).then_inc(same_ready, 1)

                def scores(i, u):
                    t, r = i * U + u, u % 2
                    dve.wait_ge(GQ[u], landed(i))
                    dve.wait_ge(GK[u], landed(i))
                    dve.wait_ge(score_ready, freed(t, 1))
                    dve.wait_ge(curve_ready, freed(t, 2))
                    dve.sem_inc(pace_dve, 1)
                    dve.tensor_tensor(qk[:, :], q_rows[u][:, :], kv_rows[u][:, 0:D], ALU.mult)
                    dve.wait_ge(gates_ready, ready(t))
                    dve.wait_ge(msg_ready, freed(t, 2))
                    dve.sem_inc(pace_dve, 1)
                    dve.tensor_tensor(vd[:, r, :], kv_rows[u][:, D:2 * D], gates[:, r, D:2 * D], ALU.mult)
                    dve.drain()
                    dve.tensor_tensor_reduce(junk[:, :], qk[:, :], gates[:, r, 0:D], 1.0, 0.0, ALU.mult, ALU.add,
                                             score[:, r, :]).then_inc(score_ready, 1)

                def message(i, u):
                    t, r = i * U + u, u % 2
                    dve.wait_ge(curve_ready, ready(t))
                    dve.wait_ge(sum_ready, freed(t, 2))
                    dve.wait_ge(msg_ready, freed(t, 1))
                    dve.sem_inc(pace_dve, 1)
                    dve.tensor_tensor(attn[:, r, :], curve[:, r, :], edgef[:, u, CUT:CUT + 1], ALU.mult)\
                        .then_inc(attn_ready, 1)
                    dve.wait_ge(attn_ready, ready(t))
                    dve.sem_inc(pace_dve, 1)
                    dve.tensor_scalar(msg[:, r, 0:D], vd[:, r, :], attn[:, r, 0:1], None, ALU.mult)\
                        .then_inc(msg_ready, 1)
                tiles_loop(dve, tiles, message, (1, compare), (1, scores))


def experts(k, xT, gate, out, count, hidden, last, outs=1):
    nc = k.nc
    units = count // outs
    blocks = NT // NB
    cols = NB * P
    half = cols // 2
    per_body = 2 * blocks
    chunks = sum(h[1] for h in hidden)
    rows_last = P // outs
    with k.phase() as (sem, sb, ps):
        w = [[sb(f"w{s}_{n}", [P, h[3], h[1] * P]) for n, h in enumerate(hidden)] for s in range(2)]
        wo = [sb(f"wo{s}", [P, last[1], D]) for s in range(2)]
        hid = [[sb(f"hid{s}_{n}", [P, h[1], cols]) for n, h in enumerate(hidden)] for s in range(2)]
        p_hid = ps("p_hid", [P, 2, 2, 512])
        p_out = ps("p_out", [P, 2, 512])
        W = [sem(f"weights_in{s}") for s in range(2)]
        hid_ready, hid_copied, out_ready, out_added = (
            sem("hid_ready"), sem("hid_copied"), sem("out_ready"), sem("out_added"))
        pace_act, pace_pe, pace_dve, pace_sp = sem("pace_act"), sem("pace_pe"), sem("pace_dve"), sem("pace_sp")
        loads = len(hidden) + 1
        ys = NB * outs
        first = [sum(h[1] for h in hidden[:n]) for n in range(len(hidden))]

        def unit_loop(eng, body):
            body(0)
            with eng.Fori(1, units // 2) as i:
                body(i)

        with nc.Block() as block:
            @block.sync
            def _(sp):
                def fetch(i):
                    for s in range(2):
                        sp.wait_ge(out_ready, past(((i - 1) * per_body + (s + 1) * blocks) * ys))
                        sp.sem_inc(pace_sp, 1)
                        e = (2 * i + s) * outs
                        for n, h in enumerate(hidden):
                            for to, source in h[0](w[s][n], e):
                                sp.dma_start(to, source).then_inc(W[s], 16)
                        sp.dma_start(wo[s][:, :, :], last[0](e)).then_inc(W[s], 16)
                unit_loop(sp, fetch)
            loads = sum(len(h[0](w[0][n], 0)) for n, h in enumerate(hidden)) + 1

            @block.tensor
            def _(pe):
                def layer(i, b, n):
                    s, it = b // blocks, i * per_body + b
                    _, outc, _, inc = hidden[n]
                    at = (b % blocks) * cols
                    for c in range(outc):
                        q = it * chunks + first[n] + c
                        qs = (b * chunks + first[n] + c) % 2
                        if n == 0 and b % blocks == 0 and c == 0:
                            pe.wait_ge(W[s], 16 * loads * (i + 1))
                        if n and c == 0:
                            pe.wait_ge(hid_copied, it * chunks + first[n])
                        pe.wait_ge(hid_copied, freed(q, 2))
                        pe.sem_inc(pace_pe, 1)
                        for z in range(2):
                            for kc in range(inc):
                                if n == 0:
                                    rhs = xT[:, kc, at + z * half:at + (z + 1) * half]
                                else:
                                    rhs = hid[b % 2][n - 1][:, kc, z * half:(z + 1) * half]
                                done = pe.matmul(p_hid[:, qs, z, 0:half], w[s][n][:, kc, c * P:(c + 1) * P], rhs,
                                                 start=(kc == 0), stop=(kc == inc - 1))
                        done.then_inc(hid_ready, 1)

                def finish(i, b):
                    s, it = b // blocks, i * per_body + b
                    pe.wait_ge(hid_copied, (it + 1) * chunks)
                    pe.sem_inc(pace_pe, 1)
                    for o in range(outs):
                        p0 = o * rows_last
                        for j in range(NB):
                            y = it * ys + o * NB + j
                            pe.wait_ge(out_added, freed(y, 2))
                            pe.sem_inc(pace_pe, 1)
                            for kc in range(last[1]):
                                done = pe.matmul(p_out[:, (b * ys + o * NB + j) % 2, 0:D],
                                                 hid[b % 2][-1][p0:p0 + rows_last, kc, j * P:(j + 1) * P],
                                                 wo[s][p0:p0 + rows_last, kc, :],
                                                 start=(kc == 0), stop=(kc == last[1] - 1))
                            done.then_inc(out_ready, 1)

                def body(i):
                    for b in range(per_body):
                        layer(i, b, 0)
                        if b:
                            finish(i, b - 1)
                        for n in range(1, len(hidden)):
                            layer(i, b, n)
                    finish(i, per_body - 1)
                unit_loop(pe, body)

            @block.scalar
            def _(act):
                def body(i):
                    for b in range(per_body):
                        it = i * per_body + b
                        e = (2 * i + b // blocks)
                        for n, (_, outc, func, _) in enumerate(hidden):
                            for c in range(outc):
                                q = it * chunks + first[n] + c
                                qs = (b * chunks + first[n] + c) % 2
                                act.wait_ge(hid_ready, q + 1)
                                act.wait_ge(out_ready, past((it - 1) * ys))
                                act.sem_inc(pace_act, 1)
                                func(act, hid[b % 2][n][:, c, :].rearrange("p (z n) -> p z n", z=2),
                                     p_hid[:, qs, :, 0:half], e, c).then_inc(hid_copied, 1)
                unit_loop(act, body)

            @block.vector
            def _(dve):
                def body(i):
                    for b in range(per_body):
                        it = i * per_body + b
                        for o in range(outs):
                            e = (2 * i + b // blocks) * outs + o
                            for j in range(NB):
                                y = it * ys + o * NB + j
                                node = (b % blocks) * NB + j
                                dve.wait_ge(out_ready, y + 1)
                                dve.wait_ge(out_added, freed(y, NB))
                                dve.sem_inc(pace_dve, 1)
                                dve.scalar_tensor_tensor(out[:, node, :], p_out[:, (b * ys + o * NB + j) % 2, 0:D],
                                                         gate[:, node, bass.ds(e, 1)], out[:, node, :],
                                                         ALU.mult, ALU.add).then_inc(out_added, 1)
                unit_loop(dve, body)


def per_node(ap, width):
    return ap.unsqueeze(2).to_broadcast([P, NT, width])


def one_hot_of_max(dve, k, logits, pick, peak, spot, scratch):
    e = logits.shape[2]
    num = wide(k.col[:, 0:e])
    dve.tensor_reduce(peak, logits, AX.X, ALU.max)
    dve.drain()
    dve.tensor_tensor(scratch, logits, per_node(peak, e), ALU.is_equal)
    dve.drain()
    dve.tensor_scalar(scratch, scratch, -float(P), float(P), ALU.mult, ALU.add)
    dve.drain()
    dve.tensor_tensor(scratch, scratch, num, ALU.add)
    dve.drain()
    dve.tensor_reduce(spot, scratch, AX.X, ALU.min)
    dve.drain()
    dve.tensor_tensor(pick, num, per_node(spot, e), ALU.is_equal)
    dve.drain()


def top2_gate(k, logits, gate):
    e = logits.shape[2]
    with ExitStack() as ctx:
        def sb(name, shape):
            return ctx.enter_context(k.nc.sbuf_tensor(f"{name}_{k.nc.next_id()}", shape, F32))
        m1, m2, spot, z, ez, w1, w2 = (sb(n, [P, NT])[:, :] for n in ("m1", "m2", "spot", "z", "ez", "w1", "w2"))
        pick1, pick2, rest, scratch = (sb(n, [P, NT, e])[:, :, :] for n in ("pick1", "pick2", "rest", "scratch"))

        def work(dve):
            one_hot_of_max(dve, k, logits, pick1, m1, spot, scratch)
            dve.scalar_tensor_tensor(rest, pick1, NEG, logits, ALU.mult, ALU.add)
            dve.drain()
            one_hot_of_max(dve, k, rest, pick2, m2, spot, scratch)
            dve.tensor_tensor(z, m2, m1, ALU.subtract)
        on_vector(k, work)

        def work(act):
            act.activation(ez, z, ACT.Exp)
        on_scalar(k, work)

        def work(dve):
            dve.tensor_scalar(w1, ez, 1.0, None, ALU.add)
            dve.drain()
            dve.reciprocal(z, w1)
            dve.drain()
            dve.tensor_tensor(w2, ez, z, ALU.mult)
            dve.drain()
            dve.tensor_tensor(pick1, pick1, per_node(z, e), ALU.mult)
            dve.drain()
            dve.tensor_tensor(pick2, pick2, per_node(w2, e), ALU.mult)
            dve.drain()
            dve.tensor_tensor(gate, pick1, pick2, ALU.add)
        on_vector(k, work)


def gelu_experts(k, xT, gate, out, name, count):
    ins, nc = k.ins, k.nc
    w1, b1, w2 = ins[f"{name}_W1"], ins[f"{name}_b1"], ins[f"{name}_W2"]
    hc = w1.shape[2] // P
    with nc.sbuf_tensor(f"b1_{name}", [P, count, hc], F32) as bias:
        with nc.allow_non_contiguous_dma(reason="4096 biases, once"):
            load(k, *[(bias[:, :, c], b1[:, c * P:(c + 1) * P].rearrange("e p -> p e")) for c in range(hc)])
        experts(
            k, xT, gate, out, count,
            [(lambda w, e: [(w[:, :, :], w1[bass.ds(e, 1), :, :].rearrange("a (c p) h -> p (a c) h", p=P))], hc,
              lambda act, to, source, e, c: act.activation(
                  to, source, ACT.Gelu, bias=bias[:, bass.ds(e, 1), c]), KC)],
            (lambda e: w2[bass.ds(e, 1), :, :].rearrange("a (c p) d -> p (a c) d", p=P), hc))


def add_to_state(k, *parts):
    def add(dve):
        for part in parts:
            dve.tensor_tensor(k.x[:, :, :], k.x[:, :, :], part, ALU.add)
            dve.drain()
    on_vector(k, add)


def layer0_ffn(k):
    ins, E = k.ins, 8
    with ExitStack() as ctx:
        def sb(name, shape, dt=F32):
            return ctx.enter_context(k.nc.sbuf_tensor(f"{name}_f0", shape, dt))
        y = sb("y", [P, NT, D])
        xT = sb("xT", [P, KC, NP])
        logits = sb("logits", [P, NT, E])
        gate = sb("gate", [P, NT, E])
        wr = sb("wr", [P, KC, E])
        br = sb("br", [1, E])
        b2 = sb("b2", [E, 1, D])
        layer_norm(k, k.x[:, :, :], y[:, :, :])
        layer_norm(k, y[:, :, :], y[:, :, :], ins["L0_ffn_gamma"], ins["L0_ffn_beta"])
        load(k, (wr[:, :, :], ins["L0_ffn_Wr"].rearrange("(c p) e -> p c e", p=P)),
             (br[:, :], ins["L0_ffn_br"].rearrange("(a e) -> a e", a=1)), (b2[:, 0, :], ins["L0_ffn_b2"]))
        project(k, y[:, :, :], wr, logits[:, :, :], bias=br[:, :], keep=xT)
        top2_gate(k, logits[:, :, :], gate[:, :, :])
        project(k, gate[:, :, :], b2, y[:, :, :])
        gelu_experts(k, xT, gate, y, "L0_ffn", E)
        add_to_state(k, y[:, :, :])


def layer1_gnn(k):
    ins, t, R = k.ins, k.t, 64
    with ExitStack() as ctx:
        def sb(name, shape, dt=F32):
            return ctx.enter_context(k.nc.sbuf_tensor(f"{name}_g1", shape, dt))
        xn = sb("xn", [P, NT, D])
        res = sb("res", [P, NT, D])
        wT = sb("wT", [P, 4, KC, D])
        bias = sb("bias", [1, 4, D])
        filters = sb("filters", [R + 1, 1, 2 * D])
        layer_norm(k, k.x[:, :, :], xn[:, :, :])
        layer_norm(k, xn[:, :, :], xn[:, :, :], ins["L1_gnn_ln_g"], ins["L1_gnn_ln_b"])
        for n, name in enumerate("qkvo"):
            load_transposed(k, (wT[:, n], ins[f"L1_gnn_W{name}"]))
        load_transposed(k, (filters[0:R, :, 0:D], ins["L1_gnn_Wdk"]), (filters[0:R, :, D:2 * D], ins["L1_gnn_Wdv"]))
        load(k, *[(bias[:, n, :], ins[f"L1_gnn_b{name}"].rearrange("(a d) -> a d", a=1)) for n, name in enumerate("qkvo")],
             (filters[R:R + 1, 0, 0:D], ins["L1_gnn_bdk"].rearrange("(a d) -> a d", a=1)),
             (filters[R:R + 1, 0, D:2 * D], ins["L1_gnn_bdv"].rearrange("(a d) -> a d", a=1)))
        for n, to in enumerate((nodes(t["query1"]), nodes(t["keyval1"])[:, :, 0:D], nodes(t["keyval1"])[:, :, D:2 * D])):
            project(k, xn[:, :, :], wT[:, n], res[:, :, :], bias=bias[:, n, :])
            store(k, (to, res[:, :, :]))
        filtered_messages(k, t["query1"], t["keyval1"], t["radial1"].rearrange("(p t) c -> p t c", p=P),
                          filters[:, 0, :], t["sum1"])
        with k.nc.sbuf_tensor("agg_g1", [P, NT, D + 1], F32) as agg:
            gather_sums(k, t["sum1"], agg[:, :, :])

            def work(dve):
                dve.tensor_scalar(k.dinv[:, :], agg[:, :, D], 1.0, 1e-12, ALU.add, ALU.max)
            on_vector(k, work)

            def work(act):
                act.activation(k.dinv[:, :], k.dinv[:, :], ACT.Sqrt)
            on_scalar(k, work)

            def work(dve):
                dve.reciprocal(k.dinv[:, :], k.dinv[:, :])
            on_vector(k, work)
            project(k, agg[:, :, 0:D], wT[:, 3], res[:, :, :], bias=bias[:, 3, :])
        layer_norm(k, k.x[:, :, :], xn[:, :, :])
        add_to_state(k, xn[:, :, :], res[:, :, :])


def layer1_ffn(k):
    ins, t, E, H1 = k.ins, k.t, 4, 4
    W = H1 * E
    with ExitStack() as ctx:
        def sb(name, shape, dt=F32):
            return ctx.enter_context(k.nc.sbuf_tensor(f"{name}_f1", shape, dt))
        y = sb("y", [P, NT, D])
        xT = sb("xT", [P, KC, NP])
        gate = sb("gate", [P, NT, E])
        b2 = sb("b2", [E, 1, D])
        layer_norm(k, k.x[:, :, :], y[:, :, :])
        with ExitStack() as inner:
            def tb(name, shape, dt=F32):
                return inner.enter_context(k.nc.sbuf_tensor(f"{name}_f1", shape, dt))
            rows = tb("rows", [P, NT, W + H1])
            sums = tb("sums", [P, NT, W + H1])
            wg = tb("wg", [P, KC, W])
            vec = tb("vec", [P, 5, W])
            src = tb("src", [P, NT, H1])
            dst = tb("dst", [P, NT, H1])
            own = tb("own", [P, NT, H1])
            peak = tb("peak", [P, NT, H1])
            scratch = tb("scratch", [P, NT, W])
            mean = tb("mean", [P, NT])
            var = tb("var", [P, NT])
            alpha = tb("alpha", [P, T2, H1])
            each = tb("each", [P, MCHAINS, NT, H1])
            flat = [ins[f"L1_ffn_{n}"].rearrange("h e -> (h e)") for n in ("att_src", "att_dst")] + [
                ins[f"L1_ffn_{n}"] for n in ("b_gat", "ln_gamma", "ln_beta")]
            load(k, (wg[:, :, :], ins["L1_ffn_W_gat"].rearrange("(c p) e -> p c e", p=P)),
                 (b2[:, 0, :], ins["L1_ffn_b2"]),
                 *[(vec[:, n, :], v.partition_broadcast(P)) for n, v in enumerate(flat)])
            project(k, y[:, :, :], wg, rows[:, :, 0:W], keep=xT)
            head_scores(k, rows[:, :, 0:W], vec[:, 0, :], src[:, :, :], scratch)
            head_scores(k, rows[:, :, 0:W], vec[:, 1, :], dst[:, :, :], scratch)

            def work(dve):
                dve.memset(rows[:, :, W:W + H1], 0.0)
                dve.drain()
                dve.tensor_tensor(own[:, :, :], src[:, :, :], dst[:, :, :], ALU.add)
                dve.drain()
                dve.scalar_tensor_tensor(own[:, :, :], own[:, :, :], 0.2, own[:, :, :], ALU.mult, ALU.max)
            on_vector(k, work)
            store(k, (nodes(t["rows1"]), rows[:, :, :]), (nodes(t["src1"]), src[:, :, :]),
                  (nodes(t["dst1"]), dst[:, :, :]))
            attention_maxima(k, k.meta2, T2, H1, t["src1"], t["dst1"], t["max1"], alpha)
            gather_maxima(k, t["max1"], peak[:, :, :], each)

            def work(dve):
                dve.tensor_tensor(peak[:, :, :], peak[:, :, :], own[:, :, :], ALU.max)
                dve.drain()
                dve.tensor_tensor(own[:, :, :], own[:, :, :], peak[:, :, :], ALU.subtract)
            on_vector(k, work)

            def work(act):
                act.activation(own[:, :, :], own[:, :, :], ACT.Exp)
            on_scalar(k, work)
            store(k, (nodes(t["peak1"]), peak[:, :, :]))
            attention_sums(k, k.meta2, T2, H1, E, t["rows1"], t["peak1"], alpha, t["sumr"])
            gather_sums(k, t["sumr"], sums[:, :, :])

            def heads(ap):
                return ap.rearrange("p j (h e) -> p j h e", h=H1)

            def spread(dve, out, a, b):
                for h in range(H1):
                    dve.tensor_tensor(heads(out)[:, :, h, :], heads(a)[:, :, h, :],
                                      b[:, :, h:h + 1].to_broadcast([P, NT, E]), ALU.mult)
            num, den, z = sums[:, :, 0:W], sums[:, :, W:W + H1], scratch[:, :, :]

            def work(dve):
                spread(dve, z, rows[:, :, 0:W], own[:, :, :])
                dve.drain()
                dve.tensor_tensor(num, num, z, ALU.add)
                dve.drain()
                dve.tensor_tensor(den, den, own[:, :, :], ALU.add)
                dve.drain()
                dve.tensor_scalar(den, den, 1e-16, None, ALU.add)
                dve.drain()
                dve.reciprocal(peak[:, :, :], den)
                dve.drain()
                spread(dve, z, num, peak[:, :, :])
                dve.drain()
                dve.tensor_tensor(z, z, wide(vec[:, 2, :]), ALU.add)
                dve.drain()
                dve.tensor_reduce(mean[:, :], z, AX.X, ALU.add)
                dve.drain()
                dve.tensor_scalar(mean[:, :], mean[:, :], 1.0 / W, None, ALU.mult)
                dve.drain()
                dve.tensor_tensor(z, z, per_node(mean[:, :], W), ALU.subtract)
                dve.drain()
                dve.tensor_tensor(num, z, z, ALU.mult)
                dve.drain()
                dve.tensor_reduce(var[:, :], num, AX.X, ALU.add)
                dve.drain()
                dve.tensor_scalar(var[:, :], var[:, :], 1.0 / W, EPS, ALU.mult, ALU.add)
            on_vector(k, work)

            def work(act):
                act.activation(mean[:, :], var[:, :], ACT.Sqrt)
            on_scalar(k, work)

            def work(dve):
                dve.reciprocal(var[:, :], mean[:, :])
                dve.drain()
                dve.tensor_tensor(z, z, per_node(var[:, :], W), ALU.mult)
                dve.drain()
                dve.tensor_tensor(z, z, wide(vec[:, 3, :]), ALU.mult)
                dve.drain()
                dve.tensor_tensor(z, z, wide(vec[:, 4, :]), ALU.add)
                dve.drain()
                dve.tensor_reduce(own[:, :, :], heads(z).rearrange('p j h e -> p j e h'), AX.X, ALU.add)
                dve.drain()
                dve.tensor_scalar(own[:, :, :], own[:, :, :], 1.0 / H1, None, ALU.mult)
            on_vector(k, work)
            top2_gate(k, own[:, :, :], gate[:, :, :])
        project(k, gate[:, :, :], b2, y[:, :, :])
        gelu_experts(k, xT, gate, y, "L1_ffn", E)
        add_to_state(k, y[:, :, :])


def layer2_gnn(k):
    ins, t = k.ins, k.t
    with ExitStack() as ctx:
        def sb(name, shape, dt=F32):
            return ctx.enter_context(k.nc.sbuf_tensor(f"{name}_g2", shape, dt))
        xn = sb("xn", [P, NT, D])
        a = sb("a", [P, NT, 2 * 64])
        b = sb("b", [P, NT, 2 * 64])
        w1 = sb("w1", [P, 2, 128])
        w2 = sb("w2", [P, 1, 64])
        w3 = sb("w3", [64, 1, 128])
        w4 = sb("w4", [P, 1, 256])
        b12 = sb("b12", [P, 2, 128])
        b34 = sb("b34", [1, 2, 256])
        layer_norm(k, k.x[:, :, :], xn[:, :, :])
        load(k, (w1[:, :, :], ins["L2_gnn_W1"].rearrange("(c p) n -> p c n", p=P)), (w2[:, 0, :], ins["L2_gnn_W2"]),
             (w3[:, 0, :], ins["L2_gnn_W3"]), (w4[:, 0, :], ins["L2_gnn_W4"]),
             (b12[:, 0, :], ins["L2_gnn_b1"].partition_broadcast(P)),
             (b12[:, 1, 0:64], ins["L2_gnn_b2"].partition_broadcast(P)),
             (b34[:, 0, 0:128], ins["L2_gnn_b3"].rearrange("(a d) -> a d", a=1)),
             (b34[:, 1, :], ins["L2_gnn_b4"].rearrange("(a d) -> a d", a=1)))

        def convolve(n, w, relu_bias):
            x, s = a[:, :, 0:w], b[:, :, 0:w]

            def scale(dve):
                dve.tensor_tensor(x, x, per_node(k.dinv[:, :], w), ALU.mult)
                dve.drain()

            def finish(dve):
                dve.tensor_tensor(x, x, s, ALU.add)
                dve.drain()
                scale(dve)
                if relu_bias is not None:
                    dve.tensor_tensor(x, x, wide(relu_bias), ALU.add)
                    dve.drain()
                    dve.tensor_scalar(x, x, 0.0, None, ALU.max)
            on_vector(k, scale)
            store(k, (nodes(t[f"conv{n}"]), x))
            aggregate(k, k.meta1, T1, t[f"conv{n}"], t[f"csum{n}"], SRC_G, DST_S, DST_F)
            gather_sums(k, t[f"csum{n}"], s)
            on_vector(k, finish)
        project(k, xn[:, :, :], w1, a[:, :, :])
        convolve(0, 128, b12[:, 0, :])
        project(k, a[:, :, :], w2, b[:, :, 0:64])

        def work(dve):
            dve.tensor_copy(a[:, :, 0:64], b[:, :, 0:64])
        on_vector(k, work)
        convolve(1, 64, b12[:, 1, 0:64])
        convolve(2, 64, None)
        project(k, a[:, :, 0:64], w3, b[:, :, :], bias=b34[:, 0, 0:128])

        def work(dve):
            dve.tensor_scalar(a[:, :, :], b[:, :, :], 0.0, None, ALU.max)
        on_vector(k, work)
        convolve(3, 128, None)
        project(k, a[:, :, :], w4, xn[:, :, :], bias=b34[:, 1, :])
        add_to_state(k, xn[:, :, :])


def layer2_ffn(k):
    ins, E = k.ins, 8
    with ExitStack() as ctx:
        def sb(name, shape, dt=F32):
            return ctx.enter_context(k.nc.sbuf_tensor(f"{name}_f2", shape, dt))
        y = sb("y", [P, NT, D])
        xT = sb("xT", [P, KC, NP])
        logits = sb("logits", [P, NT, E])
        gate = sb("gate", [P, NT, E])
        wr = sb("wr", [P, KC, E])
        br = sb("br", [1, E])
        bo = sb("bo", [E, 1, D])
        m = sb("m", [P, NT])
        names = [f"{n}{l}" for l in (1, 2) for n in ("b", "g", "be", "m", "v")]
        v = {n: sb(n, [P, KC, E]) for n in names}
        layer_norm(k, k.x[:, :, :], y[:, :, :])
        with k.nc.allow_non_contiguous_dma(reason="per-feature vectors of the experts, once"):
            load(k, (wr[:, :, :], ins["L2_ffn_Wr"].rearrange("(c p) e -> p c e", p=P)),
                 (br[:, :], ins["L2_ffn_br"].rearrange("(a e) -> a e", a=1)), (bo[:, 0, :], ins["L2_ffn_bo"]),
                 *[(v[n][:, c, :], ins[f"L2_ffn_{n}"][:, c * P:(c + 1) * P].rearrange("e p -> p e"))
                   for n in names for c in range(KC)])
        project(k, y[:, :, :], wr, logits[:, :, :], bias=br[:, :], keep=xT)
        lg, gt = logits[:, :, :], gate[:, :, :]
        g, be, vv = ([v[f"{n}{l}"][:, :, :] for l in (1, 2)] for n in ("g", "be", "v"))

        def shift_logits(dve):
            dve.tensor_reduce(m[:, :], lg, AX.X, ALU.max)
            for l in range(2):
                dve.tensor_scalar(vv[l], vv[l], 0.001, None, ALU.add)
            dve.drain()
            dve.tensor_tensor(lg, lg, per_node(m[:, :], E), ALU.subtract)

        def exps_and_deviations(act):
            act.activation(gt, lg, ACT.Exp)
            for l in range(2):
                act.activation(vv[l], vv[l], ACT.Sqrt)

        def gates_and_norms(dve):
            dve.tensor_reduce(m[:, :], gt, AX.X, ALU.add)
            dve.drain()
            dve.reciprocal(m[:, :], m[:, :])
            dve.drain()
            dve.tensor_tensor(gt, gt, per_node(m[:, :], E), ALU.mult)
            for l, n in enumerate("12"):
                bias = v["b" + n][:, :, :]
                dve.reciprocal(vv[l], vv[l])
                dve.tensor_tensor(bias, bias, v["m" + n][:, :, :], ALU.subtract)
                dve.drain()
                dve.tensor_tensor(g[l], g[l], vv[l], ALU.mult)
                dve.drain()
                dve.tensor_tensor(bias, bias, g[l], ALU.mult)
                dve.drain()
                dve.tensor_tensor(be[l], be[l], bias, ALU.add)
        on_vector(k, shift_logits)
        on_scalar(k, exps_and_deviations)
        on_vector(k, gates_and_norms)
        project(k, gate[:, :, :], bo, y[:, :, :])

        def weights(name):
            return lambda w, e: [(w[:, :, :], ins[name][bass.ds(e, 1), :, :].rearrange("a (c p) h -> p (a c) h", p=P))]

        def relu(l):
            return lambda act, to, source, e, c: act.activation(
                to, source, ACT.Relu, bias=v[f"be{l}"][:, c, bass.ds(e, 1)], scale=v[f"g{l}"][:, c, bass.ds(e, 1)])
        experts(k, xT, gate, y, E, [(weights("L2_ffn_W1"), KC, relu(1), KC), (weights("L2_ffn_W2"), KC, relu(2), KC)],
                (lambda e: ins["L2_ffn_Wo"][bass.ds(e, 1), :, :].rearrange("a (c p) d -> p (a c) d", p=P), KC))
        add_to_state(k, y[:, :, :])


def layer3_gnn(k):
    ins, t = k.ins, k.t
    with ExitStack() as ctx:
        def sb(name, shape, dt=F32):
            return ctx.enter_context(k.nc.sbuf_tensor(f"{name}_g3", shape, dt))
        xn = sb("xn", [P, NT, D])
        agg = sb("agg", [P, NT, D])
        res = sb("res", [P, NT, D])
        wT = sb("wT", [P, 2 * KC, D])
        layer_norm(k, k.x[:, :, :], xn[:, :, :])
        load_transposed(k, (wT, ins["L3_gnn_W"]))
        store(k, (nodes(t["state3"]), xn[:, :, :]))
        aggregate(k, k.meta1, T1, t["state3"], t["sum3"], DST_G, SRC_S, SRC_F, weighted=True)
        gather_sums(k, t["sum3"], agg[:, :, :])
        project(k, agg[:, :, :], wT[:, 0:KC, :], res[:, :, :])
        project(k, xn[:, :, :], wT[:, KC:2 * KC, :], agg[:, :, :])

        def work(dve):
            dve.tensor_tensor(res[:, :, :], res[:, :, :], agg[:, :, :], ALU.add)
        on_vector(k, work)
        layer_norm(k, res[:, :, :], res[:, :, :], ins["L3_gnn_gamma"], ins["L3_gnn_beta"])

        def work(dve):
            dve.scalar_tensor_tensor(k.x[:, :, :], res[:, :, :], 0.0, k.x[:, :, :], ALU.max, ALU.add)
        on_vector(k, work)


def layer3_ffn(k):
    ins, E, H = k.ins, 32, 64
    with ExitStack() as ctx:
        def sb(name, shape, dt=F32):
            return ctx.enter_context(k.nc.sbuf_tensor(f"{name}_f3", shape, dt))
        y = sb("y", [P, NT, D])
        xT = sb("xT", [P, KC, NP])
        logits = sb("logits", [P, NT, E])
        scratch = sb("scratch", [P, NT, E])
        gate = sb("gate", [P, NT, E])
        wr = sb("wr", [P, KC, E])
        br = sb("br", [1, E])
        b1 = sb("b1", [P, E // 2])
        b2 = sb("b2", [E, 1, D])
        m = sb("m", [P, NT])
        spot = sb("spot", [P, NT])
        layer_norm(k, k.x[:, :, :], y[:, :, :])
        load_transposed(k, (wr, ins["L3_ffn_router_w"]))
        with k.nc.allow_non_contiguous_dma(reason="2048 biases, once"):
            load(k, (br[:, :], ins["L3_ffn_router_b"].rearrange("(a e) -> a e", a=1)), (b2[:, 0, :], ins["L3_ffn_b2"]),
                 (b1[:, :], ins["L3_ffn_b1"].rearrange("(u o) h -> (o h) u", o=2)))
        project(k, y[:, :, :], wr, logits[:, :, :], bias=br[:, :], keep=xT)

        def work(dve):
            one_hot_of_max(dve, k, logits[:, :, :], gate[:, :, :], m[:, :], spot[:, :], scratch[:, :, :])
        on_vector(k, work)
        project(k, gate[:, :, :], b2, y[:, :, :])
        w1, w2 = ins["L3_ffn_W1"], ins["L3_ffn_W2"]

        def pair(w, e):
            return [(w[:, :, o * H:(o + 1) * H], w1[bass.ds(e + o, 1), :, :].rearrange("a (c p) h -> p (a c) h", p=P))
                    for o in range(2)]
        experts(k, xT, gate, y, E,
                [(pair, 1, lambda act, to, source, e, c: act.activation(
                    to, source, ACT.Relu, bias=b1[:, bass.ds(e, 1)]), KC)],
                (lambda e: w2[bass.ds(e, 2), :, :].rearrange("a h d -> (a h) d").unsqueeze(1), 1), outs=2)

        def work(dve):
            dve.scalar_tensor_tensor(k.x[:, :, :], y[:, :, :], 0.0, k.x[:, :, :], ALU.max, ALU.add)
        on_vector(k, work)


def copy_features(k, target, source):
    nc = k.nc
    w = source.shape[1]
    rest = T1 * P - EDGES
    with k.phase() as (sem, sb, ps):
        zeros = sb("zeros", [1, rest * w])
        zeroed, copied = sem("zeroed"), sem("copied")
        with nc.Block() as block:
            @block.vector
            def _(dve):
                dve.memset(zeros[:, :], 0.0).then_inc(zeroed, 1)

            @block.sync
            def _(sp):
                whole = EDGES // 16 * 16
                sp.dma_start(target[0:whole, :].rearrange("(a b) c -> a (b c)", a=16),
                             source[0:whole, :].rearrange("(a b) c -> a (b c)", a=16)).then_inc(copied, 16)
                sp.dma_start(target[whole:EDGES, :], source[whole:EDGES, :]).then_inc(copied, 16)
                sp.wait_ge(zeroed, 1)
                sp.dma_start(target[EDGES:T1 * P, :].rearrange("(a b) c -> a (b c)", a=1), zeros[:, :])\
                    .then_inc(copied, 16)
                sp.wait_ge(copied, 48)


def kernel_program(nc, ins, out, stages):
    k = Kernel(nc, ins, out)
    with ExitStack() as ctx:
        def sb(name, shape, dt=F32):
            return ctx.enter_context(nc.sbuf_tensor(name, shape, dt))
        k.x = sb("x_state", [P, NT, D])
        k.ident = sb("ident", [P, P])
        k.ones = sb("ones", [P, P])
        k.col = sb("col", [P, P])
        k.row = sb("row", [P, 1])
        k.lower = sb("lower", [P, P])
        k.dinv = sb("dinv", [P, NT])
        k.meta1 = k.dram("edges1", (T1 * P, EC), I32)
        k.meta2 = k.dram("edges2", (T2 * P, EC), I32)
        t = k.t = {}
        fills = []

        def chains(name, count, w, value):
            parts = t[name] = [k.dram(f"{name}_{c}", (NTAB, w)) for c in range(count)]
            fills.extend((part, value) for part in parts)
        for name, w in (("rows0", D + 8), ("scores0", 8), ("peak0", 8), ("query1", D), ("keyval1", 2 * D),
                        ("rows1", 20), ("src1", 4), ("dst1", 4), ("peak1", 4), ("conv0", 128), ("conv1", 64),
                        ("conv2", 64), ("conv3", 128), ("state3", D)):
            t[name] = k.dram(name, (NP, w))
        t["radial1"] = k.dram("radial1", (T1 * P, 64))
        chains("sum0", CHAINS, D + 8, 0.0)
        chains("max0", MCHAINS, 8, NEG)
        chains("sum1", CHAINS, D + 1, 0.0)
        chains("max1", MCHAINS, 4, NEG)
        chains("sumr", CHAINS, 20, 0.0)
        for n, w in enumerate((128, 64, 64, 128)):
            chains(f"csum{n}", CHAINS, w, 0.0)
        chains("sum3", CHAINS, D, 0.0)
        build_constants(k)
        fill_tables(k, fills)
        copy_features(k, t["radial1"], ins["edge_attr_64"])
        build_edges(k, k.meta1, T1, EDGES, ins["src"], ins["dst"], ins["edge_weight"], ins["edge_attr_3"])
        build_edges(k, k.meta2, T2, ROUTES, ins["L1_ffn_edge_index"][0], ins["L1_ffn_edge_index"][1])
        for layer in (layer0_gnn, layer0_ffn, layer1_gnn, layer1_ffn, layer2_gnn, layer2_ffn, layer3_gnn,
                      layer3_ffn)[:stages]:
            layer(k)
        store_state(k)


def store_state(k):
    nc = k.nc
    last = N - (NT - 1) * P
    with k.phase() as (sem, sb, ps):
        stored = sem("stored")
        with nc.Block() as block:
            @block.sync
            def _(sp):
                sp.dma_start(k.out[0:(NT - 1) * P, :].rearrange("(j p) w -> p j w", p=P), k.x[:, 0:NT - 1, :])\
                    .then_inc(stored, 16)
                sp.dma_start(k.out[(NT - 1) * P:N, :], k.x[0:last, NT - 1, :]).then_inc(stored, 16)
                sp.wait_ge(stored, 32)


def kernel(**inputs):
    import numpy as _np
    import concourse.bacc as _bacc
    from concourse import mybir as _mybir
    from concourse.bass_utils import run_bass_kernel_spmd as _run

    nc = _bacc.Bacc("TRN2", target_bir_lowering=False, num_devices=1)
    arrays, ins = {}, {}
    for name, value in inputs.items():
        a = _np.ascontiguousarray(value)
        arrays[f"in_{name}_dram"] = a
        ins[name] = nc.dram_tensor(f"in_{name}_dram", a.shape, _mybir.dt.from_np(a.dtype), kind="ExternalInput").ap()
    out = nc.dram_tensor("out_0_dram", (N, D), _mybir.dt.float32, kind="ExternalOutput").ap()
    kernel_program(nc, ins, out, 8)
    r = _run(nc, [arrays], core_ids=[0])
    return r.results[0]["out_0_dram"]
```

```python
from contextlib import ExitStack, contextmanager

import numpy as np

import concourse.bass as bass
from concourse import mybir
from concourse.alu_op_type import AluOpType as ALU

ACT = mybir.ActivationFunctionType
AX = mybir.AxisListType
F32 = mybir.dt.float32
I32 = mybir.dt.int32

P = 128
N = 3125
NT = -(-N // P)
NP = NT * P
NB = 5
NTAB = NP + P
D = 256
KC = D // P
EDGES = 53125
T1 = -(-EDGES // P)
ROUTES = 32768
T2 = ROUTES // P
NEG = -1.0e30
EPS = 1e-5

U = 8
LAG = 4
CR = 4
PAIRS_SPLIT = 288
CHAINS = 4
MCHAINS = 8

SRC_G, DST_G, DST_S, DST_F, CUT, ATTR = range(6)
EC = 9
CELL_SD, CELL_DS, COUNT, WSUM = range(4)
CELLS = NP * NP

def past(value):
    return max(value, 0) if isinstance(value, int) else value


def ready(t):
    return t + 1


def freed(t, ring):
    return past(t + 1 - ring)


def landed(i):
    return 16 * i + 16


def reused(i):
    return 16 * i


class Kernel:
    def __init__(self, nc, ins, out):
        self.nc, self.ins, self.out = nc, ins, out

    @contextmanager
    def phase(self):
        nc, sems = self.nc, []

        def sem(name):
            sems.append(nc.alloc_semaphore(f"{name}_{nc.next_id()}"))
            return sems[-1]
        with ExitStack() as ctx:
            def sb(name, shape, dt=F32):
                return ctx.enter_context(nc.sbuf_tensor(f"{name}_{nc.next_id()}", shape, dt))

            def ps(name, shape, dt=F32):
                return ctx.enter_context(nc.psum_tensor(f"{name}_{nc.next_id()}", shape, dt))
            yield sem, sb, ps
            nc.clear_and_free_semaphores(sems)
            nc.all_engine_barrier()

    def dram(self, name, shape, dt=F32):
        return self.nc.dram_tensor(name, shape, dt, kind="Internal").ap()


def tiles_loop(eng, tiles, body, *ahead, unroll=U):
    steps = tiles // unroll
    for before in range(max([lag for lag, _ in ahead], default=0), 0, -1):
        for lag, do in ahead:
            if lag >= before:
                do(0, lag - before)

    def step(i, last):
        for u in range(unroll):
            for lag, do in ahead:
                if not (last and u + lag >= unroll):
                    do(i + (u + lag) // unroll, (u + lag) % unroll)
            body(i, u)
    step(0, False)
    with eng.Fori(1, steps - 1) as i:
        step(i, False)
    step(steps - 1, True)


def nodes(table):
    return table[0:NP, :].rearrange("(j p) w -> p j w", p=P)


def build_constants(k):
    nc = k.nc
    with k.phase() as (sem, sb, ps):
        iota_i = sb("iota_i", [P, P], I32)
        row_i = sb("row_i", [P, 1], I32)
        made = sem("made")
        with nc.Block() as block:
            @block.gpsimd
            def _(pool):
                pool.iota(iota_i[:, :], [[1, P]], base=0, channel_multiplier=0).then_inc(made, 1)
                pool.iota(row_i[:, :], [[1, 1]], base=0, channel_multiplier=1).then_inc(made, 1)

            @block.vector
            def _(dve):
                dve.wait_ge(made, 2)
                dve.tensor_copy(k.col[:, :], iota_i[:, :])
                dve.tensor_copy(k.row[:, :], row_i[:, :])
                dve.memset(k.ones[:, :], 1.0)
                dve.memset(k.x[:, :, :], 0.0)
                dve.drain()
                dve.tensor_scalar(k.ident[:, :], k.col[:, :], k.row[:, 0:1], None, ALU.is_equal)
                dve.tensor_scalar(k.lower[:, :], k.col[:, :], k.row[:, 0:1], None, ALU.is_lt)


def fill_tables(k, zeros, lows):
    nc = k.nc
    features, source = k.t["radial1"], k.ins["edge_attr_64"]
    rest = T1 * P - EDGES
    even = EDGES // 16 * 16
    with k.phase() as (sem, sb, ps):
        low = sb("low", [P, NTAB // P * 8])
        filled, stored, loaded = sem("filled"), sem("stored"), sem("loaded")
        with nc.Block() as block:
            @block.vector
            def _(dve):
                dve.memset(k.zero[:, :], 0.0).then_inc(filled, 1)
                dve.memset(low[:, :], NEG).then_inc(filled, 1)

            @block.sync
            def _(sp):
                sp.dma_start(k.x[:, 0:NT - 1, :],
                             k.ins["x"][0:(NT - 1) * P, :].rearrange("(j p) w -> p j w", p=P)).then_inc(loaded, 16)
                sp.dma_start(k.x[0:N - (NT - 1) * P, NT - 1, :], k.ins["x"][(NT - 1) * P:N, :]).then_inc(loaded, 16)
                sp.wait_ge(filled, 2)
                for table in lows:
                    w = table.shape[1]
                    sp.dma_start(table.rearrange("(p r) w -> p (r w)", p=P), low[:, 0:NTAB // P * w])\
                        .then_inc(stored, 16)
                sp.wait_ge(stored, 16 * len(lows))
                sp.wait_ge(loaded, 32)

            @block.scalar
            def _(act):
                act.wait_ge(filled, 2)
                for table in zeros:
                    w = table.shape[1]
                    act.dma_start(table.rearrange("(p r) w -> p r w", p=P),
                                  k.zero[:, 0:w].unsqueeze(1).to_broadcast([P, NTAB // P, w])).then_inc(k.zeroed, 16)
                act.dma_start(features[0:even, :].rearrange("(a b) c -> a (b c)", a=16),
                              source[0:even, :].rearrange("(a b) c -> a (b c)", a=16)).then_inc(k.copied, 16)
                act.dma_start(features[even:EDGES, :], source[even:EDGES, :]).then_inc(k.copied, 16)
                act.dma_start(features[EDGES:T1 * P, :], k.zero[0:rest, 0:features.shape[1]]).then_inc(k.copied, 16)
                for matrix in k.matrices:
                    act.dma_start(matrix[0:CELLS, :].rearrange("(p a c) o -> p a (c o)", p=P, c=NP),
                                  k.zero[:, :].unsqueeze(1).to_broadcast([P, NP // P, NP])).then_inc(k.matrix_zeroed, 16)
                    act.dma_start(matrix[CELLS:CELLS + P, :], k.zero[:, 0:1]).then_inc(k.matrix_zeroed, 16)
        k.zeroed_all, k.copied_all = 16 * len(zeros), 48
        k.matrix_zeroed_all = 32 * len(k.matrices)


def build_edges(k, meta, tiles, edges, src, dst, weight=None, attr=None):
    nc = k.nc
    full = edges // tiles
    rest = edges - full * tiles
    assert not rest or full == P - 1
    pairs = weight is not None
    lists = 2 if pairs else 1
    R = 4
    with k.phase() as (sem, sb, ps):
        em = sb("em", [P, tiles, EC], I32)
        ids = sb("ids", [P, 2, tiles], I32)
        wt = sb("wt", [P, tiles])
        at = sb("at", [P, tiles, 3])
        pad = sb("pad", [P, tiles])
        num = sb("num", [P, 4, tiles])
        dup = sb("dup", [P, 2, tiles])
        tmp = sb("tmp", [P, 2, tiles])
        cell = sb("cell", [P, R, 4])
        junk = sb("junk", [P, R, 2, P])
        equal = sb("equal", [P, R, P])
        p_row = ps("p_row", [P, R, 512])
        p_pair = ps("p_pair", [P, R, 512])
        cleared, loaded, numbered, stored = sem("cleared"), sem("loaded"), sem("numbered"), sem("stored")
        cell_ready, row_ready, dup_ready = sem("cell_ready"), sem("row_ready"), sem("dup_ready")
        pair_ready, pair_copied = sem("pair_ready"), sem("pair_copied")
        angle_ready, cos_ready, packed = sem("angle_ready"), sem("cos_ready"), sem("packed")
        places = sem("places")
        step_act, step_pe, step_dve = sem("step_act"), sem("step_pe"), sem("step_dve")
        emf = em[:, :, :].bitcast(F32)
        loads = [(ids[:, 0, :], src), (ids[:, 1, :], dst)] + ([(wt[:, :], weight)] if pairs else [])
        n_loads = 16 * (len(loads) + (attr is not None)) * (2 if rest else 1)
        with nc.Block() as block:
            @block.sync
            def _(sp):
                sp.wait_ge(cleared, 1)
                for to, array in loads:
                    sp.dma_start(to[0:full, :], array[0:full * tiles].rearrange("(p t) -> p t", t=tiles))\
                        .then_inc(loaded, 16)
                    if rest:
                        sp.dma_start(to[full:full + 1, 0:rest],
                                     array[full * tiles:edges].rearrange("(p t) -> p t", p=1)).then_inc(loaded, 16)
                if attr is not None:
                    sp.dma_start(at[0:full, :, :], attr[0:full * tiles, :].rearrange("(p t) c -> p t c", t=tiles))\
                        .then_inc(loaded, 16)
                    if rest:
                        sp.dma_start(at[full:full + 1, 0:rest, :],
                                     attr[full * tiles:edges, :].rearrange("(p t) c -> p t c", p=1))\
                            .then_inc(loaded, 16)
                sp.wait_ge(packed, 1)
                sp.dma_start(meta.rearrange("(p t) c -> p (t c)", p=P), em[:, :, :].rearrange("p t c -> p (t c)"))\
                    .then_inc(stored, 16)
                sp.wait_ge(stored, 16)

            @block.gpsimd
            def _(pool):
                pool.iota(em[:, :, 0], [[1, tiles]], base=0, channel_multiplier=tiles).then_inc(places, 1)

            @block.vector
            def _(dve):
                dve.memset(ids[:, :, :], 0)
                dve.memset(wt[:, :], 0.0)
                dve.memset(at[:, :, :], 0.0)
                dve.memset(dup[:, :, :], 0.0)
                dve.memset(num[:, 2, :], 1.0)
                dve.drain()
                dve.memset(tmp[:, :, :], 0.0).then_inc(cleared, 1)
                dve.wait_ge(places, 1)
                dve.wait_ge(loaded, n_loads)
                dve.tensor_copy(tmp[:, 0, :], em[:, :, 0])
                dve.drain()
                dve.tensor_scalar(pad[:, :], tmp[:, 0, :], float(edges), float(NTAB - 1), ALU.is_ge, ALU.mult)
                dve.tensor_copy(num[:, 0, :], ids[:, 1, :])
                dve.tensor_copy(num[:, 1, :], ids[:, 0, :])
                dve.tensor_copy(num[:, 3, :], wt[:, :])
                dve.drain()
                for s in range(2):
                    dve.tensor_tensor(num[:, s, :], num[:, s, :], pad[:, :], ALU.add)
                dve.drain()
                if pairs:
                    dve.scalar_tensor_tensor(tmp[:, 1, :], num[:, 0, :], float(NP), num[:, 1, :], ALU.mult, ALU.add)
                    dve.scalar_tensor_tensor(num[:, 1, :], num[:, 1, :], float(NP), num[:, 0, :], ALU.mult, ALU.add)
                    dve.drain()
                    dve.tensor_copy(k.cells_f[:, :, CELL_DS], tmp[:, 1, :])
                    dve.drain()
                dve.scalar_tensor_tensor(tmp[:, 0, :], wt[:, :], -1.0, wt[:, :], ALU.mult, ALU.max)
                dve.drain()
                dve.tensor_scalar(tmp[:, 0, :], tmp[:, 0, :], 5.0, -float(np.pi / 5), ALU.min, ALU.mult)
                dve.drain()
                dve.tensor_scalar(tmp[:, 0, :], tmp[:, 0, :], float(np.pi / 2), None, ALU.add).then_inc(angle_ready, 1)
                dve.drain()
                dve.sem_inc(numbered, 1)

                def count(i, r):
                    t = bass.ds(i * R + r, 1)
                    dve.wait_ge(row_ready, ready(i * R + r))
                    if pairs:
                        dve.wait_ge(pair_ready, freed(i * R + r, R))
                    dve.sem_inc(step_dve, 1)
                    if pairs:
                        dve.tensor_scalar(equal[:, r, :], p_row[:, r, P:2 * P], num[:, 1, t], None, ALU.is_equal)
                    for s in range(lists):
                        done = dve.scalar_tensor_tensor(junk[:, r, s, :], p_row[:, r, s * P:(s + 1) * P],
                                                        num[:, s, t], k.lower[:, :], ALU.is_equal, ALU.mult,
                                                        accum_out=dup[:, s, t])
                    done.then_inc(dup_ready, 1)
                tiles_loop(dve, tiles, count, unroll=R)
                dve.wait_ge(cos_ready, 1)
                dve.drain()
                dve.tensor_scalar(tmp[:, 0, :], tmp[:, 1, :], 0.5, 0.5, ALU.mult, ALU.add)
                dve.drain()
                dve.tensor_scalar(tmp[:, 1, :], wt[:, :], 5.0, None, ALU.is_lt)
                dve.drain()
                dve.tensor_tensor(emf[:, :, CUT], tmp[:, 0, :], tmp[:, 1, :], ALU.mult)
                dve.tensor_copy(emf[:, :, ATTR:ATTR + 3], at[:, :, :])
                dve.memset(emf[:, :, ATTR + 3], 1.0)
                dve.tensor_copy(emf[:, :, DST_F], num[:, 0, :])
                dve.tensor_copy(em[:, :, SRC_G], ids[:, 0, :])
                dve.tensor_copy(em[:, :, DST_G], ids[:, 1, :])
                dve.tensor_tensor(dup[:, 1, :], dup[:, 1, :], pad[:, :], ALU.add)
                dve.drain()
                dve.tensor_scalar(dup[:, :, :], dup[:, :, :], 0.0, None, ALU.is_gt)
                dve.drain()

                def redirect(to, number, repeated, dump):
                    dve.tensor_scalar(tmp[:, 0, :], number, -1.0, float(dump), ALU.mult, ALU.add)
                    dve.drain()
                    dve.tensor_scalar(tmp[:, 0, :], tmp[:, 0, :], k.row[:, 0:1], None, ALU.add)
                    dve.drain()
                    dve.tensor_tensor(tmp[:, 0, :], tmp[:, 0, :], repeated, ALU.mult)
                    dve.drain()
                    dve.tensor_tensor(tmp[:, 0, :], tmp[:, 0, :], number, ALU.add)
                    dve.drain()
                    dve.tensor_copy(to, tmp[:, 0, :])
                    dve.drain()
                redirect(em[:, :, DST_S], num[:, 0, :], dup[:, 0, :], NP)
                dve.sem_inc(packed, 1)
                if pairs:
                    redirect(k.cells[:, :, CELL_SD], num[:, 1, :], dup[:, 1, :], CELLS)
                    redirect(k.cells[:, :, CELL_DS], k.cells_f[:, :, CELL_DS], dup[:, 1, :], CELLS)

            @block.scalar
            def _(act):
                act.wait_ge(angle_ready, 1)
                act.activation(tmp[:, 1, :], tmp[:, 0, :], ACT.Sin).then_inc(cos_ready, 1)
                act.wait_ge(numbered, 1)

                def pick(i, r):
                    act.wait_ge(row_ready, freed(i * R + r, R))
                    if pairs:
                        act.wait_ge(pair_ready, freed(i * R + r, R))
                    act.sem_inc(step_act, 1)
                    act.copy(cell[:, r, :], num[:, :, bass.ds(i * R + r, 1)].rearrange("p s t -> p (s t)"))\
                        .then_inc(cell_ready, 1)

                def keep_pair(i, r):
                    act.wait_ge(pair_ready, ready(i * R + r))
                    act.sem_inc(step_act, 1)
                    act.copy(k.cells_f[:, bass.ds(i * R + r, 1), COUNT:WSUM + 1].rearrange("p a c -> p (a c)"),
                             p_pair[:, r, 0:2]).then_inc(pair_copied, 1)
                if pairs:
                    tiles_loop(act, tiles, keep_pair, (3, pick), unroll=R)
                else:
                    tiles_loop(act, tiles, pick, unroll=R)

            @block.tensor
            def _(pe):
                def spread(i, r):
                    pe.wait_ge(cell_ready, ready(i * R + r))
                    pe.wait_ge(dup_ready, freed(i * R + r, R))
                    pe.sem_inc(step_pe, 1)
                    for s in range(lists):
                        done = pe.transpose(p_row[:, r, s * P:(s + 1) * P],
                                            cell[:, r, s:s + 1].to_broadcast([P, P]), k.ident[:, :])
                    done.then_inc(row_ready, 1)

                def add_pairs(i, r):
                    pe.wait_ge(dup_ready, ready(i * R + r))
                    pe.wait_ge(pair_copied, freed(i * R + r, R))
                    pe.sem_inc(step_pe, 1)
                    pe.matmul(p_pair[:, r, 0:2], equal[:, r, :], cell[:, r, 2:4], start=True, stop=True)\
                        .then_inc(pair_ready, 1)
                if pairs:
                    tiles_loop(pe, tiles, add_pairs, (2, spread), unroll=R)
                else:
                    tiles_loop(pe, tiles, spread, unroll=R)


def layer_norm(k, source, target, gamma=None, beta=None):
    nc = k.nc
    width = source.shape[2]
    with k.phase() as (sem, sb, ps):
        stats = sb("stats", [P, NT, 6])
        mean = sb("mean", [P, NT])
        diff = sb("diff", [P, NT])
        var = sb("var", [P, NT])
        dev = sb("dev", [P, NT])
        scale = sb("scale", [P, width])
        shift = sb("shift", [P, width])
        var_ready, dev_ready, loaded = sem("var_ready"), sem("dev_ready"), sem("loaded")
        with nc.Block() as block:
            @block.sync
            def _(sp):
                if gamma is not None:
                    sp.dma_start(scale[:, :], gamma.partition_broadcast(P)).then_inc(loaded, 16)
                    sp.dma_start(shift[:, :], beta.partition_broadcast(P)).then_inc(loaded, 16)
                    sp.wait_ge(loaded, 32)

            @block.vector
            def _(dve):
                with dve.Fori(0, NT // NB) as i:
                    for u in range(NB):
                        dve.bn_stats(stats[:, bass.ds(i * NB + u, 1), :].rearrange("p a b -> p (a b)"),
                                     source[:, bass.ds(i * NB + u, 1), :].rearrange("p a b -> p (a b)"))
                dve.drain()
                dve.tensor_tensor(mean[:, :], stats[:, :, 1], stats[:, :, 4], ALU.add)
                dve.tensor_tensor(diff[:, :], stats[:, :, 1], stats[:, :, 4], ALU.subtract)
                dve.tensor_tensor(var[:, :], stats[:, :, 2], stats[:, :, 5], ALU.add)
                dve.drain()
                dve.tensor_tensor(diff[:, :], diff[:, :], diff[:, :], ALU.mult)
                dve.tensor_scalar(mean[:, :], mean[:, :], 0.5, None, ALU.mult)
                dve.tensor_scalar(var[:, :], var[:, :], 1.0 / width, EPS, ALU.mult, ALU.add)
                dve.drain()
                dve.scalar_tensor_tensor(var[:, :], diff[:, :], 0.25, var[:, :], ALU.mult, ALU.add)\
                    .then_inc(var_ready, 1)
                dve.wait_ge(dev_ready, 1)
                dve.reciprocal(var[:, :], dev[:, :])
                dve.drain()
                with dve.Fori(0, NT // NB) as i:
                    for u in range(NB):
                        j = bass.ds(i * NB + u, 1)
                        dve.tensor_scalar(target[:, j, :].rearrange("p a b -> p (a b)"),
                                          source[:, j, :].rearrange("p a b -> p (a b)"),
                                          mean[:, j], var[:, j], ALU.subtract, ALU.mult)
                if gamma is not None:
                    dve.wait_ge(loaded, 32)
                    dve.drain()
                    dve.tensor_tensor(target, target, scale[:, :].unsqueeze(1).to_broadcast([P, NT, width]), ALU.mult)
                    dve.drain()
                    dve.tensor_tensor(target, target, shift[:, :].unsqueeze(1).to_broadcast([P, NT, width]), ALU.add)

            @block.scalar
            def _(act):
                act.wait_ge(var_ready, 1)
                act.activation(dev[:, :], var[:, :], ACT.Sqrt).then_inc(dev_ready, 1)


def load(k, *pairs):
    nc = k.nc
    with k.phase() as (sem, sb, ps):
        loaded = sem("loaded")
        with nc.Block() as block:
            @block.sync
            def _(sp):
                for to, source in pairs:
                    sp.dma_start(to, source).then_inc(loaded, 16)
                sp.wait_ge(loaded, 16 * len(pairs))


def load_transposed(k, *pairs):
    nc = k.nc
    with k.phase() as (sem, sb, ps):
        natural, moves = [], []
        for n, (target, w) in enumerate(pairs):
            outs, inner = w.shape
            op, ip = min(P, outs), min(P, inner)
            tile = sb(f"natural{n}", [op, outs // op, inner])
            natural.append((tile, w, op))
            for o in range(outs // op):
                for c in range(inner // ip):
                    moves.append((target[0:ip, c, o * op:(o + 1) * op],
                                  tile[:, o, c * ip:(c + 1) * ip], ip, op))
        turned = ps("turned", [P, 4, 512])
        loaded, turn_ready, moved = sem("loaded"), sem("turn_ready"), sem("moved")
        with nc.Block() as block:
            @block.sync
            def _(sp):
                for tile, w, op in natural:
                    sp.dma_start(tile[:, :, :], w.rearrange("(a o) i -> o a i", o=op)).then_inc(loaded, 16)
                sp.wait_ge(loaded, 16 * len(natural))

            @block.tensor
            def _(pe):
                pe.wait_ge(loaded, 16 * len(natural))
                for n, (_, source, ip, op) in enumerate(moves):
                    if n >= 4:
                        pe.wait_ge(moved, n - 3)
                    pe.transpose(turned[0:ip, n % 4, 0:op], source, k.ident[0:op, 0:op]).then_inc(turn_ready, 1)

            @block.vector
            def _(dve):
                for n, (target, _, ip, op) in enumerate(moves):
                    dve.wait_ge(turn_ready, n + 1)
                    dve.tensor_copy(target, turned[0:ip, n % 4, 0:op]).then_inc(moved, 1)


def project(k, source, weights, target, bias=None, keep=None, add=False):
    nc = k.nc
    width = source.shape[2]
    kp = min(P, width)
    chunks = width // kp
    cols = target.shape[2] if target is not None else 0
    with k.phase() as (sem, sb, ps):
        staged = sb("staged", [P, NB, width])
        turned = sb("turned", [kp, NB, chunks, P])
        bank = ps("bank", [P, NB, 512])
        p_turned, p_out = bank[:, :, 0:2 * P], bank[:, :, 2 * P:512]
        stage_ready, turn_ready, turn_copied, out_ready, out_copied, kept = (
            sem("stage_ready"), sem("turn_ready"), sem("turn_copied"), sem("out_ready"), sem("out_copied"), sem("kept"))
        pace_act, pace_pe, pace_dve, pace_pool = sem("pace_act"), sem("pace_pe"), sem("pace_dve"), sem("pace_pool")

        def flat(tensor, i, u):
            return tensor[:, bass.ds(i * NB + u, 1), :].rearrange("p a b -> p (a b)")

        with nc.Block() as block:
            @block.gpsimd
            def _(pool):

                def stage(i, u):
                    pool.wait_ge(turn_ready, freed(i * NB + u, NB))
                    pool.sem_inc(pace_pool, 1)
                    pool.tensor_copy(staged[:, u, :], flat(source, i, u)).then_inc(stage_ready, 1)
                tiles_loop(pool, NT, stage, unroll=NB)

            @block.tensor
            def _(pe):

                def turn(i, u):
                    t = i * NB + u
                    pe.wait_ge(stage_ready, ready(t))
                    pe.wait_ge(turn_copied, freed(t, NB))
                    if cols:
                        pe.wait_ge(out_copied, freed(t, NB))
                    pe.sem_inc(pace_pe, 1)
                    for c in range(chunks):
                        done = pe.transpose(p_turned[0:kp, u, c * P:(c + 1) * P],
                                            staged[:, u, c * kp:(c + 1) * kp], k.ident[:, :])
                    done.then_inc(turn_ready, 1)

                def product(i, u):
                    t = i * NB + u
                    pe.wait_ge(turn_copied, ready(t))
                    pe.sem_inc(pace_pe, 1)
                    for c in range(chunks):
                        done = pe.matmul(p_out[:, u, 0:cols], turned[:, u, c, :], weights[0:kp, c, :],
                                         start=(c == 0), stop=(c == chunks - 1 and bias is None))
                    if bias is not None:
                        done = pe.matmul(p_out[:, u, 0:cols], k.ones[0:1, :], bias, start=False, stop=True)
                    done.then_inc(out_ready, 1)
                if cols:
                    tiles_loop(pe, NT, product, (1, turn), unroll=NB)
                else:
                    tiles_loop(pe, NT, turn, unroll=NB)

            @block.vector
            def _(dve):

                def copy(i, u):
                    t = i * NB + u
                    dve.wait_ge(turn_ready, ready(t))
                    if cols:
                        dve.wait_ge(out_ready, freed(t, NB))
                    if keep is not None:
                        dve.wait_ge(kept, freed(t, NB))
                    dve.sem_inc(pace_dve, 1)
                    dve.tensor_copy(turned[:, u, :, :].rearrange("p c n -> p (c n)"),
                                    p_turned[0:kp, u, 0:chunks * P]).then_inc(turn_copied, 1)
                tiles_loop(dve, NT, copy, unroll=NB)

            @block.scalar
            def _(act):

                def keep_turned(i, u):
                    act.wait_ge(turn_copied, ready(i * NB + u))
                    act.sem_inc(pace_act, 1)
                    act.copy(keep[0:kp, :, bass.ds((i * NB + u) * P, P)], turned[:, u, :, :]).then_inc(kept, 1)

                def copy_out(i, u):
                    act.wait_ge(out_ready, ready(i * NB + u))
                    act.sem_inc(pace_act, 1)
                    act.copy(flat(target, i, u), p_out[:, u, 0:cols]).then_inc(out_copied, 1)
                if cols and keep is not None:
                    tiles_loop(act, NT, copy_out, (1, keep_turned), unroll=NB)
                elif cols:
                    tiles_loop(act, NT, copy_out, unroll=NB)
                else:
                    tiles_loop(act, NT, keep_turned, unroll=NB)


def on_vector(k, work):
    with k.nc.Block() as block:
        @block.vector
        def _(dve):
            work(dve)
            dve.drain()


def on_scalar(k, work):
    with k.nc.Block() as block:
        @block.scalar
        def _(act):
            work(act)
            act.drain()


def wide(ap, j=NT):
    return ap.unsqueeze(1).to_broadcast([P, j, ap.shape[1]])


def head_scores(k, source, vector, target, scratch):
    heads = target.shape[2]
    w = source.shape[2]

    def work(dve):
        dve.tensor_tensor(scratch[:, :, 0:w], source, wide(vector), ALU.mult)
        dve.drain()
        dve.tensor_reduce(target, scratch[:, :, 0:w].rearrange('p j (h d) -> p j h d', h=heads), AX.X, ALU.add)
    on_vector(k, work)


def attention_maxima(k, meta, tiles, heads, src_scores, dst_rows, tables, alpha, edge_w=None):
    nc = k.nc
    dw = dst_rows.shape[1]
    de = dw - heads
    with k.phase() as (sem, sb, ps):
        edge = sb("edge", [P, U, EC], I32)
        edgef = edge[:, :, :].bitcast(F32)
        s_rows = [sb(f"s_rows{u}", [P, heads]) for u in range(U)]
        d_rows = [sb(f"d_rows{u}", [P, dw]) for u in range(U)]
        old = [sb(f"old{u}", [P, heads]) for u in range(U)]
        new = [sb(f"new{u}", [P, heads]) for u in range(U)]
        other = sb("other", [P, 4, P])
        junk = sb("junk", [P, heads, P])
        al = sb("al", [P, U, heads])
        part = sb("part", [P, 2, heads])
        attr = sb("attr", [4, 2, P])
        enc = sb("enc", [P, 2, D])
        prod = sb("prod", [P, D])
        p_dst = ps("p_dst", [P, 2, 512])
        p_enc = ps("p_enc", [P, 2, 512])
        p_al = ps("p_al", [P, 2, 1024])
        S = [sem(f"edge_in{u}") for u in range(U)]
        GS = [sem(f"src_in{u}") for u in range(U)]
        GD = [sem(f"dst_in{u}") for u in range(U)]
        GO = [sem(f"old_in{u}") for u in range(U)]
        OUT = [sem(f"new_out{u}") for u in range(U)]
        row_ready, other_ready, attr_ready, enc_ready, relu_ready, alpha_ready, spread_ready, max_ready = (
            sem("row_ready"), sem("other_ready"), sem("attr_ready"), sem("enc_ready"), sem("relu_ready"),
            sem("alpha_ready"), sem("spread_ready"), sem("max_ready"))
        pace_act, pace_pe, pace_dve, pace_pool, pace_sp = (
            sem("pace_act"), sem("pace_pe"), sem("pace_dve"), sem("pace_pool"), sem("pace_sp"))
        table_v = meta.rearrange("(p t) c -> p t c", p=P)
        with nc.Block() as block:
            @block.sync
            def _(sp):
                def fetch(i, u):
                    sp.wait_ge(OUT[u], reused(i))
                    sp.sem_inc(pace_sp, 1)
                    sp.dma_start(edge[:, u, :], table_v[:, bass.ds(i * U + u, 1), :].rearrange("p a c -> p (a c)"))\
                        .then_inc(S[u], 16)
                tiles_loop(sp, tiles, fetch)

            @block.gpsimd
            def _(pool):
                def gather(i, u):
                    pool.wait_ge(S[u], landed(i))
                    pool.wait_ge(alpha_ready, freed(i * U + u, U))
                    pool.wait_ge(max_ready, freed(i * U + u, U))
                    pool.wait_ge(OUT[u], reused(i))
                    pool.sem_inc(pace_pool, 1)
                    for to, table, c, s in ((s_rows, src_scores, SRC_G, GS), (d_rows, dst_rows, DST_G, GD)):
                        pool.indirect_dma_start(to[u][:, :], None, table,
                                                bass.IndirectOffsetOnAxis(ap=edge[:, u, c:c + 1], axis=0))\
                            .then_inc(s[u], 16)
                    pool.indirect_dma_start(old[u][:, :], None, tables[u],
                                            bass.IndirectOffsetOnAxis(ap=edge[:, u, DST_G:DST_G + 1], axis=0))\
                        .then_inc(GO[u], 16)

                def scatter(i, u):
                    pool.wait_ge(max_ready, ready(i * U + u))
                    pool.sem_inc(pace_pool, 1)
                    pool.indirect_dma_start(tables[u], bass.IndirectOffsetOnAxis(ap=edge[:, u, DST_S:DST_S + 1], axis=0),
                                            new[u][:, :], None).then_inc(OUT[u], 16)
                tiles_loop(pool, tiles, scatter, (LAG, gather))
                for u in range(U):
                    pool.wait_ge(OUT[u], landed(tiles // U - 1))

            @block.tensor
            def _(pe):

                def turn(i, u):
                    t, r = i * U + u, u % 2
                    pe.wait_ge(S[u], landed(i))
                    pe.wait_ge(other_ready, freed(t, 2))
                    if edge_w is not None:
                        pe.wait_ge(relu_ready, freed(t, 2))
                    pe.sem_inc(pace_pe, 1)
                    done = pe.transpose(p_dst[:, r, 0:P], edgef[:, u, DST_F:DST_F + 1].to_broadcast([P, P]),
                                        k.ident[:, :])
                    if edge_w is not None:
                        done = pe.transpose(p_enc[0:4, r, 0:P], edgef[:, u, ATTR:ATTR + 4], k.ident[:, :])
                    done.then_inc(row_ready, 1)

                def encode(i, u):
                    t, r = i * U + u, u % 2
                    pe.wait_ge(attr_ready, ready(t))
                    pe.sem_inc(pace_pe, 1)
                    pe.matmul(p_enc[:, r, 0:D], attr[:, r, :], edge_w, start=True, stop=True).then_inc(enc_ready, 1)

                def spread(i, u):
                    t, r = i * U + u, u % 2
                    pe.wait_ge(alpha_ready, ready(t))
                    pe.wait_ge(max_ready, freed(t, 2))
                    pe.sem_inc(pace_pe, 1)
                    for h in range(heads):
                        done = pe.transpose(p_al[:, r, h * P:(h + 1) * P],
                                            al[:, u, h:h + 1].to_broadcast([P, P]), k.ident[:, :])
                    done.then_inc(spread_ready, 1)
                tiles_loop(pe, tiles, spread, (3, turn), *([(2, encode)] if edge_w is not None else []))

            @block.scalar
            def _(act):
                if edge_w is None:
                    return

                def copy_attr(i, u):
                    act.wait_ge(row_ready, ready(i * U + u))
                    act.wait_ge(enc_ready, freed(i * U + u, 2))
                    act.sem_inc(pace_act, 1)
                    act.copy(attr[:, u % 2, :], p_enc[0:4, u % 2, 0:P]).then_inc(attr_ready, 1)

                def relu(i, u):
                    act.wait_ge(enc_ready, ready(i * U + u))
                    act.wait_ge(alpha_ready, freed(i * U + u, 2))
                    act.sem_inc(pace_act, 1)
                    act.activation(enc[:, u % 2, :], p_enc[:, u % 2, 0:D], ACT.Relu).then_inc(relu_ready, 1)
                tiles_loop(act, tiles, relu, (1, copy_attr))

            @block.vector
            def _(dve):

                def compare(i, u):
                    t, r = i * U + u, u % 2
                    dve.wait_ge(row_ready, ready(t))
                    dve.wait_ge(max_ready, freed(t, 4))
                    dve.sem_inc(pace_dve, 1)
                    dve.tensor_scalar(other[:, u % 4, :], p_dst[:, r, 0:P], edgef[:, u, DST_F:DST_F + 1], NEG,
                                      ALU.not_equal, ALU.mult).then_inc(other_ready, 1)

                def scores(i, u):
                    t, r = i * U + u, u % 2
                    dve.wait_ge(GS[u], landed(i))
                    dve.wait_ge(GD[u], landed(i))
                    dve.wait_ge(spread_ready, freed(t, U))
                    dve.wait_ge(alpha_ready, freed(t, 1))
                    dve.sem_inc(pace_dve, 1)
                    dve.tensor_tensor(part[:, 0, :], s_rows[u][:, :], d_rows[u][:, de:dw], ALU.add)
                    if edge_w is not None:
                        dve.wait_ge(relu_ready, ready(t))
                        dve.sem_inc(pace_dve, 1)
                        dve.tensor_tensor(prod[:, :], enc[:, r, :], d_rows[u][:, 0:de], ALU.mult)
                        dve.drain()
                        dve.tensor_reduce(part[:, 1, :], prod[:, :].rearrange("p (h d) -> p h d", h=heads),
                                          AX.X, ALU.add)
                        dve.drain()
                        dve.tensor_tensor(part[:, 0, :], part[:, 0, :], part[:, 1, :], ALU.add)
                    dve.drain()
                    dve.scalar_tensor_tensor(al[:, u, :], part[:, 0, :], 0.2, part[:, 0, :], ALU.mult, ALU.max)
                    dve.drain()
                    dve.tensor_copy(alpha[:, bass.ds(t, 1), :].rearrange("p a h -> p (a h)"), al[:, u, :])\
                        .then_inc(alpha_ready, 1)

                def maxima(i, u):
                    t, r = i * U + u, u % 2
                    dve.wait_ge(spread_ready, ready(t))
                    dve.wait_ge(GO[u], landed(i))
                    dve.wait_ge(max_ready, freed(t, 1))
                    dve.sem_inc(pace_dve, 1)
                    for h in range(heads):
                        done = dve.tensor_tensor_reduce(junk[:, h, :], p_al[:, r, h * P:(h + 1) * P], other[:, u % 4, :],
                                                        1.0, old[u][:, h:h + 1], ALU.add, ALU.max,
                                                        new[u][:, h:h + 1])
                    done.then_inc(max_ready, 1)
                tiles_loop(dve, tiles, maxima, (2, compare), (1, scores))


def attention_sums(k, meta, tiles, heads, per, src_rows, maxima, alpha, sums):
    nc = k.nc
    fw = heads * per
    w = fw + heads
    sw = src_rows.shape[1]
    with k.phase() as (sem, sb, ps):
        edge = sb("edge", [P, U, EC], I32)
        edgef = edge[:, :, :].bitcast(F32)
        s_rows = [sb(f"s_rows{u}", [P, sw]) for u in range(U)]
        m_rows = [sb(f"m_rows{u}", [P, heads]) for u in range(U)]
        sent = [sb(f"sent{u}", [P, w]) for u in range(U)]
        same = sb("same", [P, 2, P])
        z = sb("z", [P, 2, heads])
        msg = sb("msg", [P, 2, w])
        p_dst = ps("p_dst", [P, 2, 512])
        p_sum = ps("p_sum", [P, 2, 512])
        S = [sem(f"edge_in{u}") for u in range(U)]
        GS = [sem(f"src_in{u}") for u in range(U)]
        GM = [sem(f"max_in{u}") for u in range(U)]
        OUT = [sem(f"sum_out{u}") for u in range(U)]
        row_ready, same_ready, z_ready, exp_ready, msg_ready, sum_ready, sent_ready = (
            sem("row_ready"), sem("same_ready"), sem("z_ready"), sem("exp_ready"), sem("msg_ready"),
            sem("sum_ready"), sem("sent_ready"))
        pace_act, pace_pe, pace_dve, pace_pool, pace_sp = (
            sem("pace_act"), sem("pace_pe"), sem("pace_dve"), sem("pace_pool"), sem("pace_sp"))
        table_v = meta.rearrange("(p t) c -> p t c", p=P)
        with nc.Block() as block:
            @block.sync
            def _(sp):
                def fetch(i, u):
                    sp.wait_ge(OUT[u], reused(i))
                    sp.sem_inc(pace_sp, 1)
                    sp.dma_start(edge[:, u, :], table_v[:, bass.ds(i * U + u, 1), :].rearrange("p a c -> p (a c)"))\
                        .then_inc(S[u], 16)
                tiles_loop(sp, tiles, fetch)

            @block.gpsimd
            def _(pool):
                pool.wait_ge(k.zeroed, k.zeroed_all)

                def gather(i, u):
                    pool.wait_ge(S[u], landed(i))
                    pool.wait_ge(msg_ready, freed(i * U + u, U))
                    pool.sem_inc(pace_pool, 1)
                    for to, table, c, s in ((s_rows, src_rows, SRC_G, GS), (m_rows, maxima, DST_G, GM)):
                        pool.indirect_dma_start(to[u][:, :], None, table,
                                                bass.IndirectOffsetOnAxis(ap=edge[:, u, c:c + 1], axis=0))\
                            .then_inc(s[u], 16)

                def scatter(i, u):
                    pool.wait_ge(sent_ready, ready(i * U + u))
                    pool.wait_ge(OUT[(u - CHAINS) % U], landed(i) if u >= CHAINS else reused(i))
                    pool.sem_inc(pace_pool, 1)
                    pool.indirect_dma_start(sums[u % CHAINS],
                                            bass.IndirectOffsetOnAxis(ap=edge[:, u, DST_S:DST_S + 1], axis=0),
                                            sent[u][:, :], None, compute_op=ALU.add).then_inc(OUT[u], 16)
                tiles_loop(pool, tiles, scatter, (LAG, gather))
                for u in range(U):
                    pool.wait_ge(OUT[u], landed(tiles // U - 1))

            @block.tensor
            def _(pe):

                def turn(i, u):
                    pe.wait_ge(S[u], landed(i))
                    pe.wait_ge(same_ready, freed(i * U + u, 2))
                    pe.sem_inc(pace_pe, 1)
                    pe.transpose(p_dst[:, u % 2, 0:P], edgef[:, u, DST_F:DST_F + 1].to_broadcast([P, P]),
                                 k.ident[:, :]).then_inc(row_ready, 1)

                def add_up(i, u):
                    t = i * U + u
                    pe.wait_ge(same_ready, ready(t))
                    pe.wait_ge(msg_ready, ready(t))
                    pe.wait_ge(sent_ready, freed(t, 2))
                    pe.sem_inc(pace_pe, 1)
                    pe.matmul(p_sum[:, u % 2, 0:w], same[:, u % 2, :], msg[:, u % 2, :],
                              start=True, stop=True).then_inc(sum_ready, 1)
                tiles_loop(pe, tiles, add_up, (2, turn))

            @block.scalar
            def _(act):

                def exps(i, u):
                    t = i * U + u
                    act.wait_ge(z_ready, ready(t))
                    act.wait_ge(sum_ready, freed(t, 2))
                    act.sem_inc(pace_act, 1)
                    act.activation(msg[:, u % 2, fw:w], z[:, u % 2, :], ACT.Exp).then_inc(exp_ready, 1)

                def send(i, u):
                    t = i * U + u
                    act.wait_ge(sum_ready, ready(t))
                    act.wait_ge(OUT[u], reused(i))
                    act.sem_inc(pace_act, 1)
                    act.copy(sent[u][:, :], p_sum[:, u % 2, 0:w]).then_inc(sent_ready, 1)
                tiles_loop(act, tiles, send, (1, exps))

            @block.vector
            def _(dve):

                def shift(i, u):
                    t, r = i * U + u, u % 2
                    dve.wait_ge(row_ready, ready(t))
                    dve.wait_ge(sum_ready, freed(t, 2))
                    dve.sem_inc(pace_dve, 1)
                    dve.tensor_scalar(same[:, r, :], p_dst[:, r, 0:P], edgef[:, u, DST_F:DST_F + 1], None,
                                      ALU.is_equal).then_inc(same_ready, 1)
                    dve.wait_ge(GM[u], landed(i))
                    dve.wait_ge(exp_ready, freed(t, 2))
                    dve.wait_ge(z_ready, freed(t, 1))
                    dve.sem_inc(pace_dve, 1)
                    dve.tensor_tensor(z[:, r, :], alpha[:, bass.ds(t, 1), :].rearrange("p a h -> p (a h)"),
                                      m_rows[u][:, :], ALU.subtract)
                    dve.drain()
                    dve.tensor_scalar(z[:, r, :], z[:, r, :], 0.0, None, ALU.min).then_inc(z_ready, 1)

                def message(i, u):
                    t, r = i * U + u, u % 2
                    dve.wait_ge(exp_ready, ready(t))
                    dve.wait_ge(GS[u], landed(i))
                    dve.sem_inc(pace_dve, 1)
                    dve.tensor_tensor(msg[:, r, 0:fw].rearrange("p (h d) -> p h d", h=heads),
                                      s_rows[u][:, 0:fw].rearrange("p (h d) -> p h d", h=heads),
                                      msg[:, r, fw:w].unsqueeze(2).to_broadcast([P, heads, per]), ALU.mult)\
                        .then_inc(msg_ready, 1)
                tiles_loop(dve, tiles, message, (1, shift))


def gather_sums(k, sums, target):
    nc = k.nc
    with k.phase() as (sem, sb, ps):
        first, added = sem("first"), sem("added")
        with nc.Block() as block:
            @block.sync
            def _(sp):
                sp.dma_start(target, nodes(sums[0])).then_inc(first, 16)
                sp.wait_ge(first, 16)

            @block.gpsimd
            def _(pool):
                pool.wait_ge(first, 16)
                for c in range(1, len(sums)):
                    pool.dma_start(target, nodes(sums[c]), accum_op=ALU.add).then_inc(added, 16)
                    pool.wait_ge(added, 16 * c)


def gather_maxima(k, tables, target, scratch):
    c = len(tables)
    load(k, *[(scratch[:, i, :, :], nodes(tables[i])) for i in range(c)])

    def work(dve):
        dve.tensor_reduce(target, scratch[:, :, :, :].rearrange('p c j h -> p j h c'), AX.X, ALU.max)
    on_vector(k, work)


def store(k, *pairs):
    nc = k.nc
    with k.phase() as (sem, sb, ps):
        stored = sem("stored")
        with nc.Block() as block:
            @block.sync
            def _(sp):
                for to, source in pairs:
                    sp.dma_start(to, source).then_inc(stored, 16)
                sp.wait_ge(stored, 16 * len(pairs))


def layer0_gnn(k):
    ins, H0 = k.ins, 8
    t = k.t
    with ExitStack() as ctx:
        def sb(name, shape, dt=F32):
            return ctx.enter_context(k.nc.sbuf_tensor(f"{name}_g0", shape, dt))
        xn = sb("xn", [P, NT, D])
        rows = sb("rows", [P, NT, D + H0])
        layer_norm(k, k.x[:, :, :], xn[:, :, :])
        with k.nc.sbuf_tensor("wT_g0", [P, KC, D], F32) as wT:
            load_transposed(k, (wT, ins["L0_gnn_W"]))
            project(k, xn[:, :, :], wT[:, :, :], rows[:, :, 0:D])
        scores = sb("scores", [P, NT, H0])
        vec = sb("vec", [P, 3, D])
        ew = sb("ew", [4, D])
        ewT = sb("ewT", [4, 1, D])
        load(k, (vec[:, 0, :], ins["L0_gnn_a_src"].rearrange("h d -> (h d)").partition_broadcast(P)),
             (vec[:, 1, :], ins["L0_gnn_a_dst"].rearrange("h d -> (h d)").partition_broadcast(P)),
             (vec[:, 2, :], ins["L0_gnn_bias"].partition_broadcast(P)),
             (ew[3:4, :], ins["L0_gnn_edge_b"].rearrange("(a d) -> a d", a=1)))
        load_transposed(k, (ewT, ins["L0_gnn_edge_W"]))

        def work(dve):
            dve.tensor_copy(ew[0:3, :], ewT[0:3, 0, :])
        on_vector(k, work)
        head_scores(k, rows[:, :, 0:D], vec[:, 0, :], scores[:, :, :], xn)
        head_scores(k, rows[:, :, 0:D], vec[:, 1, :], rows[:, :, D:D + H0], xn)
        store(k, (nodes(t["rows0"]), rows[:, :, :]), (nodes(t["scores0"]), scores[:, :, :]))
        alpha = sb("alpha", [P, T1, H0])
        attention_maxima(k, k.meta1, T1, H0, t["scores0"], t["rows0"], t["max0"], alpha, ew[:, :])
        peak = sb("peak", [P, NT, H0])
        with k.nc.sbuf_tensor("all_g0", [P, MCHAINS, NT, H0], F32) as each:
            gather_maxima(k, t["max0"], peak[:, :, :], each)
        store(k, (nodes(t["peak0"]), peak[:, :, :]))
        attention_sums(k, k.meta1, T1, H0, D // H0, t["rows0"], t["peak0"], alpha, t["sum0"])
        gather_sums(k, t["sum0"], rows[:, :, :])
        den = rows[:, :, D:D + H0]
        num = rows[:, :, 0:D].rearrange("p j (h d) -> p j h d", h=H0)
        res = xn[:, :, :].rearrange("p j (h d) -> p j h d", h=H0)

        def divide(dve):
            for h in range(H0):
                dve.tensor_tensor(res[:, :, h, :], num[:, :, h, :],
                                  scores[:, :, h:h + 1].to_broadcast([P, NT, D // H0]), ALU.mult)

        def work(dve):
            dve.tensor_scalar(den, den, 1e-10, None, ALU.max)
            dve.drain()
            dve.reciprocal(scores[:, :, :], den)
            dve.drain()
            divide(dve)
            dve.drain()
            dve.tensor_tensor(xn[:, :, :], xn[:, :, :], wide(vec[:, 2, :]), ALU.add)
            dve.drain()
            dve.tensor_tensor(k.x[:, :, :], k.x[:, :, :], xn[:, :, :], ALU.add)
        on_vector(k, work)


def sum_over_graph(k, matrix, source, target):
    nc = k.nc
    w = source.shape[2]
    stripes = matrix[0:CELLS, :].rearrange("(a p c) o -> p a (c o)", p=P, c=NP)
    with k.phase() as (sem, sb, ps):
        stripe = [sb(f"stripe{u}", [P, NT, P]) for u in range(NB)]
        p_sum = ps("p_sum", [P, NB, 512])
        IN = [sem(f"stripe_in{u}") for u in range(NB)]
        sum_ready, sum_copied = sem("sum_ready"), sem("sum_copied")
        pace_pe, pace_act, pace_sp = sem("pace_pe"), sem("pace_act"), sem("pace_sp")
        with nc.Block() as block:
            @block.sync
            def _(sp):
                def fetch(i, u):
                    sp.wait_ge(sum_ready, freed(i * NB + u, NB))
                    sp.sem_inc(pace_sp, 1)
                    sp.dma_start(stripe[u][:, :, :], stripes[:, :, bass.ds((i * NB + u) * P, P)]).then_inc(IN[u], 16)
                tiles_loop(sp, NT, fetch, unroll=NB)

            @block.tensor
            def _(pe):
                def product(i, u):
                    pe.wait_ge(IN[u], landed(i))
                    pe.wait_ge(sum_copied, freed(i * NB + u, NB))
                    pe.sem_inc(pace_pe, 1)
                    for j in range(NT):
                        done = pe.matmul(p_sum[:, u, 0:w], stripe[u][:, j, :], source[:, j, :],
                                         start=(j == 0), stop=(j == NT - 1))
                    done.then_inc(sum_ready, 1)
                tiles_loop(pe, NT, product, unroll=NB)

            @block.scalar
            def _(act):
                def copy_out(i, u):
                    act.wait_ge(sum_ready, ready(i * NB + u))
                    act.sem_inc(pace_act, 1)
                    act.copy(target[:, bass.ds(i * NB + u, 1), :].rearrange("p a w -> p (a w)"), p_sum[:, u, 0:w])\
                        .then_inc(sum_copied, 1)
                tiles_loop(act, NT, copy_out, unroll=NB)


def filtered_messages(k, queries, keyvals, radial, filters, sums):
    nc = k.nc
    tiles, meta = T1, k.meta1
    R = radial.shape[2]
    w = D + 1
    with k.phase() as (sem, sb, ps):
        edge = sb("edge", [P, U, EC], I32)
        edgef = edge[:, :, :].bitcast(F32)
        feats = sb("feats", [P, U, R])
        q_rows = [sb(f"q_rows{u}", [P, D]) for u in range(U)]
        kv_rows = [sb(f"kv_rows{u}", [P, 2 * D]) for u in range(U)]
        sent = [sb(f"sent{u}", [P, w]) for u in range(U)]
        same = sb("same", [P, 2, P])
        featT = sb("featT", [R + 1, 2, P])
        gates = sb("gates", [P, 2, 2 * D])
        qk = sb("qk", [P, D])
        junk = sb("junk", [P, D])
        vd = sb("vd", [P, 2, D])
        score = sb("score", [P, 2, 1])
        curve = sb("curve", [P, 2, 1])
        attn = sb("attn", [P, 2, 1])
        msg = sb("msg", [P, 2, w])
        p_num = ps("p_num", [P, 2, 512])
        p_filt = ps("p_filt", [P, 2, 512])
        p_sum = ps("p_sum", [P, 2, 512])
        p_feat = ps("p_feat", [P, 2, 512])
        S = [sem(f"edge_in{u}") for u in range(U)]
        F = [sem(f"feat_in{u}") for u in range(U)]
        GQ = [sem(f"q_in{u}") for u in range(U)]
        GK = [sem(f"kv_in{u}") for u in range(U)]
        OUT = [sem(f"sum_out{u}") for u in range(U)]
        row_ready, same_ready, sum_ready, sent_ready = (
            sem("row_ready"), sem("same_ready"), sem("sum_ready"), sem("sent_ready"))
        feat_ready, featT_ready, filt_ready, gates_ready, score_ready, curve_ready, msg_ready, ones_ready, attn_ready = (
            sem("feat_ready"), sem("featT_ready"), sem("filt_ready"), sem("gates_ready"), sem("score_ready"),
            sem("curve_ready"), sem("msg_ready"), sem("ones_ready"), sem("attn_ready"))
        pace_act, pace_pe, pace_dve, pace_pool, pace_sp = (
            sem("pace_act"), sem("pace_pe"), sem("pace_dve"), sem("pace_pool"), sem("pace_sp"))
        table_v = meta.rearrange("(p t) c -> p t c", p=P)
        with nc.Block() as block:
            @block.sync
            def _(sp):
                sp.wait_ge(k.copied, k.copied_all)

                def fetch(i, u):
                    t = bass.ds(i * U + u, 1)
                    sp.wait_ge(OUT[u], reused(i))
                    sp.sem_inc(pace_sp, 1)
                    sp.dma_start(edge[:, u, :], table_v[:, t, :].rearrange("p a c -> p (a c)")).then_inc(S[u], 16)
                    sp.dma_start(feats[:, u, :], radial[:, t, :].rearrange("p a c -> p (a c)")).then_inc(F[u], 16)
                tiles_loop(sp, tiles, fetch)

            @block.gpsimd
            def _(pool):
                pool.wait_ge(k.zeroed, k.zeroed_all)

                def gather(i, u):
                    pool.wait_ge(S[u], landed(i))
                    pool.wait_ge(msg_ready, freed(i * U + u, U))
                    pool.sem_inc(pace_pool, 1)
                    for to, table, c, s in ((q_rows, queries, DST_G, GQ), (kv_rows, keyvals, SRC_G, GK)):
                        pool.indirect_dma_start(to[u][:, :], None, table,
                                                bass.IndirectOffsetOnAxis(ap=edge[:, u, c:c + 1], axis=0))\
                            .then_inc(s[u], 16)

                def scatter(i, u):
                    pool.wait_ge(sent_ready, ready(i * U + u))
                    pool.wait_ge(OUT[(u - CHAINS) % U], landed(i) if u >= CHAINS else reused(i))
                    pool.sem_inc(pace_pool, 1)
                    pool.indirect_dma_start(sums[u % CHAINS],
                                            bass.IndirectOffsetOnAxis(ap=edge[:, u, DST_S:DST_S + 1], axis=0),
                                            sent[u][:, :], None, compute_op=ALU.add).then_inc(OUT[u], 16)
                tiles_loop(pool, tiles, scatter, (LAG, gather))
                for u in range(U):
                    pool.wait_ge(OUT[u], landed(tiles // U - 1))

            @block.tensor
            def _(pe):
                def turn(i, u):
                    t, r = i * U + u, u % 2
                    pe.wait_ge(S[u], landed(i))
                    pe.wait_ge(F[u], landed(i))
                    pe.wait_ge(same_ready, freed(t, 2))
                    pe.wait_ge(featT_ready, freed(t, 2))
                    pe.sem_inc(pace_pe, 1)
                    pe.transpose(p_num[:, r, 0:P], edgef[:, u, DST_F:DST_F + 1].to_broadcast([P, P]), k.ident[:, :])
                    pe.transpose(p_feat[0:R, r, 0:P], feats[:, u, :], k.ident[:, :]).then_inc(row_ready, 1)

                def filt(i, u):
                    t, r = i * U + u, u % 2
                    pe.wait_ge(featT_ready, ready(t))
                    pe.wait_ge(gates_ready, freed(t, 2))
                    pe.sem_inc(pace_pe, 1)
                    pe.matmul(p_filt[:, r, :], featT[:, r, :], filters, start=True, stop=True).then_inc(filt_ready, 1)

                def add_up(i, u):
                    t, r = i * U + u, u % 2
                    pe.wait_ge(same_ready, ready(t))
                    pe.wait_ge(msg_ready, ready(t))
                    pe.wait_ge(sent_ready, freed(t, 2))
                    pe.sem_inc(pace_pe, 1)
                    pe.matmul(p_sum[:, r, 0:w], same[:, r, :], msg[:, r, :], start=True, stop=True)\
                        .then_inc(sum_ready, 1)
                tiles_loop(pe, tiles, add_up, (3, turn), (2, filt))

            @block.scalar
            def _(act):
                def copy_feat(i, u):
                    t, r = i * U + u, u % 2
                    act.wait_ge(row_ready, ready(t))
                    act.wait_ge(filt_ready, freed(t, 2))
                    act.wait_ge(ones_ready, 1)
                    act.sem_inc(pace_act, 1)
                    act.copy(featT[0:R, r, :], p_feat[0:R, r, 0:P]).then_inc(featT_ready, 1)

                def gate(i, u):
                    t, r = i * U + u, u % 2
                    act.wait_ge(filt_ready, ready(t))
                    act.wait_ge(msg_ready, freed(t, 2))
                    act.sem_inc(pace_act, 1)
                    act.activation(gates[:, r, :], p_filt[:, r, :], ACT.Silu).then_inc(gates_ready, 1)

                def attention(i, u):
                    t, r = i * U + u, u % 2
                    act.wait_ge(score_ready, ready(t))
                    act.wait_ge(attn_ready, freed(t, 2))
                    act.sem_inc(pace_act, 1)
                    act.activation(curve[:, r, :], score[:, r, :], ACT.Silu).then_inc(curve_ready, 1)

                def send(i, u):
                    t = i * U + u
                    act.wait_ge(sum_ready, ready(t))
                    act.wait_ge(OUT[u], reused(i))
                    act.sem_inc(pace_act, 1)
                    act.copy(sent[u][:, :], p_sum[:, u % 2, 0:w]).then_inc(sent_ready, 1)
                tiles_loop(act, tiles, send, (3, copy_feat), (2, gate), (1, attention))

            @block.vector
            def _(dve):
                dve.memset(featT[R:R + 1, :, :], 1.0).then_inc(ones_ready, 1)
                dve.memset(msg[:, :, D:w], 1.0)

                def compare(i, u):
                    t, r = i * U + u, u % 2
                    dve.wait_ge(row_ready, ready(t))
                    dve.wait_ge(sum_ready, freed(t, 2))
                    dve.sem_inc(pace_dve, 1)
                    dve.tensor_scalar(same[:, r, :], p_num[:, r, 0:P], edgef[:, u, DST_F:DST_F + 1], None,
                                      ALU.is_equal).then_inc(same_ready, 1)

                def scores(i, u):
                    t, r = i * U + u, u % 2
                    dve.wait_ge(GQ[u], landed(i))
                    dve.wait_ge(GK[u], landed(i))
                    dve.wait_ge(score_ready, freed(t, 1))
                    dve.wait_ge(curve_ready, freed(t, 2))
                    dve.sem_inc(pace_dve, 1)
                    dve.tensor_tensor(qk[:, :], q_rows[u][:, :], kv_rows[u][:, 0:D], ALU.mult)
                    dve.wait_ge(gates_ready, ready(t))
                    dve.wait_ge(msg_ready, freed(t, 2))
                    dve.sem_inc(pace_dve, 1)
                    dve.tensor_tensor(vd[:, r, :], kv_rows[u][:, D:2 * D], gates[:, r, D:2 * D], ALU.mult)
                    dve.drain()
                    dve.tensor_tensor_reduce(junk[:, :], qk[:, :], gates[:, r, 0:D], 1.0, 0.0, ALU.mult, ALU.add,
                                             score[:, r, :]).then_inc(score_ready, 1)

                def message(i, u):
                    t, r = i * U + u, u % 2
                    dve.wait_ge(curve_ready, ready(t))
                    dve.wait_ge(sum_ready, freed(t, 2))
                    dve.wait_ge(msg_ready, freed(t, 1))
                    dve.sem_inc(pace_dve, 1)
                    dve.tensor_tensor(attn[:, r, :], curve[:, r, :], edgef[:, u, CUT:CUT + 1], ALU.mult)\
                        .then_inc(attn_ready, 1)
                    dve.wait_ge(attn_ready, ready(t))
                    dve.sem_inc(pace_dve, 1)
                    dve.tensor_scalar(msg[:, r, 0:D], vd[:, r, :], attn[:, r, 0:1], None, ALU.mult)\
                        .then_inc(msg_ready, 1)
                tiles_loop(dve, tiles, message, (1, compare), (1, scores))


def add_pairs_to_matrices(k, pool, pairs, cell, cell_ready, M):
    first, end = pairs
    pool.wait_ge(k.matrix_zeroed, k.matrix_zeroed_all)

    def pick(i, u):
        for m in range(2):
            pool.wait_ge(M[m][u], reused(i))
        pool.tensor_copy(cell[:, u, :], k.cells[:, bass.ds(first + i * CR + u, 1), :].rearrange("p a c -> p (a c)"))\
            .then_inc(cell_ready, 1)

    def scatter(i, u):
        t = i * CR + u
        for m, (where, what) in enumerate(((CELL_SD, COUNT), (CELL_DS, WSUM))):
            pool.wait_ge(M[m][(u - 1) % CR], landed(i) if u else reused(i))
            pool.wait_ge(cell_ready, ready(t))
            pool.sem_inc(k.paced, 1)
            pool.indirect_dma_start(k.matrices[m], bass.IndirectOffsetOnAxis(ap=cell[:, u, where:where + 1], axis=0),
                                    cell[:, u, what:what + 1].bitcast(F32), None, compute_op=ALU.add)\
                .then_inc(M[m][u], 16)
    tiles_loop(pool, end - first, scatter, (1, pick), unroll=CR)
    for m in range(2):
        for u in range(CR):
            pool.wait_ge(M[m][u], landed((end - first) // CR - 1))


def experts(k, xT, gate, out, count, hidden, last, outs=1, pairs=None):
    nc = k.nc
    units = count // outs
    blocks = NT // NB
    cols = NB * P
    half = cols // 2
    per_body = 2 * blocks
    chunks = sum(h[1] for h in hidden)
    rows_last = P // outs
    with k.phase() as (sem, sb, ps):
        w = [[sb(f"w{s}_{n}", [P, h[3], h[1] * P]) for n, h in enumerate(hidden)] for s in range(2)]
        wo = [sb(f"wo{s}", [P, last[1], D]) for s in range(2)]
        hid = [[sb(f"hid{s}_{n}", [P, h[1], cols]) for n, h in enumerate(hidden)] for s in range(2)]
        p_hid = ps("p_hid", [P, 2, 2, 512])
        p_out = ps("p_out", [P, 2, 512])
        W = [sem(f"weights_in{s}") for s in range(2)]
        cell, cell_ready = sb("cell", [P, CR, 4], I32), sem("cell_ready")
        M = [[sem(f"matrix{m}_out{u}") for u in range(CR)] for m in range(2)]
        hid_ready, hid_copied, out_ready, out_added = (
            sem("hid_ready"), sem("hid_copied"), sem("out_ready"), sem("out_added"))
        pace_act, pace_pe, pace_dve, pace_sp = sem("pace_act"), sem("pace_pe"), sem("pace_dve"), sem("pace_sp")
        loads = len(hidden) + 1
        ys = NB * outs
        first = [sum(h[1] for h in hidden[:n]) for n in range(len(hidden))]

        def unit_loop(eng, body):
            body(0)
            with eng.Fori(1, units // 2) as i:
                body(i)

        with nc.Block() as block:
            @block.sync
            def _(sp):
                def fetch(i):
                    for s in range(2):
                        sp.wait_ge(out_ready, past(((i - 1) * per_body + (s + 1) * blocks) * ys))
                        sp.sem_inc(pace_sp, 1)
                        e = (2 * i + s) * outs
                        for n, h in enumerate(hidden):
                            for to, source in h[0](w[s][n], e):
                                sp.dma_start(to, source).then_inc(W[s], 16)
                        sp.dma_start(wo[s][:, :, :], last[0](e)).then_inc(W[s], 16)
                unit_loop(sp, fetch)
            loads = sum(len(h[0](w[0][n], 0)) for n, h in enumerate(hidden)) + 1

            @block.gpsimd
            def _(pool):
                if pairs is not None:
                    add_pairs_to_matrices(k, pool, pairs, cell, cell_ready, M)

            @block.tensor
            def _(pe):
                def layer(i, b, n):
                    s, it = b // blocks, i * per_body + b
                    _, outc, _, inc = hidden[n]
                    at = (b % blocks) * cols
                    for c in range(outc):
                        q = it * chunks + first[n] + c
                        qs = (b * chunks + first[n] + c) % 2
                        if n == 0 and b % blocks == 0 and c == 0:
                            pe.wait_ge(W[s], 16 * loads * (i + 1))
                        if n and c == 0:
                            pe.wait_ge(hid_copied, it * chunks + first[n])
                        pe.wait_ge(hid_copied, freed(q, 2))
                        pe.sem_inc(pace_pe, 1)
                        for z in range(2):
                            for kc in range(inc):
                                if n == 0:
                                    rhs = xT[:, kc, at + z * half:at + (z + 1) * half]
                                else:
                                    rhs = hid[b % 2][n - 1][:, kc, z * half:(z + 1) * half]
                                done = pe.matmul(p_hid[:, qs, z, 0:half], w[s][n][:, kc, c * P:(c + 1) * P], rhs,
                                                 start=(kc == 0), stop=(kc == inc - 1))
                        done.then_inc(hid_ready, 1)

                def finish(i, b):
                    s, it = b // blocks, i * per_body + b
                    pe.wait_ge(hid_copied, (it + 1) * chunks)
                    pe.sem_inc(pace_pe, 1)
                    for o in range(outs):
                        p0 = o * rows_last
                        for j in range(NB):
                            y = it * ys + o * NB + j
                            pe.wait_ge(out_added, freed(y, 2))
                            pe.sem_inc(pace_pe, 1)
                            for kc in range(last[1]):
                                done = pe.matmul(p_out[:, (b * ys + o * NB + j) % 2, 0:D],
                                                 hid[b % 2][-1][p0:p0 + rows_last, kc, j * P:(j + 1) * P],
                                                 wo[s][p0:p0 + rows_last, kc, :],
                                                 start=(kc == 0), stop=(kc == last[1] - 1))
                            done.then_inc(out_ready, 1)

                def body(i):
                    for b in range(per_body):
                        layer(i, b, 0)
                        if b:
                            finish(i, b - 1)
                        for n in range(1, len(hidden)):
                            layer(i, b, n)
                    finish(i, per_body - 1)
                unit_loop(pe, body)

            @block.scalar
            def _(act):
                def body(i):
                    for b in range(per_body):
                        it = i * per_body + b
                        e = (2 * i + b // blocks)
                        for n, (_, outc, func, _) in enumerate(hidden):
                            for c in range(outc):
                                q = it * chunks + first[n] + c
                                qs = (b * chunks + first[n] + c) % 2
                                act.wait_ge(hid_ready, q + 1)
                                act.wait_ge(out_ready, past((it - 1) * ys))
                                act.sem_inc(pace_act, 1)
                                func(act, hid[b % 2][n][:, c, :].rearrange("p (z n) -> p z n", z=2),
                                     p_hid[:, qs, :, 0:half], e, c).then_inc(hid_copied, 1)
                unit_loop(act, body)

            @block.vector
            def _(dve):
                def body(i):
                    for b in range(per_body):
                        it = i * per_body + b
                        for o in range(outs):
                            e = (2 * i + b // blocks) * outs + o
                            for j in range(NB):
                                y = it * ys + o * NB + j
                                node = (b % blocks) * NB + j
                                dve.wait_ge(out_ready, y + 1)
                                dve.wait_ge(out_added, freed(y, NB))
                                dve.sem_inc(pace_dve, 1)
                                dve.scalar_tensor_tensor(out[:, node, :], p_out[:, (b * ys + o * NB + j) % 2, 0:D],
                                                         gate[:, node, bass.ds(e, 1)], out[:, node, :],
                                                         ALU.mult, ALU.add).then_inc(out_added, 1)
                unit_loop(dve, body)


def per_node(ap, width):
    return ap.unsqueeze(2).to_broadcast([P, NT, width])


def one_hot_of_max(dve, k, logits, pick, peak, spot, scratch):
    e = logits.shape[2]
    num = wide(k.col[:, 0:e])
    dve.tensor_reduce(peak, logits, AX.X, ALU.max)
    dve.drain()
    dve.tensor_tensor(scratch, logits, per_node(peak, e), ALU.is_equal)
    dve.drain()
    dve.tensor_scalar(scratch, scratch, -float(P), float(P), ALU.mult, ALU.add)
    dve.drain()
    dve.tensor_tensor(scratch, scratch, num, ALU.add)
    dve.drain()
    dve.tensor_reduce(spot, scratch, AX.X, ALU.min)
    dve.drain()
    dve.tensor_tensor(pick, num, per_node(spot, e), ALU.is_equal)
    dve.drain()


def top2_gate(k, logits, gate):
    e = logits.shape[2]
    with ExitStack() as ctx:
        def sb(name, shape):
            return ctx.enter_context(k.nc.sbuf_tensor(f"{name}_{k.nc.next_id()}", shape, F32))
        m1, m2, spot, z, ez, w1, w2 = (sb(n, [P, NT])[:, :] for n in ("m1", "m2", "spot", "z", "ez", "w1", "w2"))
        pick1, pick2, rest, scratch = (sb(n, [P, NT, e])[:, :, :] for n in ("pick1", "pick2", "rest", "scratch"))

        def work(dve):
            one_hot_of_max(dve, k, logits, pick1, m1, spot, scratch)
            dve.scalar_tensor_tensor(rest, pick1, NEG, logits, ALU.mult, ALU.add)
            dve.drain()
            one_hot_of_max(dve, k, rest, pick2, m2, spot, scratch)
            dve.tensor_tensor(z, m2, m1, ALU.subtract)
        on_vector(k, work)

        def work(act):
            act.activation(ez, z, ACT.Exp)
        on_scalar(k, work)

        def work(dve):
            dve.tensor_scalar(w1, ez, 1.0, None, ALU.add)
            dve.drain()
            dve.reciprocal(z, w1)
            dve.drain()
            dve.tensor_tensor(w2, ez, z, ALU.mult)
            dve.drain()
            dve.tensor_tensor(pick1, pick1, per_node(z, e), ALU.mult)
            dve.drain()
            dve.tensor_tensor(pick2, pick2, per_node(w2, e), ALU.mult)
            dve.drain()
            dve.tensor_tensor(gate, pick1, pick2, ALU.add)
        on_vector(k, work)


def gelu_experts(k, xT, gate, out, name, count, pairs):
    ins, nc = k.ins, k.nc
    w1, b1, w2 = ins[f"{name}_W1"], ins[f"{name}_b1"], ins[f"{name}_W2"]
    hc = w1.shape[2] // P
    with nc.sbuf_tensor(f"b1_{name}", [P, count, hc], F32) as bias:
        with nc.allow_non_contiguous_dma(reason="4096 biases, once"):
            load(k, *[(bias[:, :, c], b1[:, c * P:(c + 1) * P].rearrange("e p -> p e")) for c in range(hc)])
        experts(
            k, xT, gate, out, count,
            [(lambda w, e: [(w[:, :, :], w1[bass.ds(e, 1), :, :].rearrange("a (c p) h -> p (a c) h", p=P))], hc,
              lambda act, to, source, e, c: act.activation(
                  to, source, ACT.Gelu, bias=bias[:, bass.ds(e, 1), c]), KC)],
            (lambda e: w2[bass.ds(e, 1), :, :].rearrange("a (c p) d -> p (a c) d", p=P), hc), pairs=pairs)


def add_to_state(k, *parts):
    def add(dve):
        for part in parts:
            dve.tensor_tensor(k.x[:, :, :], k.x[:, :, :], part, ALU.add)
            dve.drain()
    on_vector(k, add)


def layer0_ffn(k):
    ins, E = k.ins, 8
    with ExitStack() as ctx:
        def sb(name, shape, dt=F32):
            return ctx.enter_context(k.nc.sbuf_tensor(f"{name}_f0", shape, dt))
        y = sb("y", [P, NT, D])
        xT = sb("xT", [P, KC, NP])
        logits = sb("logits", [P, NT, E])
        gate = sb("gate", [P, NT, E])
        wr = sb("wr", [P, KC, E])
        br = sb("br", [1, E])
        b2 = sb("b2", [E, 1, D])
        layer_norm(k, k.x[:, :, :], y[:, :, :])
        layer_norm(k, y[:, :, :], y[:, :, :], ins["L0_ffn_gamma"], ins["L0_ffn_beta"])
        load(k, (wr[:, :, :], ins["L0_ffn_Wr"].rearrange("(c p) e -> p c e", p=P)),
             (br[:, :], ins["L0_ffn_br"].rearrange("(a e) -> a e", a=1)), (b2[:, 0, :], ins["L0_ffn_b2"]))
        project(k, y[:, :, :], wr, logits[:, :, :], bias=br[:, :], keep=xT)
        top2_gate(k, logits[:, :, :], gate[:, :, :])
        project(k, gate[:, :, :], b2, y[:, :, :])
        gelu_experts(k, xT, gate, y, "L0_ffn", E, (0, PAIRS_SPLIT))
        add_to_state(k, y[:, :, :])


def layer1_gnn(k):
    ins, t, R = k.ins, k.t, 64
    with ExitStack() as ctx:
        def sb(name, shape, dt=F32):
            return ctx.enter_context(k.nc.sbuf_tensor(f"{name}_g1", shape, dt))
        xn = sb("xn", [P, NT, D])
        res = sb("res", [P, NT, D])
        wT = sb("wT", [P, 4, KC, D])
        bias = sb("bias", [1, 4, D])
        filters = sb("filters", [R + 1, 1, 2 * D])
        layer_norm(k, k.x[:, :, :], xn[:, :, :])
        layer_norm(k, xn[:, :, :], xn[:, :, :], ins["L1_gnn_ln_g"], ins["L1_gnn_ln_b"])
        for n, name in enumerate("qkvo"):
            load_transposed(k, (wT[:, n], ins[f"L1_gnn_W{name}"]))
        load_transposed(k, (filters[0:R, :, 0:D], ins["L1_gnn_Wdk"]), (filters[0:R, :, D:2 * D], ins["L1_gnn_Wdv"]))
        load(k, *[(bias[:, n, :], ins[f"L1_gnn_b{name}"].rearrange("(a d) -> a d", a=1)) for n, name in enumerate("qkvo")],
             (filters[R:R + 1, 0, 0:D], ins["L1_gnn_bdk"].rearrange("(a d) -> a d", a=1)),
             (filters[R:R + 1, 0, D:2 * D], ins["L1_gnn_bdv"].rearrange("(a d) -> a d", a=1)))
        for n, to in enumerate((nodes(t["query1"]), nodes(t["keyval1"])[:, :, 0:D], nodes(t["keyval1"])[:, :, D:2 * D])):
            project(k, xn[:, :, :], wT[:, n], res[:, :, :], bias=bias[:, n, :])
            store(k, (to, res[:, :, :]))
        filtered_messages(k, t["query1"], t["keyval1"], t["radial1"].rearrange("(p t) c -> p t c", p=P),
                          filters[:, 0, :], t["sum1"])
        with k.nc.sbuf_tensor("agg_g1", [P, NT, D + 1], F32) as agg:
            gather_sums(k, t["sum1"], agg[:, :, :])

            def work(dve):
                dve.tensor_scalar(k.dinv[:, :], agg[:, :, D], 1.0, 1e-12, ALU.add, ALU.max)
            on_vector(k, work)

            def work(act):
                act.activation(k.dinv[:, :], k.dinv[:, :], ACT.Sqrt)
            on_scalar(k, work)

            def work(dve):
                dve.reciprocal(k.dinv[:, :], k.dinv[:, :])
            on_vector(k, work)
            project(k, agg[:, :, 0:D], wT[:, 3], res[:, :, :], bias=bias[:, 3, :])
        layer_norm(k, k.x[:, :, :], xn[:, :, :])
        add_to_state(k, xn[:, :, :], res[:, :, :])


def layer1_ffn(k):
    ins, t, E, H1 = k.ins, k.t, 4, 4
    W = H1 * E
    with ExitStack() as ctx:
        def sb(name, shape, dt=F32):
            return ctx.enter_context(k.nc.sbuf_tensor(f"{name}_f1", shape, dt))
        y = sb("y", [P, NT, D])
        xT = sb("xT", [P, KC, NP])
        gate = sb("gate", [P, NT, E])
        b2 = sb("b2", [E, 1, D])
        layer_norm(k, k.x[:, :, :], y[:, :, :])
        with ExitStack() as inner:
            def tb(name, shape, dt=F32):
                return inner.enter_context(k.nc.sbuf_tensor(f"{name}_f1", shape, dt))
            rows = tb("rows", [P, NT, W + H1])
            sums = tb("sums", [P, NT, W + H1])
            wg = tb("wg", [P, KC, W])
            vec = tb("vec", [P, 5, W])
            src = tb("src", [P, NT, H1])
            dst = tb("dst", [P, NT, H1])
            own = tb("own", [P, NT, H1])
            peak = tb("peak", [P, NT, H1])
            scratch = tb("scratch", [P, NT, W])
            mean = tb("mean", [P, NT])
            var = tb("var", [P, NT])
            alpha = tb("alpha", [P, T2, H1])
            each = tb("each", [P, MCHAINS, NT, H1])
            flat = [ins[f"L1_ffn_{n}"].rearrange("h e -> (h e)") for n in ("att_src", "att_dst")] + [
                ins[f"L1_ffn_{n}"] for n in ("b_gat", "ln_gamma", "ln_beta")]
            load(k, (wg[:, :, :], ins["L1_ffn_W_gat"].rearrange("(c p) e -> p c e", p=P)),
                 (b2[:, 0, :], ins["L1_ffn_b2"]),
                 *[(vec[:, n, :], v.partition_broadcast(P)) for n, v in enumerate(flat)])
            project(k, y[:, :, :], wg, rows[:, :, 0:W], keep=xT)
            head_scores(k, rows[:, :, 0:W], vec[:, 0, :], src[:, :, :], scratch)
            head_scores(k, rows[:, :, 0:W], vec[:, 1, :], dst[:, :, :], scratch)

            def work(dve):
                dve.memset(rows[:, :, W:W + H1], 0.0)
                dve.drain()
                dve.tensor_tensor(own[:, :, :], src[:, :, :], dst[:, :, :], ALU.add)
                dve.drain()
                dve.scalar_tensor_tensor(own[:, :, :], own[:, :, :], 0.2, own[:, :, :], ALU.mult, ALU.max)
            on_vector(k, work)
            store(k, (nodes(t["rows1"]), rows[:, :, :]), (nodes(t["src1"]), src[:, :, :]),
                  (nodes(t["dst1"]), dst[:, :, :]))
            attention_maxima(k, k.meta2, T2, H1, t["src1"], t["dst1"], t["max1"], alpha)
            gather_maxima(k, t["max1"], peak[:, :, :], each)

            def work(dve):
                dve.tensor_tensor(peak[:, :, :], peak[:, :, :], own[:, :, :], ALU.max)
                dve.drain()
                dve.tensor_tensor(own[:, :, :], own[:, :, :], peak[:, :, :], ALU.subtract)
            on_vector(k, work)

            def work(act):
                act.activation(own[:, :, :], own[:, :, :], ACT.Exp)
            on_scalar(k, work)
            store(k, (nodes(t["peak1"]), peak[:, :, :]))
            attention_sums(k, k.meta2, T2, H1, E, t["rows1"], t["peak1"], alpha, t["sumr"])
            gather_sums(k, t["sumr"], sums[:, :, :])

            def heads(ap):
                return ap.rearrange("p j (h e) -> p j h e", h=H1)

            def spread(dve, out, a, b):
                for h in range(H1):
                    dve.tensor_tensor(heads(out)[:, :, h, :], heads(a)[:, :, h, :],
                                      b[:, :, h:h + 1].to_broadcast([P, NT, E]), ALU.mult)
            num, den, z = sums[:, :, 0:W], sums[:, :, W:W + H1], scratch[:, :, :]

            def work(dve):
                spread(dve, z, rows[:, :, 0:W], own[:, :, :])
                dve.drain()
                dve.tensor_tensor(num, num, z, ALU.add)
                dve.drain()
                dve.tensor_tensor(den, den, own[:, :, :], ALU.add)
                dve.drain()
                dve.tensor_scalar(den, den, 1e-16, None, ALU.add)
                dve.drain()
                dve.reciprocal(peak[:, :, :], den)
                dve.drain()
                spread(dve, z, num, peak[:, :, :])
                dve.drain()
                dve.tensor_tensor(z, z, wide(vec[:, 2, :]), ALU.add)
                dve.drain()
                dve.tensor_reduce(mean[:, :], z, AX.X, ALU.add)
                dve.drain()
                dve.tensor_scalar(mean[:, :], mean[:, :], 1.0 / W, None, ALU.mult)
                dve.drain()
                dve.tensor_tensor(z, z, per_node(mean[:, :], W), ALU.subtract)
                dve.drain()
                dve.tensor_tensor(num, z, z, ALU.mult)
                dve.drain()
                dve.tensor_reduce(var[:, :], num, AX.X, ALU.add)
                dve.drain()
                dve.tensor_scalar(var[:, :], var[:, :], 1.0 / W, EPS, ALU.mult, ALU.add)
            on_vector(k, work)

            def work(act):
                act.activation(mean[:, :], var[:, :], ACT.Sqrt)
            on_scalar(k, work)

            def work(dve):
                dve.reciprocal(var[:, :], mean[:, :])
                dve.drain()
                dve.tensor_tensor(z, z, per_node(var[:, :], W), ALU.mult)
                dve.drain()
                dve.tensor_tensor(z, z, wide(vec[:, 3, :]), ALU.mult)
                dve.drain()
                dve.tensor_tensor(z, z, wide(vec[:, 4, :]), ALU.add)
                dve.drain()
                dve.tensor_reduce(own[:, :, :], heads(z).rearrange('p j h e -> p j e h'), AX.X, ALU.add)
                dve.drain()
                dve.tensor_scalar(own[:, :, :], own[:, :, :], 1.0 / H1, None, ALU.mult)
            on_vector(k, work)
            top2_gate(k, own[:, :, :], gate[:, :, :])
        project(k, gate[:, :, :], b2, y[:, :, :])
        gelu_experts(k, xT, gate, y, "L1_ffn", E, (PAIRS_SPLIT, T1))
        add_to_state(k, y[:, :, :])


def layer2_gnn(k):
    ins = k.ins
    with ExitStack() as ctx:
        def sb(name, shape, dt=F32):
            return ctx.enter_context(k.nc.sbuf_tensor(f"{name}_g2", shape, dt))
        xn = sb("xn", [P, NT, D])
        a = sb("a", [P, NT, 2 * 64])
        b = sb("b", [P, NT, 2 * 64])
        w1 = sb("w1", [P, 2, 128])
        w2 = sb("w2", [P, 1, 64])
        w3 = sb("w3", [64, 1, 128])
        w4 = sb("w4", [P, 1, 256])
        b12 = sb("b12", [P, 2, 128])
        b34 = sb("b34", [1, 2, 256])
        layer_norm(k, k.x[:, :, :], xn[:, :, :])
        load(k, (w1[:, :, :], ins["L2_gnn_W1"].rearrange("(c p) n -> p c n", p=P)), (w2[:, 0, :], ins["L2_gnn_W2"]),
             (w3[:, 0, :], ins["L2_gnn_W3"]), (w4[:, 0, :], ins["L2_gnn_W4"]),
             (b12[:, 0, :], ins["L2_gnn_b1"].partition_broadcast(P)),
             (b12[:, 1, 0:64], ins["L2_gnn_b2"].partition_broadcast(P)),
             (b34[:, 0, 0:128], ins["L2_gnn_b3"].rearrange("(a d) -> a d", a=1)),
             (b34[:, 1, :], ins["L2_gnn_b4"].rearrange("(a d) -> a d", a=1)))

        def convolve(w, relu_bias):
            x, s = a[:, :, 0:w], b[:, :, 0:w]

            def scale(dve):
                dve.tensor_tensor(x, x, per_node(k.dinv[:, :], w), ALU.mult)
                dve.drain()

            def finish(dve):
                dve.tensor_tensor(x, x, s, ALU.add)
                dve.drain()
                scale(dve)
                if relu_bias is not None:
                    dve.tensor_tensor(x, x, wide(relu_bias), ALU.add)
                    dve.drain()
                    dve.tensor_scalar(x, x, 0.0, None, ALU.max)
            on_vector(k, scale)
            sum_over_graph(k, k.matrices[0], x, s)
            on_vector(k, finish)
        project(k, xn[:, :, :], w1, a[:, :, :])
        convolve(128, b12[:, 0, :])
        project(k, a[:, :, :], w2, b[:, :, 0:64])

        def work(dve):
            dve.tensor_copy(a[:, :, 0:64], b[:, :, 0:64])
        on_vector(k, work)
        convolve(64, b12[:, 1, 0:64])
        convolve(64, None)
        project(k, a[:, :, 0:64], w3, b[:, :, :], bias=b34[:, 0, 0:128])

        def work(dve):
            dve.tensor_scalar(a[:, :, :], b[:, :, :], 0.0, None, ALU.max)
        on_vector(k, work)
        convolve(128, None)
        project(k, a[:, :, :], w4, xn[:, :, :], bias=b34[:, 1, :])
        add_to_state(k, xn[:, :, :])


def layer2_ffn(k):
    ins, E = k.ins, 8
    with ExitStack() as ctx:
        def sb(name, shape, dt=F32):
            return ctx.enter_context(k.nc.sbuf_tensor(f"{name}_f2", shape, dt))
        y = sb("y", [P, NT, D])
        xT = sb("xT", [P, KC, NP])
        logits = sb("logits", [P, NT, E])
        gate = sb("gate", [P, NT, E])
        wr = sb("wr", [P, KC, E])
        br = sb("br", [1, E])
        bo = sb("bo", [E, 1, D])
        m = sb("m", [P, NT])
        names = [f"{n}{l}" for l in (1, 2) for n in ("b", "g", "be", "m", "v")]
        v = {n: sb(n, [P, KC, E]) for n in names}
        layer_norm(k, k.x[:, :, :], y[:, :, :])
        with k.nc.allow_non_contiguous_dma(reason="per-feature vectors of the experts, once"):
            load(k, (wr[:, :, :], ins["L2_ffn_Wr"].rearrange("(c p) e -> p c e", p=P)),
                 (br[:, :], ins["L2_ffn_br"].rearrange("(a e) -> a e", a=1)), (bo[:, 0, :], ins["L2_ffn_bo"]),
                 *[(v[n][:, c, :], ins[f"L2_ffn_{n}"][:, c * P:(c + 1) * P].rearrange("e p -> p e"))
                   for n in names for c in range(KC)])
        project(k, y[:, :, :], wr, logits[:, :, :], bias=br[:, :], keep=xT)
        lg, gt = logits[:, :, :], gate[:, :, :]
        g, be, vv = ([v[f"{n}{l}"][:, :, :] for l in (1, 2)] for n in ("g", "be", "v"))

        def shift_logits(dve):
            dve.tensor_reduce(m[:, :], lg, AX.X, ALU.max)
            for l in range(2):
                dve.tensor_scalar(vv[l], vv[l], 0.001, None, ALU.add)
            dve.drain()
            dve.tensor_tensor(lg, lg, per_node(m[:, :], E), ALU.subtract)

        def exps_and_deviations(act):
            act.activation(gt, lg, ACT.Exp)
            for l in range(2):
                act.activation(vv[l], vv[l], ACT.Sqrt)

        def gates_and_norms(dve):
            dve.tensor_reduce(m[:, :], gt, AX.X, ALU.add)
            dve.drain()
            dve.reciprocal(m[:, :], m[:, :])
            dve.drain()
            dve.tensor_tensor(gt, gt, per_node(m[:, :], E), ALU.mult)
            for l, n in enumerate("12"):
                bias = v["b" + n][:, :, :]
                dve.reciprocal(vv[l], vv[l])
                dve.tensor_tensor(bias, bias, v["m" + n][:, :, :], ALU.subtract)
                dve.drain()
                dve.tensor_tensor(g[l], g[l], vv[l], ALU.mult)
                dve.drain()
                dve.tensor_tensor(bias, bias, g[l], ALU.mult)
                dve.drain()
                dve.tensor_tensor(be[l], be[l], bias, ALU.add)
        on_vector(k, shift_logits)
        on_scalar(k, exps_and_deviations)
        on_vector(k, gates_and_norms)
        project(k, gate[:, :, :], bo, y[:, :, :])

        def weights(name):
            return lambda w, e: [(w[:, :, :], ins[name][bass.ds(e, 1), :, :].rearrange("a (c p) h -> p (a c) h", p=P))]

        def relu(l):
            return lambda act, to, source, e, c: act.activation(
                to, source, ACT.Relu, bias=v[f"be{l}"][:, c, bass.ds(e, 1)], scale=v[f"g{l}"][:, c, bass.ds(e, 1)])
        experts(k, xT, gate, y, E, [(weights("L2_ffn_W1"), KC, relu(1), KC), (weights("L2_ffn_W2"), KC, relu(2), KC)],
                (lambda e: ins["L2_ffn_Wo"][bass.ds(e, 1), :, :].rearrange("a (c p) d -> p (a c) d", p=P), KC))
        add_to_state(k, y[:, :, :])


def layer3_gnn(k):
    ins = k.ins
    with ExitStack() as ctx:
        def sb(name, shape, dt=F32):
            return ctx.enter_context(k.nc.sbuf_tensor(f"{name}_g3", shape, dt))
        xn = sb("xn", [P, NT, D])
        agg = sb("agg", [P, NT, D])
        layer_norm(k, k.x[:, :, :], xn[:, :, :])
        sum_over_graph(k, k.matrices[1], xn[:, :, :], agg[:, :, :])
        wT = sb("wT", [P, 2 * KC, D])
        res = sb("res", [P, NT, D])
        load_transposed(k, (wT, ins["L3_gnn_W"]))
        project(k, agg[:, :, :], wT[:, 0:KC, :], res[:, :, :])
        project(k, xn[:, :, :], wT[:, KC:2 * KC, :], agg[:, :, :])

        def work(dve):
            dve.tensor_tensor(res[:, :, :], res[:, :, :], agg[:, :, :], ALU.add)
        on_vector(k, work)
        layer_norm(k, res[:, :, :], res[:, :, :], ins["L3_gnn_gamma"], ins["L3_gnn_beta"])

        def work(dve):
            dve.scalar_tensor_tensor(k.x[:, :, :], res[:, :, :], 0.0, k.x[:, :, :], ALU.max, ALU.add)
        on_vector(k, work)


def layer3_ffn(k):
    ins, E, H = k.ins, 32, 64
    with ExitStack() as ctx:
        def sb(name, shape, dt=F32):
            return ctx.enter_context(k.nc.sbuf_tensor(f"{name}_f3", shape, dt))
        y = sb("y", [P, NT, D])
        xT = sb("xT", [P, KC, NP])
        logits = sb("logits", [P, NT, E])
        scratch = sb("scratch", [P, NT, E])
        gate = sb("gate", [P, NT, E])
        wr = sb("wr", [P, KC, E])
        br = sb("br", [1, E])
        b1 = sb("b1", [P, E // 2])
        b2 = sb("b2", [E, 1, D])
        m = sb("m", [P, NT])
        spot = sb("spot", [P, NT])
        layer_norm(k, k.x[:, :, :], y[:, :, :])
        load_transposed(k, (wr, ins["L3_ffn_router_w"]))
        with k.nc.allow_non_contiguous_dma(reason="2048 biases, once"):
            load(k, (br[:, :], ins["L3_ffn_router_b"].rearrange("(a e) -> a e", a=1)), (b2[:, 0, :], ins["L3_ffn_b2"]),
                 (b1[:, :], ins["L3_ffn_b1"].rearrange("(u o) h -> (o h) u", o=2)))
        project(k, y[:, :, :], wr, logits[:, :, :], bias=br[:, :], keep=xT)

        def work(dve):
            one_hot_of_max(dve, k, logits[:, :, :], gate[:, :, :], m[:, :], spot[:, :], scratch[:, :, :])
        on_vector(k, work)
        project(k, gate[:, :, :], b2, y[:, :, :])
        w1, w2 = ins["L3_ffn_W1"], ins["L3_ffn_W2"]

        def pair(w, e):
            return [(w[:, :, o * H:(o + 1) * H], w1[bass.ds(e + o, 1), :, :].rearrange("a (c p) h -> p (a c) h", p=P))
                    for o in range(2)]
        experts(k, xT, gate, y, E,
                [(pair, 1, lambda act, to, source, e, c: act.activation(
                    to, source, ACT.Relu, bias=b1[:, bass.ds(e, 1)]), KC)],
                (lambda e: w2[bass.ds(e, 2), :, :].rearrange("a h d -> (a h) d").unsqueeze(1), 1), outs=2)

        def work(dve):
            dve.scalar_tensor_tensor(k.x[:, :, :], y[:, :, :], 0.0, k.x[:, :, :], ALU.max, ALU.add)
        on_vector(k, work)


def kernel_program(nc, ins, out, stages):
    k = Kernel(nc, ins, out)
    with ExitStack() as ctx:
        def sb(name, shape, dt=F32):
            return ctx.enter_context(nc.sbuf_tensor(name, shape, dt))
        k.x = sb("x_state", [P, NT, D])
        k.ident = sb("ident", [P, P])
        k.ones = sb("ones", [P, P])
        k.col = sb("col", [P, P])
        k.row = sb("row", [P, 1])
        k.lower = sb("lower", [P, P])
        k.dinv = sb("dinv", [P, NT])
        k.zero = sb("zero", [P, NP])
        k.cells = sb("cells", [P, T1, 4], I32)
        k.cells_f = k.cells[:, :, :].bitcast(F32)
        k.zeroed, k.copied, k.matrix_zeroed, k.paced = (
            nc.alloc_semaphore(n) for n in ("zeroed", "copied", "matrix_zeroed", "paced"))
        k.meta1 = k.dram("edges1", (T1 * P, EC), I32)
        k.meta2 = k.dram("edges2", (T2 * P, EC), I32)
        k.matrices = [k.dram(f"matrix{m}", (CELLS + P, 1)) for m in range(2)]
        t = k.t = {}
        for name, w in (("rows0", D + 8), ("scores0", 8), ("peak0", 8), ("query1", D), ("keyval1", 2 * D),
                        ("rows1", 20), ("src1", 4), ("dst1", 4), ("peak1", 4)):
            t[name] = k.dram(name, (NP, w))
        t["radial1"] = k.dram("radial1", (T1 * P, 64))
        for name, count, w in (("sum0", CHAINS, D + 8), ("sum1", CHAINS, D + 1), ("sumr", CHAINS, 20),
                               ("max0", MCHAINS, 8), ("max1", MCHAINS, 4)):
            t[name] = [k.dram(f"{name}_{c}", (NTAB, w)) for c in range(count)]
        build_constants(k)
        fill_tables(k, t["sum0"] + t["sum1"] + t["sumr"], t["max0"] + t["max1"])
        build_edges(k, k.meta1, T1, EDGES, ins["src"], ins["dst"], ins["edge_weight"], ins["edge_attr_3"])
        build_edges(k, k.meta2, T2, ROUTES, ins["L1_ffn_edge_index"][0], ins["L1_ffn_edge_index"][1])
        for layer in (layer0_gnn, layer0_ffn, layer1_gnn, layer1_ffn, layer2_gnn, layer2_ffn, layer3_gnn,
                      layer3_ffn)[:stages]:
            layer(k)
        store_state(k)


def store_state(k):
    nc = k.nc
    last = N - (NT - 1) * P
    with k.phase() as (sem, sb, ps):
        stored = sem("stored")
        with nc.Block() as block:
            @block.sync
            def _(sp):
                sp.dma_start(k.out[0:(NT - 1) * P, :].rearrange("(j p) w -> p j w", p=P), k.x[:, 0:NT - 1, :])\
                    .then_inc(stored, 16)
                sp.dma_start(k.out[(NT - 1) * P:N, :], k.x[0:last, NT - 1, :]).then_inc(stored, 16)
                sp.wait_ge(stored, 32)


def kernel(**inputs):
    import numpy as _np
    import concourse.bacc as _bacc
    from concourse import mybir as _mybir
    from concourse.bass_utils import run_bass_kernel_spmd as _run

    nc = _bacc.Bacc("TRN2", target_bir_lowering=False, num_devices=1)
    arrays, ins = {}, {}
    for name, value in inputs.items():
        a = _np.ascontiguousarray(value)
        arrays[f"in_{name}_dram"] = a
        ins[name] = nc.dram_tensor(f"in_{name}_dram", a.shape, _mybir.dt.from_np(a.dtype), kind="ExternalInput").ap()
    out = nc.dram_tensor("out_0_dram", (N, D), _mybir.dt.float32, kind="ExternalOutput").ap()
    kernel_program(nc, ins, out, 8)
    r = _run(nc, [arrays], core_ids=[0])
    return r.results[0]["out_0_dram"]
```
